# Optimizing a Trainium2 kernel written in Bass

```python
import numpy as np
import jax
import jax.numpy as jnp

def _softmax(x, axis=-1):
    return jax.nn.softmax(x, axis=axis)

def _gelu(x):
    return jax.nn.gelu(x, approximate=True)

def _silu(x):
    return jax.nn.silu(x)

def _sigmoid(x):
    return jax.nn.sigmoid(x)

def _layernorm(x, axis=-1, eps=1e-05):
    m = jnp.mean(x, axis=axis, keepdims=True)
    v = jnp.var(x, axis=axis, keepdims=True)
    return (x - m) / jnp.sqrt(v + eps)

def _scatter_add(tgt, idx, src, axis=0):
    return tgt.at[idx].add(src)

def _segment_sum(src, seg, n):
    return jax.ops.segment_sum(src, seg, n)
kernel_name = 'mk_gps_d1_gnn_r32_3b2598'

def setup_inputs(seed: int=0):
    np.random.seed(seed)
    _w = jnp.asarray

    def _rec_inputs():
        import jax
        import jax.numpy as jnp
        _gk = jax.random.key(seed)
        x = -0.0001126 + 1 * jax.random.normal(jax.random.fold_in(_gk, 1), (3125, 256), jnp.float32)
        _s = jax.random.randint(jax.random.fold_in(_gk, 2), (25000,), 0, 3125, jnp.int32)
        _d = jax.random.randint(jax.random.fold_in(_gk, 3), (25000,), 0, 3125, jnp.int32)
        _loop = jnp.arange(3125, dtype=jnp.int32)
        src = jnp.concatenate([_s, _d, _loop])
        dst = jnp.concatenate([_d, _s, _loop])
        _o = jnp.argsort(dst, stable=True)
        src = src[_o]
        dst = dst[_o]
        edge_attr_4 = 0.00117183 + 1.0004 * jax.random.normal(jax.random.fold_in(_gk, 12), (53125, 4), jnp.float32)
        edge_attr_8 = -0.000615933 + 0.999959 * jax.random.normal(jax.random.fold_in(_gk, 13), (53125, 8), jnp.float32)
        node_vec1 = jax.random.uniform(jax.random.fold_in(_gk, 14), (3125, 1), jnp.float32, 0.0, 1)
        return (x, src, dst, edge_attr_4, edge_attr_8, node_vec1)
    x, src, dst, edge_attr_4, edge_attr_8, node_vec1 = _rec_inputs()

    def _L0_gnn_setup():
        import jax, jax.numpy as jnp
        import numpy as np
        import math
        N = 30000
        E = 18750
        MUL = 64
        NES = 8
        FCN = 64
        NUM_NEIGHBORS = 20.0
        SILU_NORM = 1.679
        INV_SQRT3 = 1.0 / math.sqrt(3.0)

        def _split(x):
            return (x[:, :MUL], x[:, MUL:].reshape(-1, MUL, 3))
        key = jax.random.key(seed)
        ks = jax.random.split(key, 16)
        inp = {'node_input': jax.random.normal(ks[0], (N, 4 * MUL), jnp.float32), 'node_attr': jnp.ones((N, 1), jnp.float32), 'edge_src': jax.random.randint(ks[1], (E,), 0, N), 'edge_dst': jax.random.randint(ks[2], (E,), 0, N), 'edge_attr': jax.random.normal(ks[3], (E, 4), jnp.float32), 'edge_scalars': jax.random.normal(ks[4], (E, NES), jnp.float32), 'sc_w0': jax.random.normal(ks[5], (MUL, MUL), jnp.float32), 'sc_w1': jax.random.normal(ks[6], (MUL, MUL), jnp.float32), 'lin1_w0': jax.random.normal(ks[7], (MUL, MUL), jnp.float32), 'lin1_w1': jax.random.normal(ks[8], (MUL, MUL), jnp.float32), 'fc_w1': jax.random.normal(ks[9], (NES, FCN), jnp.float32), 'fc_w2': jax.random.normal(ks[10], (FCN, 4 * MUL), jnp.float32), 'lin2_w00': jax.random.normal(ks[11], (MUL, MUL), jnp.float32), 'lin2_w01': jax.random.normal(ks[12], (MUL, MUL), jnp.float32), 'lin2_w10': jax.random.normal(ks[13], (MUL, MUL), jnp.float32), 'lin2_w11': jax.random.normal(ks[14], (MUL, MUL), jnp.float32)}
        return inp
    _L0_gnn_all = _L0_gnn_setup()
    _L0_gnn_in = {k: v for k, v in _L0_gnn_all.items() if k in ('sc_w0', 'sc_w1', 'lin1_w0', 'lin1_w1', 'fc_w1', 'fc_w2', 'lin2_w00', 'lin2_w01', 'lin2_w10', 'lin2_w11')}
    del _L0_gnn_all

    def _L0_mix_setup():
        import jax, jax.numpy as jnp
        import numpy as np
        DIM = 256
        HEADS = 4
        DIM_HEAD = 32
        NUM_MEM = 4
        HIDDEN = HEADS * DIM_HEAD
        SCALE = DIM_HEAD ** (-0.5)

        def rmsnorm(x, g):
            n = jnp.linalg.norm(x, axis=-1, keepdims=True)
            return x / jnp.maximum(n, 1e-12) * g * x.shape[-1] ** 0.5
        key = jax.random.key(seed)
        ks = jax.random.split(key, 8)
        B, N = (4, 512)
        return {'x': jax.random.normal(ks[0], (B, N, DIM), jnp.float32), 't': jax.random.normal(ks[1], (B,), jnp.float32), 'w_qkv': jax.random.normal(ks[2], (DIM, 3 * HIDDEN), jnp.float32) * 0.02, 'mem_kv': jax.random.normal(ks[3], (2, HEADS, DIM_HEAD, NUM_MEM), jnp.float32), 'w_out': jax.random.normal(ks[4], (HIDDEN, DIM), jnp.float32) * 0.02, 'b_out': jnp.zeros((DIM,), jnp.float32), 'g_out': jnp.ones((DIM,), jnp.float32), 'g_pre': jnp.ones((DIM,), jnp.float32)}
    _L0_mix_all = _L0_mix_setup()
    _L0_mix_in = {k: v for k, v in _L0_mix_all.items() if k in ('t', 'w_qkv', 'mem_kv', 'w_out', 'b_out', 'g_out', 'g_pre')}
    del _L0_mix_all

    def _L0_ffn_setup():
        import math
        import jax, jax.numpy as jnp
        import numpy as np
        CAPACITY_FACTOR = 1.25
        key = jax.random.key(seed)
        ks = jax.random.split(key, 5)
        B, L, D, F, E = (8, 256, 256, 1024, 8)
        h = jax.random.normal(ks[0], (B, L, D), dtype=jnp.float32)
        gate_w = jax.random.normal(ks[1], (D, E), dtype=jnp.float32) * 0.02
        gate_b = jnp.zeros((E,), dtype=jnp.float32)
        w1 = jax.random.normal(ks[2], (E, D, F), dtype=jnp.float32) * (1.0 / math.sqrt(D))
        b1 = jnp.zeros((E, F), dtype=jnp.float32)
        w2 = jax.random.normal(ks[3], (E, F, D), dtype=jnp.float32) * (1.0 / math.sqrt(F))
        b2 = jnp.zeros((E, D), dtype=jnp.float32)
        return {'h': h, 'gate_w': gate_w, 'gate_b': gate_b, 'w1': w1, 'b1': b1, 'w2': w2, 'b2': b2}
    _L0_ffn_all = _L0_ffn_setup()
    _L0_ffn_in = {k: v for k, v in _L0_ffn_all.items() if k in ('gate_w', 'gate_b', 'w1', 'b1', 'w2', 'b2')}
    del _L0_ffn_all
    return {'x': x, 'src': src, 'dst': dst, 'edge_attr_4': edge_attr_4, 'edge_attr_8': edge_attr_8, 'node_vec1': node_vec1, 'L0_gnn_sc_w0': _L0_gnn_in['sc_w0'], 'L0_gnn_sc_w1': _L0_gnn_in['sc_w1'], 'L0_gnn_lin1_w0': _L0_gnn_in['lin1_w0'], 'L0_gnn_lin1_w1': _L0_gnn_in['lin1_w1'], 'L0_gnn_fc_w1': _L0_gnn_in['fc_w1'], 'L0_gnn_fc_w2': _L0_gnn_in['fc_w2'], 'L0_gnn_lin2_w00': _L0_gnn_in['lin2_w00'], 'L0_gnn_lin2_w01': _L0_gnn_in['lin2_w01'], 'L0_gnn_lin2_w10': _L0_gnn_in['lin2_w10'], 'L0_gnn_lin2_w11': _L0_gnn_in['lin2_w11'], 'L0_mix_t': _L0_mix_in['t'], 'L0_mix_w_qkv': _L0_mix_in['w_qkv'], 'L0_mix_mem_kv': _L0_mix_in['mem_kv'], 'L0_mix_w_out': _L0_mix_in['w_out'], 'L0_mix_b_out': _L0_mix_in['b_out'], 'L0_mix_g_out': _L0_mix_in['g_out'], 'L0_mix_g_pre': _L0_mix_in['g_pre'], 'L0_ffn_gate_w': _L0_ffn_in['gate_w'], 'L0_ffn_gate_b': _L0_ffn_in['gate_b'], 'L0_ffn_w1': _L0_ffn_in['w1'], 'L0_ffn_b1': _L0_ffn_in['b1'], 'L0_ffn_w2': _L0_ffn_in['w2'], 'L0_ffn_b2': _L0_ffn_in['b2']}

def reference(x, src, dst, edge_attr_4, edge_attr_8, node_vec1, L0_gnn_sc_w0, L0_gnn_sc_w1, L0_gnn_lin1_w0, L0_gnn_lin1_w1, L0_gnn_fc_w1, L0_gnn_fc_w2, L0_gnn_lin2_w00, L0_gnn_lin2_w01, L0_gnn_lin2_w10, L0_gnn_lin2_w11, L0_mix_t, L0_mix_w_qkv, L0_mix_mem_kv, L0_mix_w_out, L0_mix_b_out, L0_mix_g_out, L0_mix_g_pre, L0_ffn_gate_w, L0_ffn_gate_b, L0_ffn_w1, L0_ffn_b1, L0_ffn_w2, L0_ffn_b2):
    import jax
    import jax.numpy as jnp

    def _L0_gnn_ref(node_input, node_attr, edge_src, edge_dst, edge_attr, edge_scalars, sc_w0, sc_w1, lin1_w0, lin1_w1, fc_w1, fc_w2, lin2_w00, lin2_w01, lin2_w10, lin2_w11):
        import jax, jax.numpy as jnp
        import numpy as np
        import math
        N = 30000
        E = 18750
        MUL = 64
        NES = 8
        FCN = 64
        NUM_NEIGHBORS = 20.0
        SILU_NORM = 1.679
        INV_SQRT3 = 1.0 / math.sqrt(3.0)

        def _split(x):
            return (x[:, :MUL], x[:, MUL:].reshape(-1, MUL, 3))
        n = node_input.shape[0]
        inv_mul = 1.0 / math.sqrt(MUL)
        x0, x1 = _split(node_input)
        a = node_attr
        s0 = x0 @ sc_w0 * a * inv_mul
        s1 = jnp.einsum('nuc,uv->nvc', x1, sc_w1) * a[:, :, None] * inv_mul
        y0 = x0 @ lin1_w0 * a * inv_mul
        y1 = jnp.einsum('nuc,uv->nvc', x1, lin1_w1) * a[:, :, None] * inv_mul
        h = jax.nn.silu(edge_scalars @ fc_w1 * (1.0 / math.sqrt(NES))) * SILU_NORM
        w = h @ fc_w2 * (1.0 / math.sqrt(FCN))
        w_a, w_b, w_c, w_d = (w[:, :MUL], w[:, MUL:2 * MUL], w[:, 2 * MUL:3 * MUL], w[:, 3 * MUL:])
        xg0 = y0[edge_src]
        xg1 = y1[edge_src]
        ea0 = edge_attr[:, :1]
        ea1 = edge_attr[:, 1:4]
        mid0 = w_a * xg0 * ea0
        mid1 = w_b * jnp.einsum('euc,ec->eu', xg1, ea1) * INV_SQRT3
        mid2 = (w_c * xg0)[:, :, None] * ea1[:, None, :]
        mid3 = (w_d * ea0)[:, :, None] * xg1
        mids = jnp.concatenate([mid0, mid1, mid2.reshape(-1, 3 * MUL), mid3.reshape(-1, 3 * MUL)], axis=1)
        agg = jax.ops.segment_sum(mids, edge_dst, num_segments=n)
        agg = agg * (1.0 / math.sqrt(NUM_NEIGHBORS))
        z0a = agg[:, :MUL]
        z0b = agg[:, MUL:2 * MUL]
        z1a = agg[:, 2 * MUL:5 * MUL].reshape(n, MUL, 3)
        z1b = agg[:, 5 * MUL:].reshape(n, MUL, 3)
        inv2 = 1.0 / math.sqrt(2 * MUL)
        o0 = (z0a @ lin2_w00 + z0b @ lin2_w01) * a * inv2
        o1 = (jnp.einsum('nuc,uv->nvc', z1a, lin2_w10) + jnp.einsum('nuc,uv->nvc', z1b, lin2_w11)) * a[:, :, None] * inv2
        c_s = math.sin(math.pi / 8.0)
        c_x = math.cos(math.pi / 8.0)
        out0 = c_s * s0 + c_x * o0
        out1 = c_s * s1 + c_x * o1
        return jnp.concatenate([out0, out1.reshape(n, 3 * MUL)], axis=1)

    def _L0_mix_ref(x, t, w_qkv, mem_kv, w_out, b_out, g_out, g_pre):
        import jax, jax.numpy as jnp
        import numpy as np
        DIM = 256
        HEADS = 4
        DIM_HEAD = 32
        NUM_MEM = 4
        HIDDEN = HEADS * DIM_HEAD
        SCALE = DIM_HEAD ** (-0.5)

        def rmsnorm(x, g):
            n = jnp.linalg.norm(x, axis=-1, keepdims=True)
            return x / jnp.maximum(n, 1e-12) * g * x.shape[-1] ** 0.5
        b, n, c = x.shape
        xn = rmsnorm(x, g_pre)
        qkv = xn @ w_qkv
        q, k, v = jnp.split(qkv, 3, axis=-1)

        def to_heads(z):
            return z.reshape(b, n, HEADS, DIM_HEAD).transpose(0, 2, 3, 1)
        q, k, v = map(to_heads, (q, k, v))
        mk = jnp.broadcast_to(mem_kv[0], (b, HEADS, DIM_HEAD, NUM_MEM))
        mv = jnp.broadcast_to(mem_kv[1], (b, HEADS, DIM_HEAD, NUM_MEM))
        k = jnp.concatenate([mk, k], axis=-1)
        v = jnp.concatenate([mv, v], axis=-1)
        q = jax.nn.softmax(q, axis=-2) * SCALE
        k = jax.nn.softmax(k, axis=-1)
        context = jnp.einsum('bhdn,bhen->bhde', k, v)
        out = jnp.einsum('bhde,bhdn->bhen', context, q)
        out = out.transpose(0, 3, 1, 2).reshape(b, n, HIDDEN)
        out = rmsnorm(out @ w_out + b_out, g_out)
        return out + x

    def _L0_ffn_ref(h, gate_w, gate_b, w1, b1, w2, b2):
        import math
        import jax, jax.numpy as jnp
        import numpy as np
        CAPACITY_FACTOR = 1.25
        B, L, D = h.shape
        E = gate_w.shape[1]
        T = B * L
        C = max(1, math.ceil(CAPACITY_FACTOR * T / E))
        x = h.reshape(T, D)
        logits = x @ gate_w + gate_b
        probs = jax.nn.softmax(logits, axis=-1)
        idx = jnp.argmax(probs, axis=-1)
        prb = jnp.take_along_axis(probs, idx[:, None], axis=1)[:, 0]
        one_hot = jax.nn.one_hot(idx, E, dtype=jnp.float32)
        pos = (jnp.cumsum(one_hot, axis=0) * one_hot).sum(-1).astype(jnp.int32) - 1
        kept = pos < C
        pos_safe = jnp.where(kept, pos, C)
        buf = jnp.zeros((E, C, D), dtype=h.dtype).at[idx, pos_safe].set(x, mode='drop')
        hmid = jax.nn.relu(jnp.einsum('ecd,edf->ecf', buf, w1) + b1[:, None, :])
        ybuf = jnp.einsum('ecf,efd->ecd', hmid, w2) + b2[:, None, :]
        pos_g = jnp.minimum(pos, C - 1)
        y_tok = ybuf[idx, pos_g] * (prb * kept)[:, None]
        y = y_tok.reshape(B, L, D)
        y = jnp.nan_to_num(y, nan=0.0, posinf=10000.0, neginf=-10000.0)
        return y
    xn = _layernorm(x, axis=-1)
    x = x + _L0_gnn_ref(xn, node_vec1, src, dst, edge_attr_4, edge_attr_8, L0_gnn_sc_w0, L0_gnn_sc_w1, L0_gnn_lin1_w0, L0_gnn_lin1_w1, L0_gnn_fc_w1, L0_gnn_fc_w2, L0_gnn_lin2_w00, L0_gnn_lin2_w01, L0_gnn_lin2_w10, L0_gnn_lin2_w11) + _L0_mix_ref(xn[None], L0_mix_t, L0_mix_w_qkv, L0_mix_mem_kv, L0_mix_w_out, L0_mix_b_out, L0_mix_g_out, L0_mix_g_pre)[0]
    x = x + _L0_ffn_ref(_layernorm(x, axis=-1)[None], L0_ffn_gate_w, L0_ffn_gate_b, L0_ffn_w1, L0_ffn_b1, L0_ffn_w2, L0_ffn_b2)[0]
    return x

_drawn_inputs = setup_inputs


def setup_inputs(seed=0):
    import zlib

    import numpy as np

    out = dict(_drawn_inputs(seed))
    spreads = {'L0_mix_b_out': (0.0, 0.1),
     'L0_mix_g_out': (1.0, 0.2),
     'L0_mix_g_pre': (1.0, 0.6),
     'L0_ffn_gate_b': (0.0, 0.1),
     'L0_ffn_b1': (0.0, 0.8),
     'L0_ffn_b2': (0.0, 0.8)}
    factors = {'L0_mix_w_qkv': 8.0, 'L0_mix_mem_kv': 8.0, 'L0_mix_w_out': 8.0}
    for name, (base, spread) in spreads.items():
        noise = np.random.default_rng([zlib.crc32(name.encode()), seed]).standard_normal(out[name].shape)
        drawn = base * np.exp(spread * noise) if base else spread * noise
        out[name] = jnp.asarray(drawn.astype(out[name].dtype))
    for name, factor in factors.items():
        out[name] = (out[name] * factor).astype(out[name].dtype)
    return out
```

```python
from contextlib import ExitStack
import math

import concourse.bass as bass
from concourse import mybir

F32 = mybir.dt.float32
I32 = mybir.dt.int32
F32R = mybir.dt.float32r
ALU = mybir.AluOpType
ACT = mybir.ActivationFunctionType
AX = mybir.AxisListType

P = 128
N = 3125
D = 256
MUL = 64
NT = 25
TB = 5
NODE_TURNS = NT // TB
NPAD = NT * P
LAST = N - (NT - 1) * P
EDGES = 53125
GT = 2
GROUPS_PER_TURN = 4
TPT = GT * GROUPS_PER_TURN
EDGE_TURNS = -(-EDGES // (P * TPT))
ET = EDGE_TURNS * TPT
EG = ET // GT
CHUNK = 4 * P
WIN = 24
STRAY_WIN = 120
STRAY_TURNS = -(-N // STRAY_WIN)
NZ = STRAY_TURNS * STRAY_WIN
assert NZ >= N + WIN and NZ >= NPAD
HD = 128
HEADS, DH = 4, 32
NUM_MEM = 4
E = 8
CAP = -(-5 * N // (4 * E))
SLOTS = CAP
F = 1024
FB = F // P
LAST_C = CAP - 3 * P
TRASH = E * SLOTS

W_SCALE = 1.679 / 8.0
INV_SQRT3 = 1.0 / math.sqrt(3.0)
Y_SCALE = 1.0 / 8.0
S_SCALE = math.sin(math.pi / 8.0) / 8.0
Z_SCALE = math.cos(math.pi / 8.0) / math.sqrt(128.0) / math.sqrt(20.0)
SM_SCALE = DH ** -0.5
ES_SCALE = 1.0 / math.sqrt(8.0)
EPS = 1e-5
FLT_MAX = 3.4028234663852886e38

C_IDENT, C_TRI, C_BLOCK, C_ONES, C_IOTA, C_VALID, C_RESET, C_IOTA8, C_TRASH, C_HIGH, C_LOW, C_END = (
    0, 128, 256, 384, 512, 632, 633, 833, 841, 866, 867, 868)


class Chain:

    def __init__(self, eng, sem):
        self.eng, self.sem, self.n, self.offset = eng, sem, 0, 0

    def link(self, ins):
        self.n += 1
        ins.then_inc(self.sem, 1)
        self.eng.wait_ge(self.sem, self.offset + self.n)

    def enter(self, i, per_turn):
        self.start, self.per_turn, self.offset = self.n, per_turn, i * per_turn

    def leave(self, turns):
        assert self.n - self.start == self.per_turn, (self.n - self.start, self.per_turn)
        self.n, self.offset = self.start + turns * self.per_turn, 0


def bc(ap, axis, n):
    v = ap.unsqueeze(axis)
    shape = list(v.shape)
    shape[axis] = n
    return v.to_broadcast(shape)


def program(nc, x, node_a, src, dst, dst_first, ea, es, w_y, w_s, w_z, fc1, fc2, w_qkv, g_pre,
            mem_kt, mem_k, mem_v, w_out, b_out, g_out, gate_w, gate_b, w1, b1, w2, b2, consts, out):
    y_dram = nc.dram_tensor("y_dram", (NPAD, D), F32)
    buf_dram = nc.dram_tensor("buf_dram", (TRASH + NPAD, D), F32)
    es_len = es.shape[1] * P // 8
    es_hl = nc.dram_tensor("es_hl", (2 * 8, es_len), F32)
    ybuf_dram = nc.dram_tensor("ybuf_dram", (E * SLOTS, D), F32)

    with ExitStack() as ctx:
        def sb(name, shape, dt=F32):
            return ctx.enter_context(nc.sbuf_tensor(name, shape, dt))

        def sem(name):
            return ctx.enter_context(nc.semaphore(name))

        ps = ctx.enter_context(nc.psum_tensor("ps", [P, 8, 512], F32))

        cst = sb("cst", [P, C_END])
        ident, tri, block_mask = cst[:, C_IDENT:C_TRI], cst[:, C_TRI:C_BLOCK], cst[:, C_BLOCK:C_ONES]
        ones, iota = cst[:, C_ONES:C_IOTA], cst[:, C_IOTA:C_VALID]
        valid, reset, iota8 = cst[:, C_VALID:C_RESET], cst[:, C_RESET:C_IOTA8], cst[:, C_IOTA8:C_TRASH]
        trash_row = cst[:, C_TRASH:C_HIGH]
        resid = sb("resid", [P, NT, D])
        zT = sb("zT", [P, 5, NZ])
        wy = sb("wy", [P, 2, P])
        ws = sb("ws", [P, 2, P])
        wz = sb("wz", [P, 4, MUL])
        fc1_sb = sb("fc1_sb", [4 * 8, P])
        fc1_hl = sb("fc1_hl", [4 * 8, 2, P])
        fc1_r = sb("fc1_r", [P, P], F32R)
        fc2_sb = sb("fc2_sb", [P, 256])
        fc2_r = sb("fc2_r", [P, 2, 256], F32R)
        es_r = sb("es_r", [P, 2, CHUNK], F32R)
        h_r = sb("h_r", [P, 2, CHUNK], F32R)
        wqkv = sb("wqkv", [P, 2, 3 * HD])
        gpre = sb("gpre", [P, 2])
        node_a_sb = sb("node_a_sb", [P, NT])
        memkt = sb("memkt", [P, NUM_MEM])
        memk = sb("memk", [NUM_MEM, HD])
        memv = sb("memv", [NUM_MEM, HD])
        wout = sb("wout", [P, D])
        bout_b = sb("bout_b", [P, D])
        gout_b = sb("gout_b", [P, D])
        gatew = sb("gatew", [P, 2, E])
        gateb_b = sb("gateb_b", [P, E])
        mix_w = sb("mix_w", [P, D])
        small = sb("small", [P, 16])
        ea_sb = sb("ea_sb", [P, ET, 4])
        dst_i = sb("dst_i", [P, ET], I32)
        first_i = sb("first_i", [1, 1 + EG], I32)
        region = sb("region", [P, 14200])
        kv = region[:, 0:NT * 256].rearrange("p (t c) -> p t c", t=NT)
        r0 = NT * 256
        xn = region[:, r0:r0 + TB * D].rearrange("p (t c) -> p t c", t=TB)
        xm = region[:, r0 + 1280:r0 + 2560].rearrange("p (t c) -> p t c", t=TB)
        xT = region[:, r0 + 2560:r0 + 3840].rearrange("p (t k c) -> p t k c", t=TB, k=2)
        ysb = region[:, r0 + 3840:r0 + 5120].rearrange("p (t c) -> p t c", t=TB)
        qs = region[:, r0 + 5120:r0 + 5760].rearrange("p (t c) -> p t c", t=TB)
        qn = region[:, r0 + 5760:r0 + 6400].rearrange("p (t c) -> p t c", t=TB)
        st = region[:, r0 + 6400:r0 + 6430].rearrange("p (t c) -> p t c", t=TB)
        sq_junk = region[:, r0 + 6440:r0 + 7720].rearrange("p (t c) -> p t c", t=TB)
        mv = sb("mv", [P, TB, 2])
        col = sb("col", [P, 8, TB])
        qcol = sb("qcol", [P, 2, TB * HEADS])
        kmx = sb("kmx", [P, 4])
        relf = region[:, 0:ET]
        first_f = region[0:1, ET:ET + EG]
        inw = region[:, 700:700 + ET]
        junk = region[:, 1200:1200 + ET]
        xg = region[:, 1700:1700 + 2048].rearrange("p (g j c) -> p g j c", g=4, j=GT)
        prod = region[:, 3800:3800 + 2048].rearrange("p (g j c) -> p g j c", g=2, j=GT)
        h_f = region[:, 5900:5900 + 1024].rearrange("p (s c) -> p s c", s=2)
        sel = region[:, 8100:8100 + 8 * 4 * WIN].rearrange("p (s t c w) -> p s t c w", s=2, t=4, c=4)
        hot = region[:, 8900:8900 + 8 * WIN].rearrange("p (s t w) -> p s t w", s=2, t=4)
        stage = region[:, 9200:9200 + 2 * 4 * WIN].rearrange("p (s b w) -> p s b w", s=2, b=4)
        stray_dst = region[:, 9400:9400 + ET]
        stray_cur = region[:, 9820:9822]
        stray_hot = region[:, 9830:9830 + STRAY_WIN]
        stray_sel = region[:, 9950:9950 + 4 * STRAY_WIN].rearrange("p (c w) -> p c w", c=4)
        idx_sb = sb("idx_sb", [P, GROUPS_PER_TURN, GT], I32)
        flag_i = sb("flag_i", [1, 2], I32)
        flag_f = sb("flag_f", [P, 2])
        xl = region[:, 0:NT * 256].rearrange("p (t c) -> p t c", t=NT)
        zst = region[:, 6400:6400 + 1280].rearrange("p (s b c) -> p s b c", s=2, b=5)
        om = region[:, 7700:7700 + 512].rearrange("p (s c) -> p s c", s=2)
        om2 = region[:, 8220:8220 + 512].rearrange("p (s c) -> p s c", s=2)
        xlT = region[:, 8740:8740 + 512].rearrange("p (s k c) -> p s k c", s=2, k=2)
        om_junk = region[:, 9260:9260 + 256]
        rt = region[:, 9600:9600 + 12 * NT * E].rearrange("p (a c) -> p a c", a=12)
        logits = sb("logits", [P, NT * E])
        rcol = sb("rcol", [P, 12, NT])
        cst6 = sb("cst6", [P, 2, 8])
        scat_i = sb("scat_i", [P, NT], I32)
        gath_i = sb("gath_i", [P, NT], I32)
        w1_sb = sb("w1_sb", [P, 2, 2, F])
        w2_sb = zT[:].rearrange("p b z -> p (b z)")[:, 0:2 * FB * D].rearrange("p (s f d) -> p s f d", s=2, f=FB)
        zflat = zT[:].rearrange("p b z -> p (b z)")
        ew = es.shape[1]
        es_hi, es_lo, es_in_f = (zflat[:, n * ew:(n + 1) * ew] for n in range(3))
        o = 2 * FB * D
        hid = zflat[:, o:o + FB * CAP].rearrange("p (f c) -> p f c", f=FB)
        o += FB * CAP + 8
        xb = zflat[:, o:o + 2048].rearrange("p (s c d) -> p s c d", s=2, c=4)
        o += 2048
        xbT = zflat[:, o:o + 1024].rearrange("p (k c) -> p k c", k=2)
        o += 1024
        yst = zflat[:, o:o + 2048].rearrange("p (s c d) -> p s c d", s=2, c=4)
        o += 2048
        assert o <= 5 * NZ
        b1_sb = sb("b1_sb", [P, 2, FB])
        b2_sb = sb("b2_sb", [P, 2, D])

        S = {}
        for name in """consts_in weights_in es_raw_in es_split es_stored zeroed lo_ready x_in edges_in scaled dve_chain act_chain turn_dve turn_pe turn_act turn_pool turn_sp
            var_ready std_ready xn_ready norm_ready xm_ready xT_ps xT_sb ys_ps y_sb s_sb qkv_ps qkv_sb kt_ps kmax_sb q_sub q_exp
            qn_ready qT_ps qT_sb y_stored ysb_free kdiag kmax_b k_sub k_exp ctx_ps ctx_sb mixw_ps mixw_sb
            first_row first_ps strays_sum flag_ps flag_ready h_ready silu_done w_ready prod_ready sel_done z_evac added
            stray_gathered stray_step_dve stray_step_act stray_step_pe
            zst_ready gnn_ps om_ready om_sq om_norm x2_var x2_std xl_ready xlT_ps xlT_sb gate_ps logit_sb
            l_sub l_exp hot_ready pre_ps slots_ready scattered zero_in
            xbT_ps xbT_sb hid_ps hid_sb yexp_ps yst_ready out_ready out_stored""".split():
            S[name] = sem(name)
        es_in = [sem(f"es_in{s}") for s in range(2)]
        idx_in = [sem(f"idx_in{k}") for k in range(4)]
        rows_in = [sem(f"rows_in{k}") for k in range(4)]
        we_in = [sem(f"we_in{s}") for s in range(2)]
        xb_in = [sem(f"xb_in{s}") for s in range(2)]
        y_out = [sem(f"y_out{s}") for s in range(2)]
        back_in = [sem(f"back_in{s}") for s in range(NODE_TURNS)]

        x_v = x.rearrange("(t p) c -> p t c", p=P)
        y_v = y_dram[:].rearrange("(t p) c -> p t c", p=P)
        out_v = out.rearrange("(t p) c -> p t c", p=P)
        N_WEIGHTS = 19

        block = ctx.enter_context(nc.Block())

        @block.sync
        def _(sp):
            def load_scalars(s, first, n):
                for half in range(2):
                    sp.dma_start(es_r[16 * half:16 * half + 16, s, 0:n].bitcast(F32), es_hl[:, bass.ds(first, n)]).then_inc(es_in[s], 16)

            def load_rows(s, e):
                sp.dma_start(xb[:, s, 0:3, :], buf_dram[bass.ds(e * SLOTS, 3 * P), :].rearrange("(c p) d -> p c d", p=P)).then_inc(xb_in[s], 16)
                sp.dma_start(xb[0:LAST_C, s, 3, :], buf_dram[bass.ds(e * SLOTS + 3 * P, LAST_C), :]).then_inc(xb_in[s], 16)

            sp.dma_start(cst[:], consts).then_inc(S["consts_in"], 16)
            sp.dma_start(node_a_sb[:], node_a).then_inc(S["consts_in"], 16)
            with sp.Fori(0, NODE_TURNS) as i:
                sp.dma_start(resid[:, bass.ds(i * TB, TB), :], x_v[:, bass.ds(i * TB, TB), :]).then_inc(S["x_in"], 16)
                sp.wait_ge(S["x_in"], i * 16 + 16)
                sp.sem_inc(S["turn_sp"], 1)
            sp.dma_start(ea_sb[:], ea).then_inc(S["edges_in"], 16)
            sp.dma_start(dst_i[:], dst).then_inc(S["edges_in"], 16)
            sp.dma_start(first_i[:], dst_first).then_inc(S["edges_in"], 16)
            sp.wait_ge(S["zeroed"], 1)
            sp.dma_start(buf_dram[0:TRASH, :].rearrange("r d -> (r d)").rearrange("(p f) -> p f", p=P),
                         zT[:].rearrange("p b z -> p (b z)")[:, 0:TRASH * D // P]).then_inc(S["zero_in"], 16)
            sp.wait_ge(S["ctx_sb"], 1)
            for s in range(2):
                load_scalars(s, s * CHUNK, CHUNK)
            for k in range(GROUPS_PER_TURN):
                sp.dma_start(idx_sb[:, k, :], src[:, k, :]).then_inc(idx_in[k], 16)
            with sp.Fori(1, EDGE_TURNS) as i:
                for s in range(2):
                    sp.wait_ge(S["h_ready"], i * 2 + (s - 1))
                    sp.sem_inc(S["turn_sp"], 1)
                    load_scalars(s, i * (2 * CHUNK) + s * CHUNK, CHUNK)
                    for k in range(2 * s, 2 * s + 2):
                        sp.wait_ge(rows_in[k], i * (16 * GT))
                        sp.sem_inc(S["turn_sp"], 1)
                        sp.dma_start(idx_sb[:, k, :], src[:, bass.ds(i * GROUPS_PER_TURN + k, 1), :]
                                     .rearrange("p a j -> p (a j)")).then_inc(idx_in[k], 16)
            sp.wait_ge(S["h_ready"], 2 * EDGE_TURNS - 1)
            load_scalars(0, 2 * EDGE_TURNS * CHUNK, CHUNK)
            sp.wait_ge(S["flag_ready"], 1)
            flag = sp.value_load(flag_i[0:1, 0:1], min_val=0, max_val=ET * P)
            sp.wait_ge(S["added"], EG + 3)
            with sp.If(flag > 0):
                with sp.Fori(0, ET) as t:
                    sp.wait_ge(S["stray_step_dve"], t * (STRAY_TURNS + 3) + 1)
                    sp.sem_inc(S["turn_sp"], 1)
                    load_scalars(1, t * P, P)
                    sp.wait_ge(es_in[1], t * 32 + 32 * (EDGE_TURNS + 1))
                    sp.sem_inc(S["turn_sp"], 1)
                    sp.dma_start(idx_sb[:, 0, 0:1], src.rearrange("p g j -> p (g j)")[:, bass.ds(t, 1)],
                                 allow_slow_non_contiguous=True).then_inc(idx_in[0], 16)
            with sp.Else():
                sp.sem_inc(S["turn_sp"], 1)
            sp.wait_ge(S["logit_sb"], NT)
            for e in range(2):
                sp.dma_start(w1_sb[:, e], w1[e]).then_inc(we_in[e], 16)
                sp.dma_start(w2_sb[:, e], w2[e]).then_inc(we_in[e], 16)
                sp.dma_start(b1_sb[:, e], b1[e]).then_inc(we_in[e], 16)
                sp.dma_start(b2_sb[:, e], b2[e:e + 1, :].partition_broadcast(P)).then_inc(we_in[e], 16)
            sp.wait_ge(S["scattered"], 16 * NT)
            for e in range(2):
                load_rows(e, e)
            with sp.Fori(0, E // 2 - 1) as i:
                for s in range(2):
                    e = i * 2 + (2 + s)
                    sp.wait_ge(S["xbT_ps"], i * 4 + 2 * s + 2)
                    sp.sem_inc(S["turn_sp"], 1)
                    load_rows(s, e)
                    sp.wait_ge(S["yst_ready"], i * 8 + 4 * s + 4)
                    sp.sem_inc(S["turn_sp"], 1)
                    sp.dma_start(w1_sb[:, s], w1[bass.ds(e, 1)].rearrange("a p k f -> p (a k) f")).then_inc(we_in[s], 16)
                    sp.dma_start(w2_sb[:, s], w2[bass.ds(e, 1)].rearrange("a p k f -> p (a k) f")).then_inc(we_in[s], 16)
                    sp.dma_start(b1_sb[:, s], b1[bass.ds(e, 1)].rearrange("a p k -> p (a k)")).then_inc(we_in[s], 16)
                    sp.dma_start(b2_sb[:, s], b2[bass.ds(e, 1), :].partition_broadcast(P)).then_inc(we_in[s], 16)
            for g in range(NODE_TURNS):
                sp.wait_ge(S["out_ready"], g + 1)
                sp.dma_start(out_v[:, g * TB:(g + 1) * TB, :], resid[:, g * TB:(g + 1) * TB, :]).then_inc(S["out_stored"], 16)
            sp.wait_ge(S["out_stored"], 16 * NODE_TURNS)

        @block.gpsimd
        def _(pool):
            pool.wait_ge(S["es_raw_in"], 16)
            nc.gpsimd.tensor_copy(es_hi.bitcast(F32R), es_in_f).then_inc(S["es_split"], 1)
            pool.wait_ge(S["es_split"], 1)
            nc.gpsimd.tensor_tensor(es_lo.bitcast(F32R), es_in_f, es_hi, ALU.subtract).then_inc(S["es_split"], 1)
            pool.wait_ge(S["es_split"], 2)
            for part, rows in ((es_hi, es_hl[0:8, :]), (es_lo, es_hl[8:16, :])):
                pool.dma_start(rows.rearrange("r e -> (r e)").rearrange("(p f) -> p f", p=P),
                               part).then_inc(S["es_stored"], 16)
            pool.wait_ge(S["es_stored"], 32)
            nc.gpsimd.memset(zT[:, 0:4], 0.0).then_inc(S["zeroed"], 1)
            pool.sem_inc(S["ysb_free"], 1)
            with pool.Fori(0, NODE_TURNS) as i:
                pool.wait_ge(S["y_sb"], i * TB + (TB + 2))
                pool.sem_inc(S["turn_pool"], 1)
                pool.dma_start(y_v[:, bass.ds(i * TB, TB), :], ysb).then_inc(S["y_stored"], 16)
                pool.wait_ge(S["y_stored"], i * 16 + 16)
                pool.sem_inc(S["ysb_free"], 1)
            pool.wait_ge(S["y_stored"], 16 * NODE_TURNS)
            pool.wait_ge(S["ctx_sb"], 1)

            def gather(k):
                for j in range(GT):
                    pool.indirect_dma_start(xg[:, k, j, :], None, y_dram[:], bass.IndirectOffsetOnAxis(
                        ap=idx_sb[:, k, j:j + 1], axis=0)).then_inc(rows_in[k], 16)

            for k in range(GROUPS_PER_TURN):
                pool.wait_ge(idx_in[k], 16)
                gather(k)
            with pool.Fori(1, EDGE_TURNS) as i:
                for k in range(GROUPS_PER_TURN):
                    pool.wait_ge(S["prod_ready"], i * 4 + (k - 3))
                    pool.sem_inc(S["turn_pool"], 1)
                    pool.wait_ge(idx_in[k], i * 16 + 16)
                    pool.sem_inc(S["turn_pool"], 1)
                    gather(k)
            pool.wait_ge(S["flag_ready"], 1)
            flag = pool.value_load(flag_i[0:1, 0:1], min_val=0, max_val=ET * P)
            pool.wait_ge(S["added"], EG + 3)
            with pool.If(flag > 0):
                with pool.Fori(0, ET) as t:
                    pool.wait_ge(idx_in[0], t * 16 + 16 * (EDGE_TURNS + 1))
                    pool.sem_inc(S["turn_pool"], 1)
                    pool.indirect_dma_start(xg[:, 0, 0, :], None, y_dram[:], bass.IndirectOffsetOnAxis(
                        ap=idx_sb[:, 0, 0:1], axis=0)).then_inc(S["stray_gathered"], 16)
                    pool.wait_ge(S["stray_gathered"], t * 16 + 16)
                    pool.sem_inc(S["turn_pool"], 1)
            with pool.Else():
                pool.sem_inc(S["turn_pool"], 1)
            pool.wait_ge(S["slots_ready"], 1)
            pool.wait_ge(S["zero_in"], 16)
            for t in range(NT):
                pool.indirect_dma_start(buf_dram[:], bass.IndirectOffsetOnAxis(ap=scat_i[:, t:t + 1], axis=0),
                                        xl[:, t, :], None).then_inc(S["scattered"], 16)
            pool.wait_ge(S["scattered"], 16 * NT)
            for s in range(2):
                pool.wait_ge(y_out[s], 16 * 4 * (E // 2))
            for t in range(NT):
                pool.indirect_dma_start(xl[:, t, :], None, ybuf_dram[:], bass.IndirectOffsetOnAxis(
                    ap=gath_i[:, t:t + 1], axis=0)).then_inc(back_in[t // TB], 16)

        @block.scalar
        def _(act):
            A = nc.scalar
            chain = Chain(act, S["act_chain"])
            act.dma_start(es_in_f, es).then_inc(S["es_raw_in"], 16)
            loads = [(wy[:], w_y), (ws[:], w_s), (wqkv[:], w_qkv), (gpre[:], g_pre), (wz[:], w_z), (fc1_sb[:], fc1),
                     (fc2_sb[:], fc2), (memkt[:], mem_kt), (memk[:], mem_k), (memv[:], mem_v), (wout[:], w_out),
                     (bout_b[:], b_out.partition_broadcast(P)), (gout_b[:], g_out.partition_broadcast(P)),
                     (gatew[:], gate_w), (gateb_b[:], gate_b.partition_broadcast(P))]
            for to, of in loads:
                act.dma_start(to, of).then_inc(S["weights_in"], 16)
            assert len(loads) == 15
            act.sem_inc(S["xT_sb"], 2)
            act.sem_inc(S["y_sb"], 2)
            act.sem_inc(S["qkv_sb"], 2)
            act.sem_inc(S["qT_sb"], 1)

            def x_transposed(i, j):
                act.wait_ge(S["xT_ps"], i * TB + (j + 1))
                act.wait_ge(S["kt_ps"], i + 1)
                A.copy(xT[:, j], ps[:, j % 2, 0:256].rearrange("p (k c) -> p k c", k=2)).then_inc(S["xT_sb"], 1)

            with act.Fori(0, NODE_TURNS) as i:
                act.wait_ge(S["var_ready"], i + 1)
                A.activation(col[:, 1, :], col[:, 0, :], ACT.Sqrt).then_inc(S["std_ready"], 1)
                act.wait_ge(S["xn_ready"], i + 1)
                for j in range(TB):
                    last = A.activation(sq_junk[:, j, :], xn[:, j, :], ACT.Square, accum_out=col[:, 3, j:j + 1])
                last.then_inc(S["act_chain"], 1)
                act.wait_ge(S["act_chain"], i + 1)
                A.activation(col[:, 4, :], col[:, 3, :], ACT.Sqrt).then_inc(S["norm_ready"], 1)
                x_transposed(i, 0)
                x_transposed(i, 1)
                for j in range(TB):
                    act.wait_ge(S["ys_ps"], i * TB + (j + 1))
                    if j == 0:
                        act.wait_ge(S["ysb_free"], i + 1)
                    A.activation(ysb[:, j, :], ps[:, 2 + j % 2, 0:256], ACT.Copy, scale=col[:, 7, j:j + 1]).then_inc(S["y_sb"], 1)
                    act.wait_ge(S["qkv_ps"], i * TB + (j + 1))
                    if j == 0:
                        act.wait_ge(S["qn_ready"], i + 1)
                    A.copy(qs[:, j, :], ps[:, 4 + j % 2, 0:HD])
                    A.copy(kv[:, bass.ds(i * TB + j, 1), :].rearrange("p a c -> p (a c)"),
                           ps[:, 4 + j % 2, HD:3 * HD]).then_inc(S["qkv_sb"], 1)
                    if j + 2 < TB:
                        x_transposed(i, j + 2)
                act.wait_ge(S["q_sub"], i + 1)
                A.activation(qs[:], qs[:], ACT.Exp).then_inc(S["q_exp"], 1)
                act.wait_ge(S["qT_ps"], i + 1)
                A.copy(zT[:, 4, bass.ds(i * (TB * P), TB * P)],
                       ps[:, 0:2, :].rearrange("p b c -> p (b c)")[:, 0:TB * P]).then_inc(S["qT_sb"], 1)
            chain.n = NODE_TURNS
            act.wait_ge(S["k_sub"], 1)
            A.activation(kv[:, :, 0:HD], kv[:, :, 0:HD], ACT.Exp)
            A.activation(memk[:], memk[:], ACT.Exp).then_inc(S["k_exp"], 1)

            act.sem_inc(S["z_evac"], 2)

            def evacuate(i, k):
                g1 = i * 4 + (k + 1)
                b = k % 2
                act.wait_ge(S["sel_done"], g1 + 2)
                act.wait_ge(S["added"], g1)
                bank = ps[:, 4 + b, 0:8 * WIN].rearrange("p (q w) -> p q w", q=8)
                A.copy(stage[0:64, b], bank[0:64, 0:4])
                A.copy(stage[64:128, b], bank[64:128, 4:8]).then_inc(S["z_evac"], 1)

            act.wait_ge(S["ctx_sb"], 1)
            def silu(s, n=CHUNK):
                A.activation(h_r[:, s, 0:n], ps[:, s, 0:n], ACT.Silu, scale=ES_SCALE)
                return A.activation(h_f[64:128, s, 0:n], ps[64:128, s, 0:n], ACT.Silu, scale=ES_SCALE)

            act.wait_ge(S["h_ready"], 1)
            silu(0).then_inc(S["silu_done"], 1)
            with act.Fori(0, EDGE_TURNS) as i:
                act.wait_ge(S["h_ready"], i * 2 + 2)
                act.wait_ge(S["w_ready"], i * 4 + 1)
                silu(1).then_inc(S["silu_done"], 1)
                evacuate(i, 0)
                act.wait_ge(S["h_ready"], i * 2 + 3)
                act.wait_ge(S["w_ready"], i * 4 + 2)
                silu(0).then_inc(S["silu_done"], 1)
                evacuate(i, 1)
                evacuate(i, 2)
                evacuate(i, 3)
            act.wait_ge(S["flag_ready"], 1)
            flag = act.value_load(flag_i[0:1, 0:1], min_val=0, max_val=ET * P)
            act.wait_ge(S["added"], EG + 3)
            with act.If(flag > 0):
                with act.Fori(0, ET) as t:
                    act.wait_ge(S["stray_step_pe"], t * (STRAY_TURNS + 2) + 1)
                    silu(0, P).then_inc(S["stray_step_act"], 1)
            with act.Else():
                act.sem_inc(S["turn_act"], 1)
            act.wait_ge(S["zst_ready"], 1)

            act.sem_inc(S["xlT_sb"], 1)
            with act.Fori(0, NT) as t:
                act.wait_ge(S["gnn_ps"], t + 1)
                A.copy(zst[:, 0], zT[:, :, bass.ds(t * P, P)]).then_inc(S["zst_ready"], 1)
                act.wait_ge(S["om_ready"], t + 1)
                A.activation(om_junk, om[:, 0, :], ACT.Square, accum_out=col[:, 0, 0:1]).then_inc(S["om_sq"], 1)
                act.wait_ge(S["om_sq"], t + 1)
                A.activation(col[:, 1, 0:1], col[:, 0, 0:1], ACT.Sqrt).then_inc(S["om_norm"], 1)
                act.wait_ge(S["x2_var"], t + 1)
                A.activation(col[:, 3, 0:1], col[:, 2, 0:1], ACT.Sqrt).then_inc(S["x2_std"], 1)
                act.wait_ge(S["xlT_ps"], t + 1)
                A.copy(xlT[:, 0], ps[:, 2, 0:256].rearrange("p (k c) -> p k c", k=2)).then_inc(S["xlT_sb"], 1)
            act.wait_ge(S["l_sub"], 1)
            A.activation(rt[:, 1, :], rt[:, 0, :], ACT.Exp).then_inc(S["l_exp"], 1)
            with act.Fori(0, E // 2) as i:
                for s in range(2):
                    act.wait_ge(we_in[s], i * 64 + 64)
                    act.wait_ge(S["yexp_ps"], i * 8 + (4 * s + 1))
                    for f in range(FB):
                        act.wait_ge(S["hid_ps"], i * (2 * FB) + s * FB + f + 1)
                        A.activation(hid[:, f, :], ps[:, 2 + f % 3, 0:CAP], ACT.Relu, bias=b1_sb[:, s, f:f + 1]).then_inc(S["hid_sb"], 1)
                    act.wait_ge(S["yst_ready"], i * 8 + (4 * s + 4))
                    act.sem_inc(S["turn_act"], 1)
                    e = i * 2 + s
                    for c in range(4):
                        rows = P if c < 3 else LAST_C
                        act.dma_start(ybuf_dram[bass.ds(e * SLOTS + c * P, rows), :], yst[0:rows, s, c, :]).then_inc(y_out[s], 16)

        @block.vector
        def _(dve):
            V = nc.vector
            chain = Chain(dve, S["dve_chain"])
            link = chain.link
            V.memset(es_r[:].bitcast(F32), 0.0)
            link(V.memset(fc1_r[:].bitcast(F32), 0.0))
            V.memset(kmx[:], -FLT_MAX)
            dve.wait_ge(S["weights_in"], 16 * 15)
            dve.wait_ge(S["consts_in"], 32)
            V.tensor_scalar(wy[:], wy[:], Y_SCALE, None, ALU.mult)
            V.tensor_scalar(ws[:], ws[:], S_SCALE, None, ALU.mult)
            V.tensor_scalar(wz[:], wz[:], Z_SCALE, None, ALU.mult)
            V.tensor_scalar(gout_b[:], gout_b[:], math.sqrt(D), None, ALU.mult)
            V.tensor_scalar(fc2_sb[:, 0:192], fc2_sb[:, 0:192], W_SCALE, None, ALU.mult)
            link(V.tensor_scalar(fc2_sb[:, 192:256], fc2_sb[:, 192:256], W_SCALE * INV_SQRT3, None, ALU.mult))
            V.tensor_copy(fc2_r[:, 0, :], fc2_sb[:])
            link(V.tensor_copy(fc1_hl[:, 0, :].bitcast(F32R), fc1_sb[:]))
            V.tensor_tensor(fc2_r[:, 1, :], fc2_sb[:], fc2_r[:, 0, :].bitcast(F32), ALU.subtract)
            link(V.tensor_tensor(fc1_hl[:, 1, :].bitcast(F32R), fc1_sb[:], fc1_hl[:, 0, :], ALU.subtract))
            link(V.tensor_scalar(fc1_hl[:, 1, :], fc1_hl[:, 1, :], cst[0:32, C_LOW:C_END], None, ALU.mult))
            V.scalar_tensor_tensor(fc1_r[0:32, :], fc1_hl[:, 0, :], cst[0:32, C_HIGH:C_LOW], fc1_hl[:, 1, :], ALU.mult, ALU.add)
            for k in range(2):
                last = V.tensor_scalar(wqkv[:, k, :], wqkv[:, k, :], gpre[:, k:k + 1], math.sqrt(D), ALU.mult, ALU.mult)
            last.then_inc(S["scaled"], 1)
            dve.sem_inc(S["s_sb"], 2)
            dve.sem_inc(S["kmax_sb"], 1)
            dve.sem_inc(S["qn_ready"], 1)

            with dve.Fori(0, NODE_TURNS) as i:
                chain.enter(i, 10)
                xc = resid[:, bass.ds(i * TB, TB), :]
                dve.wait_ge(S["x_in"], i * 16 + 16)
                dve.sem_inc(S["turn_dve"], 1)
                for j in range(TB):
                    last = V.bn_stats(st[:, j, :], resid[:, bass.ds(i * TB + j, 1), :].rearrange("p a c -> p (a c)"))
                link(last)
                dve.sem_inc(S["turn_dve"], 1)
                for j in range(TB):
                    last = V.bn_aggr(mv[:, j, :], st[:, j, :])
                link(last)
                V.tensor_scalar(col[:, 0, :], mv[:, :, 1], EPS, None, ALU.add).then_inc(S["var_ready"], 1)
                dve.wait_ge(S["std_ready"], i + 1)
                link(V.reciprocal(col[:, 2, :], col[:, 1, :]))
                for j in range(TB):
                    last = V.tensor_scalar(xn[:, j, :], resid[:, bass.ds(i * TB + j, 1), :].rearrange("p a c -> p (a c)"),
                                           mv[:, j, 0:1], col[:, 2, j:j + 1], ALU.subtract, ALU.mult)
                last.then_inc(S["xn_ready"], 1)
                dve.wait_ge(S["xn_ready"], i + 1)
                link(V.tensor_tensor(xc, xc, xn[:], ALU.add))
                dve.wait_ge(S["norm_ready"], i + 1)
                link(V.tensor_scalar(col[:, 5, :], col[:, 4, :], 1e-12, None, ALU.max))
                link(V.reciprocal(col[:, 6, :], col[:, 5, :]))
                V.tensor_tensor(col[:, 7, :], col[:, 5, :], node_a_sb[:, bass.ds(i * TB, TB)], ALU.mult)
                for j in range(TB):
                    V.tensor_scalar(xm[:, j, :], xn[:, j, :], col[:, 6, j:j + 1], None, ALU.mult).then_inc(S["xm_ready"], 1)
                dve.wait_ge(S["xm_ready"], i * TB + TB)
                for j in range(TB):
                    dve.wait_ge(S["y_sb"], i * TB + (j + 3))
                    xt = resid[:, bass.ds(i * TB + j, 1), :].rearrange("p a c -> p (a c)")
                    V.scalar_tensor_tensor(xt, ps[:, 2 + j % 2, 256:512], col[:, 7, j:j + 1], xt, ALU.mult, ALU.add).then_inc(S["s_sb"], 1)
                dve.wait_ge(S["qkv_sb"], i * TB + (TB + 2))
                q4 = qs[:].rearrange("p t (h d) -> p (t h) d", d=DH)
                n4 = qn[:].rearrange("p t (h d) -> p (t h) d", d=DH)
                link(V.tensor_reduce(qcol[:, 0, :], q4, AX.X, ALU.max))
                V.tensor_tensor(q4, q4, bc(qcol[:, 0, :], 2, DH), ALU.subtract).then_inc(S["q_sub"], 1)
                dve.wait_ge(S["q_exp"], i + 1)
                link(V.tensor_reduce(qcol[:, 0, :], q4, AX.X, ALU.add))
                link(V.reciprocal(qcol[:, 1, :], qcol[:, 0, :]))
                dve.wait_ge(S["qT_sb"], i + 1)
                V.tensor_tensor(n4, q4, bc(qcol[:, 1, :], 2, DH), ALU.mult).then_inc(S["qn_ready"], 1)
                dve.wait_ge(S["kt_ps"], i + 2)
                link(V.tensor_reduce(kmx[:, 1:2], ps[:, 6:8, :].rearrange("p b c -> p (b c)")[:, 0:TB * P], AX.X, ALU.max))
                V.tensor_tensor(kmx[:, 0:1], kmx[:, 0:1], kmx[:, 1:2], ALU.max).then_inc(S["kmax_sb"], 1)
                dve.wait_ge(S["kmax_sb"], i + 2)
            chain.leave(NODE_TURNS)

            link(V.tensor_reduce(kmx[:, 1:2], memkt[:], AX.X, ALU.max))
            link(V.tensor_tensor(kmx[:, 0:1], kmx[:, 0:1], kmx[:, 1:2], ALU.max))
            V.tensor_scalar(xn[:, 0, 0:P], ident, kmx[:, 0:1], None, ALU.mult).then_inc(S["kdiag"], 1)
            dve.wait_ge(S["kmax_b"], 1)
            dve.wait_ge(S["qkv_sb"], NT + 2)
            V.tensor_tensor(kv[:, :, 0:HD], kv[:, :, 0:HD], bc(ps[:, 0, 0:HD], 1, NT), ALU.subtract)
            V.tensor_tensor(memk[:], memk[:], ps[0:NUM_MEM, 0, 0:HD], ALU.subtract).then_inc(S["k_sub"], 1)
            dve.wait_ge(S["k_exp"], 1)
            V.tensor_scalar(kv[:, NT - 1, 0:HD], kv[:, NT - 1, 0:HD], valid, None, ALU.mult).then_inc(S["kdiag"], 1)
            dve.wait_ge(S["ctx_ps"], 1)
            link(V.reciprocal(small[:, 0:1], ps[:, 2, 0:1]))
            V.tensor_tensor(xn[:, 1, 0:P], ps[:, 1, 0:HD], block_mask, ALU.mult).then_inc(S["ctx_sb"], 1)
            dve.wait_ge(S["mixw_ps"], 1)
            V.tensor_scalar(mix_w[:], ps[:, 3, 0:D], small[:, 0:1], SM_SCALE, ALU.mult, ALU.mult).then_inc(S["mixw_sb"], 1)
            dve.wait_ge(S["mixw_sb"], 1)

            dve.wait_ge(S["edges_in"], 48)
            V.tensor_copy(first_f, first_i[0:1, 1:1 + EG]).then_inc(S["first_row"], 1)
            link(V.tensor_copy(relf, dst_i[:]))
            dve.wait_ge(S["first_ps"], 1)
            rel3 = relf.rearrange("p (g j) -> p g j", j=GT)
            dst3 = stray_dst.rearrange("p (g j) -> p g j", j=GT)
            V.tensor_copy(stray_dst, relf)
            link(V.tensor_tensor(rel3, rel3, bc(ps[:, 7, 0:EG], 2, GT), ALU.subtract))
            link(V.tensor_scalar(inw, relf, 0.0, None, ALU.is_ge))
            link(V.scalar_tensor_tensor(inw, relf, float(WIN), inw, ALU.is_lt, ALU.mult))
            dve.wait_ge(S["zero_in"], 16)
            link(V.scalar_tensor_tensor(junk, inw, -8192.0, stray_dst, ALU.mult, ALU.add))
            V.tensor_copy(stray_dst, junk)
            V.tensor_reduce(flag_f[:, 0:1], inw, AX.X, ALU.add).then_inc(S["strays_sum"], 1)
            V.memset(stage[:], 0.0)
            dve.wait_ge(S["flag_ps"], 1)
            V.tensor_scalar(flag_i[0:1, 0:1], ps[0:1, 6, 0:1], -1.0, float(ET * P), ALU.mult, ALU.add).then_inc(S["flag_ready"], 1)
            dve.wait_ge(S["flag_ready"], 1)
            dve.sem_inc(S["added"], 1)

            def low_part(s, n=CHUNK):
                return V.tensor_tensor(h_r[64:128, s, 0:n], h_f[64:128, s, 0:n], h_r[64:128, s, 0:n].bitcast(F32), ALU.subtract)

            def products(i, k):
                g1 = i * 4 + (k + 1)
                b = k % 2
                dve.wait_ge(rows_in[k], i * (16 * GT) + 16 * GT)
                dve.wait_ge(S["w_ready"], g1)
                dve.wait_ge(S["sel_done"], g1)
                w = ps[:, 2 + b, :].rearrange("p (j c) -> p j c", j=GT)
                V.tensor_tensor(prod[:, b, :, 0:128].rearrange("p j (a u) -> p j a u", a=2),
                                w[:, :, 0:128].rearrange("p j (a u) -> p j a u", a=2),
                                bc(xg[:, k, :, 0:64], 2, 2), ALU.mult)
                for j in range(GT):
                    last = V.tensor_tensor(prod[:, b, j, 128:512].rearrange("p (c a u) -> p c a u", c=3, a=2),
                                           bc(w[:, j, 128:256].rearrange("p (a u) -> p a u", a=2), 1, 3),
                                           bc(xg[:, k, j, 64:256].rearrange("p (c u) -> p c u", c=3), 2, 2), ALU.mult)
                last.then_inc(S["prod_ready"], 1)

            def add(i, k, first):
                g = i * 4 + (k + 1)
                b = k % 2
                base = dve.value_load(first_i[0:1, bass.ds(g, 1)] if first is None else first, min_val=0, max_val=N - 1)
                z = zT[:, 0:4, bass.ds(base, WIN)]
                dve.wait_ge(S["z_evac"], g + 2)
                dve.wait_ge(S["added"], g + 1)
                V.tensor_tensor(z, z, stage[:, b % 2], ALU.add).then_inc(S["added"], 1)

            def selection(i, s):
                dve.wait_ge(S["sel_done"], i * 4 + (2 * s + 1))
                dve.sem_inc(S["turn_dve"], 1)
                link(V.tensor_tensor(hot[:, s], bc(iota[:, 0:WIN], 1, 4), bc(relf[:, bass.ds(i * TPT + 4 * s, 4)], 2, WIN), ALU.is_equal))
                V.tensor_tensor(sel[:, s], bc(hot[:, s], 2, 4), bc(ea_sb[:, bass.ds(i * TPT + 4 * s, 4), :], 3, WIN), ALU.mult)

            dve.wait_ge(S["silu_done"], 1)
            low_part(0).then_inc(S["lo_ready"], 1)
            with dve.Fori(0, EDGE_TURNS) as i:
                chain.enter(i, 2)
                selection(i, 0)
                products(i, 0)
                dve.wait_ge(S["silu_done"], i * 2 + 2)
                low_part(1).then_inc(S["lo_ready"], 1)
                add(i, -1, None)
                products(i, 1)
                add(i, 0, None)
                selection(i, 1)
                products(i, 2)
                dve.wait_ge(S["silu_done"], i * 2 + 3)
                low_part(0).then_inc(S["lo_ready"], 1)
                add(i, 1, None)
                products(i, 3)
                add(i, 2, None)
            chain.leave(EDGE_TURNS)
            add(EDGE_TURNS, -1, first_i[0:1, EG:EG + 1])
            dve.wait_ge(S["added"], EG + 2)
            dve.sem_inc(S["added"], 1)
            flag = dve.value_load(flag_i[0:1, 0:1], min_val=0, max_val=ET * P)
            with dve.If(flag > 0):
                dve.sem_inc(S["stray_step_dve"], 1)
                with dve.Fori(0, ET) as t:
                    base = STRAY_TURNS + 3
                    dve.wait_ge(S["stray_step_act"], t + 1)
                    low_part(0, P).then_inc(S["stray_step_dve"], 1)
                    dve.wait_ge(S["stray_gathered"], t * 16 + 16)
                    dve.wait_ge(S["stray_step_pe"], t * (STRAY_TURNS + 2) + 2)
                    w = ps[:, 2, 0:256]
                    V.tensor_tensor(prod[:, 0, 0, 0:128].rearrange("p (a u) -> p a u", a=2),
                                    w[:, 0:128].rearrange("p (a u) -> p a u", a=2), bc(xg[:, 0, 0, 0:64], 1, 2), ALU.mult)
                    V.tensor_tensor(prod[:, 0, 0, 128:512].rearrange("p (c a u) -> p c a u", c=3, a=2),
                                    bc(w[:, 128:256].rearrange("p (a u) -> p a u", a=2), 1, 3),
                                    bc(xg[:, 0, 0, 64:256].rearrange("p (c u) -> p c u", c=3), 2, 2), ALU.mult)
                    V.tensor_copy(stray_cur[:, 0:1], stray_dst[:, bass.ds(t, 1)]).then_inc(S["stray_step_dve"], 1)
                    dve.wait_ge(S["stray_step_dve"], t * base + 3)
                    dve.sem_inc(S["turn_dve"], 1)
                    with dve.Fori(0, STRAY_TURNS) as n:
                        step = t * (3 * STRAY_TURNS) + n * 3
                        V.tensor_scalar(stray_hot, iota, stray_cur[:, 0:1], None, ALU.is_equal).then_inc(S["kdiag"], 1)
                        dve.wait_ge(S["kdiag"], step + 3)
                        V.tensor_scalar(stray_cur[:, 0:1], stray_cur[:, 0:1], -float(STRAY_WIN), None, ALU.add).then_inc(S["kdiag"], 1)
                        dve.wait_ge(S["kdiag"], step + 4)
                        V.tensor_tensor(stray_sel, bc(stray_hot, 1, 4),
                                        bc(ea_sb[:, bass.ds(t, 1), :].rearrange("p a c -> p (a c)"), 2, STRAY_WIN), ALU.mult).then_inc(S["kdiag"], 1)
                        dve.wait_ge(S["kdiag"], step + 5)
                        dve.wait_ge(S["stray_step_pe"], t * (STRAY_TURNS + 2) + n + 3)
                        cols = bass.ds(n * STRAY_WIN, STRAY_WIN)
                        V.tensor_tensor(zT[0:64, 3, cols], zT[0:64, 3, cols], ps[0:64, 4, 0:STRAY_WIN], ALU.add)
                        V.tensor_tensor(zT[64:128, 0:3, cols], zT[64:128, 0:3, cols],
                                        ps[64:128, 4, STRAY_WIN:4 * STRAY_WIN].rearrange("p (c w) -> p c w", c=3), ALU.add)
                        V.tensor_tensor(zT[0:64, 0:3, cols], zT[0:64, 0:3, cols], ps[0:64, 5:8, 0:STRAY_WIN], ALU.add)
                        V.tensor_tensor(zT[64:128, 3, cols], zT[64:128, 3, cols], ps[64:128, 5, STRAY_WIN:2 * STRAY_WIN], ALU.add).then_inc(S["stray_step_dve"], 1)
                        dve.wait_ge(S["stray_step_dve"], t * base + n + 4)
                    dve.sem_inc(S["stray_step_dve"], 1)
            with dve.Else():
                dve.sem_inc(S["turn_dve"], 1)
            dve.sem_inc(S["zst_ready"], 1)

            with dve.Fori(0, NT) as t:
                chain.enter(t, 8)
                xt = resid[:, bass.ds(t, 1), :].rearrange("p a c -> p (a c)")
                dve.wait_ge(S["gnn_ps"], t + 2)
                V.tensor_tensor(om[:, 0, :], ps[:, 0, 256:512], bout_b[:], ALU.add).then_inc(S["om_ready"], 1)
                link(V.scalar_tensor_tensor(xt, ps[:, 0, 0:256], node_a_sb[:, bass.ds(t, 1)], xt, ALU.mult, ALU.add))
                dve.wait_ge(S["om_norm"], t + 1)
                link(V.tensor_scalar(col[:, 4, 0:1], col[:, 1, 0:1], 1e-12, None, ALU.max))
                link(V.reciprocal(col[:, 5, 0:1], col[:, 4, 0:1]))
                link(V.scalar_tensor_tensor(om2[:, 0, :], om[:, 0, :], col[:, 5, 0:1], gout_b[:], ALU.mult, ALU.mult))
                link(V.tensor_tensor(xt, xt, om2[:, 0, :], ALU.add))
                dve.sem_inc(S["turn_dve"], 1)
                link(V.bn_stats(cst6[:, 0, 0:6], xt))
                dve.sem_inc(S["turn_dve"], 1)
                link(V.bn_aggr(cst6[:, 1, 0:2], cst6[:, 0, 0:6]))
                V.tensor_scalar(col[:, 2, 0:1], cst6[:, 1, 1:2], EPS, None, ALU.add).then_inc(S["x2_var"], 1)
                dve.wait_ge(S["x2_std"], t + 1)
                link(V.reciprocal(col[:, 6, 0:1], col[:, 3, 0:1]))
                dve.wait_ge(S["gate_ps"], t + 1)
                xlt = xl[:, bass.ds(t, 1), :].rearrange("p a c -> p (a c)")
                V.tensor_scalar(om2[:, 1, :], xt, cst6[:, 1, 0:1], col[:, 6, 0:1], ALU.subtract, ALU.mult).then_inc(S["xl_ready"], 1)
                V.tensor_scalar(xlt, xt, cst6[:, 1, 0:1], col[:, 6, 0:1], ALU.subtract, ALU.mult)
                dve.wait_ge(S["gate_ps"], t + 2)
                V.tensor_tensor(logits[:, bass.ds(t * E, E)], ps[:, 4, 0:E], gateb_b[:], ALU.add).then_inc(S["logit_sb"], 1)
            chain.leave(NT)
            dve.wait_ge(S["logit_sb"], NT)

            l3 = logits[:].rearrange("p (t e) -> p t e", e=E)

            def r(n):
                return rt[:, n, :].rearrange("p (t e) -> p t e", e=E)

            link(V.tensor_reduce(rcol[:, 0, :], l3, AX.X, ALU.max))
            V.tensor_tensor(r(0), l3, bc(rcol[:, 0, :], 2, E), ALU.subtract).then_inc(S["l_sub"], 1)
            dve.wait_ge(S["l_exp"], 1)
            link(V.tensor_reduce(rcol[:, 1, :], r(1), AX.X, ALU.add))
            link(V.reciprocal(rcol[:, 2, :], rcol[:, 1, :]))
            link(V.tensor_scalar(r(2), r(0), 0.0, None, ALU.is_ge))
            link(V.scalar_tensor_tensor(r(3), r(2), -float(E), bc(iota8, 1, NT), ALU.mult, ALU.add))
            link(V.tensor_reduce(rcol[:, 3, :], r(3), AX.X, ALU.min))
            link(V.tensor_tensor(r(4), r(3), bc(rcol[:, 3, :], 2, E), ALU.is_equal))
            V.tensor_scalar(rt[:, 4, (NT - 1) * E:], rt[:, 4, (NT - 1) * E:], valid, None, ALU.mult).then_inc(S["hot_ready"], 1)
            dve.wait_ge(S["hot_ready"], 1)
            dve.wait_ge(S["pre_ps"], 1)
            tot_et = rt[:, 5, :].rearrange("p (e t) -> p e t", t=NT)
            link(V.tensor_copy(tot_et, ps[:, 6, 0:NT * E].rearrange("p (t e) -> p e t", e=E)))
            link(V.tensor_tensor_scan(rt[:, 6, :], reset, rt[:, 5, :], 0.0, ALU.mult, ALU.add))
            link(V.tensor_tensor(rt[:, 7, :], rt[:, 6, :], rt[:, 5, :], ALU.subtract))
            link(V.tensor_tensor(r(8), ps[:, 5, 0:NT * E].rearrange("p (t e) -> p t e", e=E),
                                 rt[:, 7, :].rearrange("p (e t) -> p t e", t=NT), ALU.add))
            link(V.tensor_tensor(r(9), r(8), r(4), ALU.mult))
            link(V.tensor_reduce(rcol[:, 4, :], r(9), AX.X, ALU.add))
            link(V.tensor_scalar(rcol[:, 5, :], rcol[:, 4, :], float(CAP), None, ALU.is_le))
            link(V.tensor_scalar(rcol[:, 5, NT - 1:NT], rcol[:, 5, NT - 1:NT], valid, None, ALU.mult))
            link(V.tensor_scalar(rcol[:, 6, :], rcol[:, 3, :], float(E), float(SLOTS), ALU.add, ALU.mult))
            link(V.tensor_scalar(rcol[:, 7, :], rcol[:, 4, :], -1.0, None, ALU.add))
            link(V.tensor_tensor(rcol[:, 8, :], rcol[:, 6, :], rcol[:, 7, :], ALU.add))
            link(V.tensor_tensor(rcol[:, 8, :], rcol[:, 8, :], trash_row, ALU.subtract))
            link(V.tensor_tensor(rcol[:, 8, :], rcol[:, 8, :], rcol[:, 5, :], ALU.mult))
            link(V.tensor_tensor(scat_i[:], rcol[:, 8, :], trash_row, ALU.add))
            link(V.tensor_scalar(rcol[:, 9, :], rcol[:, 7, :], float(CAP - 1), 0.0, ALU.min, ALU.max))
            V.tensor_tensor(rcol[:, 10, :], rcol[:, 2, :], rcol[:, 5, :], ALU.mult)
            V.tensor_tensor(gath_i[:], rcol[:, 6, :], rcol[:, 9, :], ALU.add).then_inc(S["slots_ready"], 1)

            dve.sem_inc(S["xbT_sb"], 1)
            with dve.Fori(0, E // 2) as i:
                for s in range(2):
                    for k in range(2):
                        dve.wait_ge(S["xbT_ps"], i * 4 + (2 * s + k + 1))
                        V.tensor_copy(xbT[:, k, 0:CAP], ps[:, k, 0:CAP]).then_inc(S["xbT_sb"], 1)
                    dve.wait_ge(we_in[s], i * 64 + 64)
                    for c in range(4):
                        dve.wait_ge(S["yexp_ps"], i * 8 + (4 * s + c + 2))
                        rows = P if c < 3 else LAST_C
                        V.tensor_tensor(yst[0:rows, s, c, :], ps[0:rows, 5 + c % 2, 0:D], b2_sb[0:rows, s, :], ALU.add).then_inc(S["yst_ready"], 1)
                    dve.wait_ge(y_out[s], i * 64 + 64)
                    dve.sem_inc(S["turn_dve"], 1)
            for g in range(NODE_TURNS):
                dve.wait_ge(back_in[g], 16 * TB)
                y = xl[:, g * TB:(g + 1) * TB, :]
                big = zflat[:, 0:TB * D].rearrange("p (t c) -> p t c", t=TB)
                low = zflat[:, 1280:1280 + TB * D].rearrange("p (t c) -> p t c", t=TB)
                fin = zflat[:, 2560:2560 + TB * D].rearrange("p (t c) -> p t c", t=TB)
                link(V.tensor_tensor(y, y, bc(rcol[:, 10, g * TB:(g + 1) * TB], 2, D), ALU.mult))
                V.tensor_scalar(fin.bitcast(I32), y, 0.0, 0.0, ALU.mult, ALU.is_equal)
                link(V.tensor_scalar(big, y, FLT_MAX, 1e4, ALU.is_gt, ALU.mult))
                link(V.tensor_scalar(low, y, -FLT_MAX, -1e4, ALU.is_lt, ALU.mult))
                link(V.tensor_tensor(big, big, low, ALU.add))
                link(V.copy_predicated(big, fin.bitcast(I32), y))
                x2 = resid[:, g * TB:(g + 1) * TB, :]
                V.tensor_tensor(x2, x2, big, ALU.add).then_inc(S["out_ready"], 1)

        @block.tensor
        def _(pe):
            T = nc.tensor

            def keep_busy(n):
                for _ in range(n):
                    T.matmul(ps[:, 3, :], ident, cst[:, 0:512], start=True, stop=True)

            pe.wait_ge(S["scaled"], 1)
            pe.sem_inc(S["kt_ps"], 1)

            def transposes(i, j):
                pe.wait_ge(S["xm_ready"], i * TB + (j + 1))
                if j == 0:
                    pe.wait_ge(S["qT_sb"], i + 1)
                else:
                    pe.wait_ge(S["xT_sb"], i * TB + (j + 1))
                for k in range(2):
                    last = T.transpose(ps[:, j % 2, k * P:(k + 1) * P], xm[:, j, k * P:(k + 1) * P], ident)
                last.then_inc(S["xT_ps"], 1)

            with pe.Fori(0, NODE_TURNS) as i:
                transposes(i, 0)
                transposes(i, 1)
                for j in range(TB):
                    n = i * TB + (j + 1) + (1 if j == 0 else 0)
                    pe.wait_ge(S["xT_sb"], i * TB + (j + 3))
                    pe.wait_ge(S["y_sb"], n)
                    pe.wait_ge(S["s_sb"], n)
                    for k in range(2):
                        T.matmul(ps[:, 2 + j % 2, k * P:(k + 1) * P], xT[:, j, k, :], wy[:, k, :], start=(k == 0), stop=False, skip_group_check=True)
                    for k in range(2):
                        last = T.matmul(ps[:, 2 + j % 2, 256 + k * P:256 + (k + 1) * P], xT[:, j, k, :], ws[:, k, :], start=False, stop=(k == 1), skip_group_check=True)
                    last.then_inc(S["ys_ps"], 1)
                    pe.wait_ge(S["qkv_sb"], n)
                    for k in range(2):
                        last = T.matmul(ps[:, 4 + j % 2, 0:3 * HD], xT[:, j, k, :], wqkv[:, k, :], start=(k == 0), stop=(k == 1))
                    last.then_inc(S["qkv_ps"], 1)
                    if j + 2 < TB:
                        transposes(i, j + 2)
                pe.wait_ge(S["kmax_sb"], i + 1)
                for n, (a, b) in enumerate(((0, 2), (2, 4), (4, 5))):
                    bank, c0 = 6 + n // 2, 256 * (n % 2)
                    for k in range(2):
                        last = T.matmul(ps[:, bank, c0:c0 + (b - a) * P], wqkv[:, k, HD:2 * HD], xT[:, a:b, k, :],
                                        start=(k == 0), stop=(k == 1))
                last.then_inc(S["kt_ps"], 1)
                pe.wait_ge(S["qn_ready"], i + 2)
                pe.wait_ge(S["xT_sb"], i * TB + (TB + 2))
                for j in range(TB):
                    last = T.transpose(ps[:, j // 4, (j % 4) * P:(j % 4 + 1) * P], qn[:, j, :], ident)
                last.then_inc(S["qT_ps"], 1)
            pe.wait_ge(S["kdiag"], 1)
            pe.wait_ge(S["qT_sb"], NODE_TURNS + 1)
            T.matmul(ps[:, 0, 0:P], ones, xn[:, 0, 0:P], start=True, stop=True).then_inc(S["kmax_b"], 1)
            pe.wait_ge(S["kdiag"], 2)
            pe.wait_ge(S["k_exp"], 1)
            pe.wait_ge(S["y_sb"], NT + 2)
            pe.wait_ge(S["s_sb"], NT + 2)
            for t in range(NT):
                T.matmul(ps[:, 1, 0:HD], kv[:, t, HD:2 * HD], kv[:, t, 0:HD], start=(t == 0), stop=False)
                T.matmul(ps[:, 2, 0:1], kv[:, t, 0:HD], ones[:, 0:1], start=(t == 0), stop=False)
            T.matmul(ps[:, 1, 0:HD], memv[:], memk[:], start=False, stop=True)
            T.matmul(ps[:, 2, 0:1], memk[:], ones[0:NUM_MEM, 0:1], start=False, stop=True).then_inc(S["ctx_ps"], 1)
            pe.wait_ge(S["ctx_sb"], 1)
            T.matmul(ps[:, 3, 0:D], xn[:, 1, 0:P], wout[:], start=True, stop=True).then_inc(S["mixw_ps"], 1)
            pe.wait_ge(S["first_row"], 1)
            T.matmul(ps[:, 7, 0:EG], ones[0:1, :], first_f, start=True, stop=True).then_inc(S["first_ps"], 1)
            pe.wait_ge(S["strays_sum"], 1)
            T.matmul(ps[0:1, 6, 0:1], flag_f[:, 0:1], ones[:, 0:1], start=True, stop=True).then_inc(S["flag_ps"], 1)
            pe.sem_inc(S["sel_done"], 2)

            def hidden(s, landed, silus):
                pe.wait_ge(es_in[s], landed)
                if silus is not None:
                    pe.wait_ge(S["silu_done"], silus)
                T.matmul(ps[:, s, :], fc1_r[:], es_r[:, s, :], start=True, stop=True).then_inc(S["h_ready"], 1)

            def tile_weights(out, s, c0):
                for part in range(2):
                    last = T.matmul(out, h_r[:, s, c0:c0 + P], fc2_r[:, part, :], start=(part == 0), stop=(part == 1))
                return last

            def weights(k, lows, free):
                pe.wait_ge(S["lo_ready"], lows)
                if free is not None:
                    pe.wait_ge(S["prod_ready"], free)
                for j in range(GT):
                    c0 = (GT * (k % 2) + j) * P
                    last = tile_weights(ps[:, 2 + k % 2, j * 256:(j + 1) * 256], k // 2, c0)
                last.then_inc(S["w_ready"], 1)

            def sums(i, k):
                g1 = i * 4 + (k + 1)
                b = k % 2
                pe.wait_ge(S["prod_ready"], g1)
                pe.wait_ge(S["z_evac"], g1)
                bank = ps[:, 4 + b, 0:8 * WIN].rearrange("p (q w) -> p q w", q=8)
                for j in range(GT):
                    m = sel[:, k // 2, (k % 2) * GT + j]
                    T.matmul(bank[:, 3:7], prod[:, b, j, 0:P], m, start=(j == 0), stop=False, skip_group_check=True)
                    for c in range(1, 4):
                        last = T.matmul(bank[:, c - 1:8:8 - c], prod[:, b, j, c * P:(c + 1) * P], m[:, 0:c + 1:c],
                                        start=False, stop=(j == GT - 1 and c == 3), skip_group_check=True)
                last.then_inc(S["sel_done"], 1)

            hidden(0, 32, None)
            pe.wait_ge(S["flag_ready"], 1)
            keep_busy(5)
            weights(0, 1, None)
            with pe.Fori(0, EDGE_TURNS) as i:
                hidden(1, i * 32 + 32, i * 2 + 1)
                weights(1, i * 2 + 1, None)
                sums(i, 0)
                hidden(0, i * 32 + 64, i * 2 + 1)
                weights(2, i * 2 + 2, i * 4 + 1)
                sums(i, 1)
                weights(3, i * 2 + 2, i * 4 + 2)
                sums(i, 2)
                weights(0, i * 2 + 3, i * 4 + 3)
                sums(i, 3)
            pe.wait_ge(S["flag_ready"], 1)
            flag = pe.value_load(flag_i[0:1, 0:1], min_val=0, max_val=ET * P)
            pe.wait_ge(S["added"], EG + 3)
            with pe.If(flag > 0):
                with pe.Fori(0, ET) as t:
                    base = STRAY_TURNS + 3
                    pe.wait_ge(es_in[1], t * 32 + 32 * (EDGE_TURNS + 1))
                    T.matmul(ps[:, 0, 0:P], fc1_r[:], es_r[:, 1, 0:P], start=True, stop=True).then_inc(S["stray_step_pe"], 1)
                    pe.wait_ge(S["stray_step_dve"], t * base + 2)
                    tile_weights(ps[:, 2, 0:256], 0, 0).then_inc(S["stray_step_pe"], 1)
                    with pe.Fori(0, STRAY_TURNS) as n:
                        pe.wait_ge(S["kdiag"], t * (3 * STRAY_TURNS) + n * 3 + 5)
                        pe.wait_ge(S["stray_step_dve"], t * base + n + 3)
                        T.matmul(ps[:, 4, 0:4 * STRAY_WIN], prod[:, 0, 0, 0:P], stray_sel, start=True, stop=True)
                        for c in range(1, 4):
                            T.matmul(ps[:, 4 + c, 0:STRAY_WIN], prod[:, 0, 0, c * P:(c + 1) * P], stray_sel[:, 0, :],
                                     start=True, stop=False, skip_group_check=True)
                            last = T.matmul(ps[:, 5, STRAY_WIN:2 * STRAY_WIN], prod[:, 0, 0, c * P:(c + 1) * P], stray_sel[:, c, :],
                                            start=False, stop=(c == 3), skip_group_check=True)
                        last.then_inc(S["stray_step_pe"], 1)
            with pe.Else():
                pe.sem_inc(S["turn_pe"], 1)
            pe.wait_ge(S["zst_ready"], 1)

            pe.sem_inc(S["gnn_ps"], 1)
            pe.sem_inc(S["gate_ps"], 1)
            with pe.Fori(0, NT) as t:
                pe.wait_ge(S["zst_ready"], t + 2)
                for b, c0 in ((3, 0), (0, 64), (1, 128), (2, 192)):
                    T.matmul(ps[:, 0, c0:c0 + MUL], zst[:, 0, b, :], wz[:, b, :], start=(b == 3), stop=False, skip_group_check=True)
                T.matmul(ps[:, 0, 256:512], zst[:, 0, 4, :], mix_w[:], start=False, stop=True, skip_group_check=True).then_inc(S["gnn_ps"], 1)
                pe.wait_ge(S["xl_ready"], t + 1)
                for k in range(2):
                    last = T.transpose(ps[:, 2, k * P:(k + 1) * P], om2[:, 1, k * P:(k + 1) * P], ident)
                last.then_inc(S["xlT_ps"], 1)
                pe.wait_ge(S["xlT_sb"], t + 2)
                for k in range(2):
                    last = T.matmul(ps[:, 4, 0:E], xlT[:, 0, k, :], gatew[:, k, :], start=(k == 0), stop=(k == 1))
                last.then_inc(S["gate_ps"], 1)
                pe.wait_ge(S["logit_sb"], t + 1)
                pe.sem_inc(S["turn_pe"], 1)
            pe.wait_ge(S["hot_ready"], 1)
            T.matmul(ps[:, 5, 0:NT * E], tri, rt[:, 4, :], start=True, stop=True)
            T.matmul(ps[:, 6, 0:NT * E], ones, rt[:, 4, :], start=True, stop=True).then_inc(S["pre_ps"], 1)
            pe.wait_ge(S["slots_ready"], 1)
            pe.sem_inc(S["yexp_ps"], 1)
            with pe.Fori(0, E // 2) as i:
                for s in range(2):
                    pe.wait_ge(xb_in[s], i * 32 + 32)
                    pe.wait_ge(S["xbT_sb"], i * 4 + (2 * s + 1))
                    for k in range(2):
                        for c in range(4):
                            rows = P if c < 3 else LAST_C
                            last = T.transpose(ps[:, k, c * P:c * P + rows], xb[0:rows, s, c, k * P:(k + 1) * P], ident[0:rows, 0:rows])
                        last.then_inc(S["xbT_ps"], 1)
                    pe.wait_ge(we_in[s], i * 64 + 64)
                    pe.wait_ge(S["xbT_sb"], i * 4 + (2 * s + 3))
                    for f in range(FB):
                        if f >= 3:
                            pe.wait_ge(S["hid_sb"], i * (2 * FB) + s * FB + f - 2)
                        for k in range(2):
                            last = T.matmul(ps[:, 2 + f % 3, 0:CAP], w1_sb[:, s, k, f * P:(f + 1) * P], xbT[:, k, 0:CAP],
                                            start=(k == 0), stop=(k == 1))
                        last.then_inc(S["hid_ps"], 1)
                    pe.wait_ge(S["hid_sb"], i * (2 * FB) + (s + 1) * FB)
                    for c in range(4):
                        if c >= 2:
                            pe.wait_ge(S["yst_ready"], i * 8 + 4 * s + c - 1)
                        rows = P if c < 3 else LAST_C
                        for f in range(FB):
                            last = T.matmul(ps[0:rows, 5 + c % 2, 0:D], hid[:, f, c * P:c * P + rows], w2_sb[:, s, f, :],
                                            start=(f == 0), stop=(f == FB - 1))
                        last.then_inc(S["yexp_ps"], 1)
                    pe.wait_ge(S["yst_ready"], i * 8 + (4 * s + 4))
                    pe.sem_inc(S["turn_pe"], 1)


def kernel(**inputs):
    import numpy as np
    import concourse.bacc as bacc
    from concourse.bass_utils import run_bass_kernel_spmd as run

    g = {k: np.asarray(v) for k, v in inputs.items()}
    perm = np.concatenate([np.arange(MUL)] + [MUL + 3 * np.arange(MUL) + c for c in range(3)])
    back = np.argsort(perm)
    zero = np.zeros((MUL, MUL), np.float32)

    def rows128(a):
        return a.reshape(2, P, -1).transpose(1, 0, 2)

    def diag(a, b):
        return np.block([[a, zero], [zero, b]])

    pad_e = ET * P - EDGES
    src = np.pad(g["src"], (0, pad_e), mode="edge")
    dst = np.pad(g["dst"], (0, pad_e), mode="edge")
    ea = np.pad(g["edge_attr_4"], ((0, pad_e), (0, 0)))
    es = np.pad(g["edge_attr_8"], ((0, pad_e + CHUNK), (0, 0))).T
    sc0, sc1, l0, l1 = (g["L0_gnn_" + n] for n in ("sc_w0", "sc_w1", "lin1_w0", "lin1_w1"))
    w00, w01, w10, w11 = (g["L0_gnn_lin2_w" + n] for n in ("00", "01", "10", "11"))
    fc2 = g["L0_gnn_fc_w2"].reshape(MUL, 4, MUL)[:, [0, 2, 3, 1]].reshape(MUL, 4 * MUL)
    zc = np.concatenate([w11, w10])
    mem = g["L0_mix_mem_kv"].reshape(2, HD, NUM_MEM)
    consts = np.zeros((P, C_END), np.float32)
    consts[:, C_IDENT:C_TRI] = np.eye(P)
    consts[:, C_TRI:C_BLOCK] = np.triu(np.ones((P, P)))
    consts[:, C_BLOCK:C_ONES] = np.kron(np.eye(HEADS), np.ones((DH, DH)))
    consts[:, C_ONES:C_IOTA] = 1.0
    consts[:, C_IOTA:C_VALID] = np.arange(STRAY_WIN)
    consts[:LAST, C_VALID] = 1.0
    consts[:, C_RESET:C_IOTA8] = (np.arange(NT * E) % NT != 0)
    consts[:, C_IOTA8:C_TRASH] = np.arange(E)
    consts[:, C_TRASH:C_HIGH] = TRASH + np.arange(NT)[None, :] * P + np.arange(P)[:, None]
    consts[0:16, C_HIGH] = 1.0
    consts[16:32, C_LOW] = 1.0
    arrays = dict(
        x=np.pad(g["x"][:, perm], ((0, NPAD - N), (0, 0)), mode="edge"),
        node_a=np.pad(g["node_vec1"][:, 0], (0, NPAD - N), mode="edge").reshape(NT, P).T,
        src=src.reshape(EG, GT, P).transpose(2, 0, 1),
        dst=dst.reshape(ET, P).T,
        dst_first=np.concatenate([np.zeros(1, dst.dtype), dst[::GT * P]])[None],
        ea=ea.reshape(ET, P, 4).transpose(1, 0, 2),
        es=es.reshape(P, -1),
        w_y=rows128(np.concatenate([diag(l0, l1), diag(l1, l1)])),
        w_s=rows128(np.concatenate([diag(sc0, sc1), diag(sc1, sc1)])),
        w_z=np.stack([zc, zc, zc, np.concatenate([w00, w01])], 1),
        fc1=np.tile(g["L0_gnn_fc_w1"], (4, 2)),
        fc2=np.tile(fc2, (2, 1)),
        w_qkv=rows128(g["L0_mix_w_qkv"][perm]),
        g_pre=g["L0_mix_g_pre"][perm].reshape(2, P).T,
        mem_kt=mem[0],
        mem_k=mem[0].T,
        mem_v=mem[1].T,
        w_out=g["L0_mix_w_out"][:, perm],
        b_out=g["L0_mix_b_out"][perm][None],
        g_out=g["L0_mix_g_out"][perm][None],
        gate_w=rows128(g["L0_ffn_gate_w"][perm]),
        gate_b=g["L0_ffn_gate_b"][None],
        w1=g["L0_ffn_w1"][:, perm].reshape(E, 2, P, F).transpose(0, 2, 1, 3),
        b1=g["L0_ffn_b1"].reshape(E, FB, P).transpose(0, 2, 1),
        w2=g["L0_ffn_w2"][:, :, perm].reshape(E, FB, P, D).transpose(0, 2, 1, 3),
        b2=g["L0_ffn_b2"][:, perm],
        consts=consts,
    )
    nc = bacc.Bacc("TRN2", target_bir_lowering=False, num_devices=1)
    data, args = {}, {}
    for name, a in arrays.items():
        data[f"in_{name}"] = np.ascontiguousarray(a)
        args[name] = nc.dram_tensor(f"in_{name}", a.shape, mybir.dt.from_np(a.dtype), kind="ExternalInput").ap()
    args["out"] = nc.dram_tensor("out_0", (NPAD, D), F32, kind="ExternalOutput").ap()
    program(nc, **args)
    result = run(nc, [data], core_ids=[0])
    return result.results[0]["out_0"][:N][:, back]
```

```python
from contextlib import ExitStack
import math

import concourse.bass as bass
from concourse import mybir

F32 = mybir.dt.float32
I32 = mybir.dt.int32
F32R = mybir.dt.float32r
ALU = mybir.AluOpType
ACT = mybir.ActivationFunctionType
AX = mybir.AxisListType

P = 128
N = 3125
D = 256
MUL = 64
NT = 25
TB = 5
NODE_TURNS = NT // TB
NPAD = NT * P
LAST = N - (NT - 1) * P
EDGES = 53125
GT = 2
GROUPS_PER_TURN = 4
TPT = GT * GROUPS_PER_TURN
EDGE_TURNS = -(-EDGES // (P * TPT))
ET = EDGE_TURNS * TPT
EG = ET // GT
CHUNK = 4 * P
WIN = 24
STRAY_WIN = 120
STRAY_TURNS = -(-N // STRAY_WIN)
NZ = STRAY_TURNS * STRAY_WIN
assert NZ >= N + WIN and NZ >= NPAD
HD = 128
HEADS, DH = 4, 32
NUM_MEM = 4
E = 8
CAP = -(-5 * N // (4 * E))
SLOTS = CAP
F = 1024
FB = F // P
LAST_C = CAP - 3 * P
TRASH = E * SLOTS

W_SCALE = 1.679 / 8.0
INV_SQRT3 = 1.0 / math.sqrt(3.0)
Y_SCALE = 1.0 / 8.0
S_SCALE = math.sin(math.pi / 8.0) / 8.0
Z_SCALE = math.cos(math.pi / 8.0) / math.sqrt(128.0) / math.sqrt(20.0)
SM_SCALE = DH ** -0.5
ES_SCALE = 1.0 / math.sqrt(8.0)
EPS = 1e-5
FLT_MAX = 3.4028234663852886e38

C_IDENT, C_TRI, C_BLOCK, C_ONES, C_IOTA, C_VALID, C_RESET, C_IOTA8, C_TRASH, C_HIGH, C_LOW, C_END = (
    0, 128, 256, 384, 512, 632, 633, 833, 841, 866, 867, 868)


class Chain:

    def __init__(self, eng, sem):
        self.eng, self.sem, self.n, self.offset = eng, sem, 0, 0

    def link(self, ins):
        self.n += 1
        ins.then_inc(self.sem, 1)
        self.eng.wait_ge(self.sem, self.offset + self.n)

    def enter(self, i, per_turn):
        self.start, self.per_turn, self.offset = self.n, per_turn, i * per_turn

    def leave(self, turns):
        assert self.n - self.start == self.per_turn, (self.n - self.start, self.per_turn)
        self.n, self.offset = self.start + turns * self.per_turn, 0


def bc(ap, axis, n):
    v = ap.unsqueeze(axis)
    shape = list(v.shape)
    shape[axis] = n
    return v.to_broadcast(shape)


def program(nc, x, node_a, src, dst, dst_first, ea, es, w_y, w_s, w_z, fc1, fc2, w_qkv, g_pre,
            mem_kt, mem_k, mem_v, w_out, b_out, g_out, gate_w, gate_b, w1, b1, w2, b2, consts, out):
    y_dram = nc.dram_tensor("y_dram", (NPAD, D), F32)
    buf_dram = nc.dram_tensor("buf_dram", (TRASH + NPAD, D), F32)
    es_len = es.shape[1] * P // 8
    es_hl = nc.dram_tensor("es_hl", (2 * 8, es_len), F32)
    ybuf_dram = nc.dram_tensor("ybuf_dram", (E * SLOTS, D), F32)

    with ExitStack() as ctx:
        def sb(name, shape, dt=F32):
            return ctx.enter_context(nc.sbuf_tensor(name, shape, dt))

        def sem(name):
            return ctx.enter_context(nc.semaphore(name))

        ps = ctx.enter_context(nc.psum_tensor("ps", [P, 8, 512], F32))

        cst = sb("cst", [P, C_END])
        ident, tri, block_mask = cst[:, C_IDENT:C_TRI], cst[:, C_TRI:C_BLOCK], cst[:, C_BLOCK:C_ONES]
        ones, iota = cst[:, C_ONES:C_IOTA], cst[:, C_IOTA:C_VALID]
        valid, reset, iota8 = cst[:, C_VALID:C_RESET], cst[:, C_RESET:C_IOTA8], cst[:, C_IOTA8:C_TRASH]
        trash_row = cst[:, C_TRASH:C_HIGH]
        resid = sb("resid", [P, NT, D])
        zT = sb("zT", [P, 5, NZ])
        wy = sb("wy", [P, 2, P])
        ws = sb("ws", [P, 2, P])
        wz = sb("wz", [P, 4, MUL])
        fc1_sb = sb("fc1_sb", [4 * 8, P])
        fc1_hl = sb("fc1_hl", [4 * 8, 2, P])
        fc1_r = sb("fc1_r", [P, P], F32R)
        fc2_sb = sb("fc2_sb", [P, 256])
        fc2_r = sb("fc2_r", [P, 2, 256], F32R)
        es_r = sb("es_r", [P, 2, CHUNK], F32R)
        h_r = sb("h_r", [P, 2, CHUNK], F32R)
        wqkv = sb("wqkv", [P, 2, 3 * HD])
        gpre = sb("gpre", [P, 2])
        node_a_sb = sb("node_a_sb", [P, NT])
        memkt = sb("memkt", [P, NUM_MEM])
        memk = sb("memk", [NUM_MEM, HD])
        memv = sb("memv", [NUM_MEM, HD])
        wout = sb("wout", [P, D])
        bout_b = sb("bout_b", [P, D])
        gout_b = sb("gout_b", [P, D])
        gatew = sb("gatew", [P, 2, E])
        gateb_b = sb("gateb_b", [P, E])
        mix_w = sb("mix_w", [P, D])
        small = sb("small", [P, 16])
        ea_sb = sb("ea_sb", [P, ET, 4])
        dst_i = sb("dst_i", [P, ET], I32)
        first_i = sb("first_i", [1, 1 + EG], I32)
        region = sb("region", [P, 14200])
        kv = region[:, 0:NT * 256].rearrange("p (t c) -> p t c", t=NT)
        r0 = NT * 256
        xn = region[:, r0:r0 + TB * D].rearrange("p (t c) -> p t c", t=TB)
        xm = region[:, r0 + 1280:r0 + 2560].rearrange("p (t c) -> p t c", t=TB)
        xT = region[:, r0 + 2560:r0 + 3840].rearrange("p (t k c) -> p t k c", t=TB, k=2)
        ysb = region[:, r0 + 3840:r0 + 5120].rearrange("p (t c) -> p t c", t=TB)
        qs = region[:, r0 + 5120:r0 + 5760].rearrange("p (t c) -> p t c", t=TB)
        qn = region[:, r0 + 5760:r0 + 6400].rearrange("p (t c) -> p t c", t=TB)
        st = region[:, r0 + 6400:r0 + 6430].rearrange("p (t c) -> p t c", t=TB)
        sq_junk = region[:, r0 + 6440:r0 + 7720].rearrange("p (t c) -> p t c", t=TB)
        mv = sb("mv", [P, TB, 2])
        col = sb("col", [P, 8, TB])
        qcol = sb("qcol", [P, 2, TB * HEADS])
        kmx = sb("kmx", [P, 4])
        relf = region[:, 0:ET]
        first_f = region[0:1, ET:ET + EG]
        inw = region[:, 700:700 + ET]
        junk = region[:, 1200:1200 + ET]
        xg = region[:, 1700:1700 + 2048].rearrange("p (g j c) -> p g j c", g=4, j=GT)
        prod = region[:, 3800:3800 + 2048].rearrange("p (g j c) -> p g j c", g=2, j=GT)
        h_f = region[:, 5900:5900 + 1024].rearrange("p (s c) -> p s c", s=2)
        sel = region[:, 8100:8100 + 8 * 4 * WIN].rearrange("p (s t c w) -> p s t c w", s=2, t=4, c=4)
        hot = region[:, 8900:8900 + 8 * WIN].rearrange("p (s t w) -> p s t w", s=2, t=4)
        stage = region[:, 9200:9200 + 2 * 4 * WIN].rearrange("p (s b w) -> p s b w", s=2, b=4)
        stray_dst = region[:, 9400:9400 + ET]
        stray_cur = region[:, 9820:9822]
        stray_hot = region[:, 9830:9830 + STRAY_WIN]
        stray_sel = region[:, 9950:9950 + 4 * STRAY_WIN].rearrange("p (c w) -> p c w", c=4)
        idx_sb = sb("idx_sb", [P, GROUPS_PER_TURN, GT], I32)
        flag_i = sb("flag_i", [1, 2], I32)
        flag_f = sb("flag_f", [P, 2])
        xl = region[:, 0:NT * 256].rearrange("p (t c) -> p t c", t=NT)
        om = region[:, 9600:10880].rearrange("p (t c) -> p t c", t=TB)
        xls = region[:, 10880:12160].rearrange("p (t c) -> p t c", t=TB)
        gnn = region[:, 12160:13440].rearrange("p (t c) -> p t c", t=TB)
        xlT = region[:, 13440:13952].rearrange("p (s k c) -> p s k c", s=2, k=2)
        rt = region[:, 9600:9600 + 12 * NT * E].rearrange("p (a c) -> p a c", a=12)
        logits_all = sb("logits_all", [P, (NODE_TURNS + 1) * TB * E])
        logits = logits_all[:, TB * E:]
        rcol = sb("rcol", [P, 12, NT])
        cstat = sb("cstat", [P, TB, 6])
        scat_i = sb("scat_i", [P, NT], I32)
        gath_i = sb("gath_i", [P, NT], I32)
        w1_sb = sb("w1_sb", [P, 2, 2, F])
        w2_sb = zT[:].rearrange("p b z -> p (b z)")[:, 0:2 * FB * D].rearrange("p (s f d) -> p s f d", s=2, f=FB)
        zflat = zT[:].rearrange("p b z -> p (b z)")
        ew = es.shape[1]
        es_hi, es_lo, es_in_f = (zflat[:, n * ew:(n + 1) * ew] for n in range(3))
        o = 2 * FB * D
        hid = zflat[:, o:o + FB * CAP].rearrange("p (f c) -> p f c", f=FB)
        o += FB * CAP + 8
        xb = zflat[:, o:o + 2048].rearrange("p (s c d) -> p s c d", s=2, c=4)
        o += 2048
        xbT = zflat[:, o:o + 1024].rearrange("p (k c) -> p k c", k=2)
        o += 1024
        yst = zflat[:, o:o + 2048].rearrange("p (s c d) -> p s c d", s=2, c=4)
        o += 2048
        assert o <= 5 * NZ
        b1_sb = sb("b1_sb", [P, 2, FB])
        b2_sb = sb("b2_sb", [P, 2, D])

        S = {}
        for name in """consts_in weights_in es_raw_in es_split es_stored zeroed lo_ready x_in edges_in scaled dve_chain act_chain turn_dve turn_pe turn_act turn_pool turn_sp
            var_ready std_ready xn_ready norm_ready xm_ready xT_ps xT_sb ys_ps y_sb s_sb qkv_ps qkv_sb kt_ps kmax_sb q_sub q_exp
            qn_ready qT_ps qT_sb y_stored ysb_free kdiag kmax_b k_sub k_exp ctx_ps ctx_sb mixw_ps mixw_sb
            first_row first_ps strays_sum flag_ps flag_ready h_ready silu_done w_ready prod_ready sel_done z_evac added
            stray_gathered stray_step_dve stray_step_act stray_step_pe
            sums_ready gnn_ps om_ready om_var om_norm gnn_sb x_summed x2_var x2_std xl_scale xl_ready xl_stored xlT_ps xlT_sb gate_ps logit_sb
            l_sub l_exp hot_ready pre_ps slots_ready scattered zero_in
            xbT_ps xbT_sb hid_ps hid_sb yexp_ps yst_ready out_ready out_stored""".split():
            S[name] = sem(name)
        es_in = [sem(f"es_in{s}") for s in range(2)]
        idx_in = [sem(f"idx_in{k}") for k in range(4)]
        rows_in = [sem(f"rows_in{k}") for k in range(4)]
        we_in = [sem(f"we_in{s}") for s in range(2)]
        xb_in = [sem(f"xb_in{s}") for s in range(2)]
        y_out = [sem(f"y_out{s}") for s in range(2)]
        back_in = [sem(f"back_in{s}") for s in range(NODE_TURNS)]

        x_v = x.rearrange("(t p) c -> p t c", p=P)
        y_v = y_dram[:].rearrange("(t p) c -> p t c", p=P)
        out_v = out.rearrange("(t p) c -> p t c", p=P)
        N_WEIGHTS = 19

        block = ctx.enter_context(nc.Block())

        @block.sync
        def _(sp):
            def load_scalars(s, first, n):
                for half in range(2):
                    sp.dma_start(es_r[16 * half:16 * half + 16, s, 0:n].bitcast(F32), es_hl[:, bass.ds(first, n)]).then_inc(es_in[s], 16)

            def load_rows(s, e):
                sp.dma_start(xb[:, s, 0:3, :], buf_dram[bass.ds(e * SLOTS, 3 * P), :].rearrange("(c p) d -> p c d", p=P)).then_inc(xb_in[s], 16)
                sp.dma_start(xb[0:LAST_C, s, 3, :], buf_dram[bass.ds(e * SLOTS + 3 * P, LAST_C), :]).then_inc(xb_in[s], 16)

            sp.dma_start(cst[:], consts).then_inc(S["consts_in"], 16)
            sp.dma_start(node_a_sb[:], node_a).then_inc(S["consts_in"], 16)
            with sp.Fori(0, NODE_TURNS) as i:
                sp.dma_start(resid[:, bass.ds(i * TB, TB), :], x_v[:, bass.ds(i * TB, TB), :]).then_inc(S["x_in"], 16)
                sp.wait_ge(S["x_in"], i * 16 + 16)
                sp.sem_inc(S["turn_sp"], 1)
            sp.dma_start(ea_sb[:], ea).then_inc(S["edges_in"], 16)
            sp.dma_start(dst_i[:], dst).then_inc(S["edges_in"], 16)
            sp.dma_start(first_i[:], dst_first).then_inc(S["edges_in"], 16)
            sp.wait_ge(S["zeroed"], 1)
            sp.dma_start(buf_dram[0:TRASH, :].rearrange("r d -> (r d)").rearrange("(p f) -> p f", p=P),
                         zT[:].rearrange("p b z -> p (b z)")[:, 0:TRASH * D // P]).then_inc(S["zero_in"], 16)
            sp.wait_ge(S["ctx_sb"], 1)
            for s in range(2):
                load_scalars(s, s * CHUNK, CHUNK)
            for k in range(GROUPS_PER_TURN):
                sp.dma_start(idx_sb[:, k, :], src[:, k, :]).then_inc(idx_in[k], 16)
            with sp.Fori(1, EDGE_TURNS) as i:
                for s in range(2):
                    sp.wait_ge(S["h_ready"], i * 2 + (s - 1))
                    sp.sem_inc(S["turn_sp"], 1)
                    load_scalars(s, i * (2 * CHUNK) + s * CHUNK, CHUNK)
                    for k in range(2 * s, 2 * s + 2):
                        sp.wait_ge(rows_in[k], i * (16 * GT))
                        sp.sem_inc(S["turn_sp"], 1)
                        sp.dma_start(idx_sb[:, k, :], src[:, bass.ds(i * GROUPS_PER_TURN + k, 1), :]
                                     .rearrange("p a j -> p (a j)")).then_inc(idx_in[k], 16)
            sp.wait_ge(S["h_ready"], 2 * EDGE_TURNS - 1)
            load_scalars(0, 2 * EDGE_TURNS * CHUNK, CHUNK)
            sp.wait_ge(S["flag_ready"], 1)
            flag = sp.value_load(flag_i[0:1, 0:1], min_val=0, max_val=ET * P)
            sp.wait_ge(S["added"], EG + 3)
            with sp.If(flag > 0):
                with sp.Fori(0, ET) as t:
                    sp.wait_ge(S["stray_step_dve"], t * (STRAY_TURNS + 3) + 1)
                    sp.sem_inc(S["turn_sp"], 1)
                    load_scalars(1, t * P, P)
                    sp.wait_ge(es_in[1], t * 32 + 32 * (EDGE_TURNS + 1))
                    sp.sem_inc(S["turn_sp"], 1)
                    sp.dma_start(idx_sb[:, 0, 0:1], src.rearrange("p g j -> p (g j)")[:, bass.ds(t, 1)],
                                 allow_slow_non_contiguous=True).then_inc(idx_in[0], 16)
            with sp.Else():
                sp.sem_inc(S["turn_sp"], 1)
            for e in range(2):
                sp.dma_start(w1_sb[:, e], w1[e]).then_inc(we_in[e], 16)
                sp.dma_start(b1_sb[:, e], b1[e]).then_inc(we_in[e], 16)
                sp.dma_start(b2_sb[:, e], b2[e:e + 1, :].partition_broadcast(P)).then_inc(we_in[e], 16)
            sp.wait_ge(S["gnn_ps"], NT)
            for e in range(2):
                sp.dma_start(w2_sb[:, e], w2[e]).then_inc(we_in[e], 16)
            sp.wait_ge(S["scattered"], 16 * NT)
            for e in range(2):
                load_rows(e, e)
            with sp.Fori(0, E // 2 - 1) as i:
                for s in range(2):
                    e = i * 2 + (2 + s)
                    sp.wait_ge(S["xbT_ps"], i * 4 + 2 * s + 2)
                    sp.sem_inc(S["turn_sp"], 1)
                    load_rows(s, e)
                    sp.wait_ge(S["hid_sb"], i * (2 * FB) + (s + 1) * FB + 3)
                    sp.sem_inc(S["turn_sp"], 1)
                    sp.dma_start(w1_sb[:, s], w1[bass.ds(e, 1)].rearrange("a p k f -> p (a k) f")).then_inc(we_in[s], 16)
                    sp.dma_start(b1_sb[:, s], b1[bass.ds(e, 1)].rearrange("a p k -> p (a k)")).then_inc(we_in[s], 16)
                    sp.wait_ge(S["yst_ready"], i * 8 + 4 * s + 6)
                    sp.sem_inc(S["turn_sp"], 1)
                    sp.dma_start(w2_sb[:, s], w2[bass.ds(e, 1)].rearrange("a p k f -> p (a k) f")).then_inc(we_in[s], 16)
                    sp.dma_start(b2_sb[:, s], b2[bass.ds(e, 1), :].partition_broadcast(P)).then_inc(we_in[s], 16)
            for g in range(NODE_TURNS):
                sp.wait_ge(S["out_ready"], g + 1)
                sp.dma_start(out_v[:, g * TB:(g + 1) * TB, :], resid[:, g * TB:(g + 1) * TB, :]).then_inc(S["out_stored"], 16)
            sp.wait_ge(S["out_stored"], 16 * NODE_TURNS)

        @block.gpsimd
        def _(pool):
            pool.wait_ge(S["es_raw_in"], 16)
            nc.gpsimd.tensor_copy(es_hi.bitcast(F32R), es_in_f).then_inc(S["es_split"], 1)
            pool.wait_ge(S["es_split"], 1)
            nc.gpsimd.tensor_tensor(es_lo.bitcast(F32R), es_in_f, es_hi, ALU.subtract).then_inc(S["es_split"], 1)
            pool.wait_ge(S["es_split"], 2)
            for part, rows in ((es_hi, es_hl[0:8, :]), (es_lo, es_hl[8:16, :])):
                pool.dma_start(rows.rearrange("r e -> (r e)").rearrange("(p f) -> p f", p=P),
                               part).then_inc(S["es_stored"], 16)
            pool.wait_ge(S["es_stored"], 32)
            nc.gpsimd.memset(zT[:, 0:4], 0.0).then_inc(S["zeroed"], 1)
            pool.sem_inc(S["ysb_free"], 1)
            with pool.Fori(0, NODE_TURNS) as i:
                pool.wait_ge(S["y_sb"], i * TB + (TB + 2))
                pool.sem_inc(S["turn_pool"], 1)
                pool.dma_start(y_v[:, bass.ds(i * TB, TB), :], ysb).then_inc(S["y_stored"], 16)
                pool.wait_ge(S["y_stored"], i * 16 + 16)
                pool.sem_inc(S["ysb_free"], 1)
            pool.wait_ge(S["y_stored"], 16 * NODE_TURNS)
            pool.wait_ge(S["ctx_sb"], 1)

            def gather(k):
                for j in range(GT):
                    pool.indirect_dma_start(xg[:, k, j, :], None, y_dram[:], bass.IndirectOffsetOnAxis(
                        ap=idx_sb[:, k, j:j + 1], axis=0)).then_inc(rows_in[k], 16)

            for k in range(GROUPS_PER_TURN):
                pool.wait_ge(idx_in[k], 16)
                gather(k)
            with pool.Fori(1, EDGE_TURNS) as i:
                for k in range(GROUPS_PER_TURN):
                    pool.wait_ge(S["prod_ready"], i * 4 + (k - 3))
                    pool.sem_inc(S["turn_pool"], 1)
                    pool.wait_ge(idx_in[k], i * 16 + 16)
                    pool.sem_inc(S["turn_pool"], 1)
                    gather(k)
            pool.wait_ge(S["flag_ready"], 1)
            flag = pool.value_load(flag_i[0:1, 0:1], min_val=0, max_val=ET * P)
            pool.wait_ge(S["added"], EG + 3)
            with pool.If(flag > 0):
                with pool.Fori(0, ET) as t:
                    pool.wait_ge(idx_in[0], t * 16 + 16 * (EDGE_TURNS + 1))
                    pool.sem_inc(S["turn_pool"], 1)
                    pool.indirect_dma_start(xg[:, 0, 0, :], None, y_dram[:], bass.IndirectOffsetOnAxis(
                        ap=idx_sb[:, 0, 0:1], axis=0)).then_inc(S["stray_gathered"], 16)
                    pool.wait_ge(S["stray_gathered"], t * 16 + 16)
                    pool.sem_inc(S["turn_pool"], 1)
            with pool.Else():
                pool.sem_inc(S["turn_pool"], 1)
            pool.sem_inc(S["x_summed"], 1)
            with pool.Fori(0, NODE_TURNS) as i:
                pool.wait_ge(S["gnn_sb"], i * TB + 2 * TB)
                xt = resid[:, bass.ds(i * TB, TB), :]
                nc.gpsimd.tensor_tensor(xt, xt, gnn[:], ALU.add).then_inc(S["x_summed"], 1)
            pool.wait_ge(S["slots_ready"], 1)
            pool.wait_ge(S["zero_in"], 16)
            for t in range(NT):
                pool.indirect_dma_start(buf_dram[:], bass.IndirectOffsetOnAxis(ap=scat_i[:, t:t + 1], axis=0),
                                        xl[:, t, :], None).then_inc(S["scattered"], 16)
            pool.wait_ge(S["scattered"], 16 * NT)
            for s in range(2):
                pool.wait_ge(y_out[s], 16 * 4 * (E // 2))
            for t in range(NT):
                pool.indirect_dma_start(xl[:, t, :], None, ybuf_dram[:], bass.IndirectOffsetOnAxis(
                    ap=gath_i[:, t:t + 1], axis=0)).then_inc(back_in[t // TB], 16)

        @block.scalar
        def _(act):
            A = nc.scalar
            chain = Chain(act, S["act_chain"])
            act.dma_start(es_in_f, es).then_inc(S["es_raw_in"], 16)
            loads = [(wy[:], w_y), (ws[:], w_s), (wqkv[:], w_qkv), (gpre[:], g_pre), (wz[:], w_z), (fc1_sb[:], fc1),
                     (fc2_sb[:], fc2), (memkt[:], mem_kt), (memk[:], mem_k), (memv[:], mem_v), (wout[:], w_out),
                     (bout_b[:], b_out.partition_broadcast(P)), (gout_b[:], g_out.partition_broadcast(P)),
                     (gatew[:], gate_w), (gateb_b[:], gate_b.partition_broadcast(P))]
            for to, of in loads:
                act.dma_start(to, of).then_inc(S["weights_in"], 16)
            assert len(loads) == 15
            act.sem_inc(S["xT_sb"], 2)
            act.sem_inc(S["y_sb"], 2)
            act.sem_inc(S["qkv_sb"], 2)
            act.sem_inc(S["qT_sb"], 1)

            def x_transposed(i, j):
                act.wait_ge(S["xT_ps"], i * TB + (j + 1))
                act.wait_ge(S["kt_ps"], i + 1)
                A.copy(xT[:, j], ps[:, j % 2, 0:256].rearrange("p (k c) -> p k c", k=2)).then_inc(S["xT_sb"], 1)

            with act.Fori(0, NODE_TURNS) as i:
                act.wait_ge(S["var_ready"], i + 1)
                A.activation(col[:, 1, :], col[:, 0, :], ACT.Sqrt).then_inc(S["std_ready"], 1)
                act.wait_ge(S["xn_ready"], i + 1)
                for j in range(TB):
                    last = A.activation(sq_junk[:, j, :], xn[:, j, :], ACT.Square, accum_out=col[:, 3, j:j + 1])
                last.then_inc(S["act_chain"], 1)
                act.wait_ge(S["act_chain"], i + 1)
                A.activation(col[:, 4, :], col[:, 3, :], ACT.Sqrt).then_inc(S["norm_ready"], 1)
                x_transposed(i, 0)
                x_transposed(i, 1)
                for j in range(TB):
                    act.wait_ge(S["ys_ps"], i * TB + (j + 1))
                    if j == 0:
                        act.wait_ge(S["ysb_free"], i + 1)
                    A.activation(ysb[:, j, :], ps[:, 2 + j % 2, 0:256], ACT.Copy, scale=col[:, 7, j:j + 1]).then_inc(S["y_sb"], 1)
                    act.wait_ge(S["qkv_ps"], i * TB + (j + 1))
                    if j == 0:
                        act.wait_ge(S["qn_ready"], i + 1)
                    A.copy(qs[:, j, :], ps[:, 4 + j % 2, 0:HD])
                    A.copy(kv[:, bass.ds(i * TB + j, 1), :].rearrange("p a c -> p (a c)"),
                           ps[:, 4 + j % 2, HD:3 * HD]).then_inc(S["qkv_sb"], 1)
                    if j + 2 < TB:
                        x_transposed(i, j + 2)
                act.wait_ge(S["q_sub"], i + 1)
                A.activation(qs[:], qs[:], ACT.Exp).then_inc(S["q_exp"], 1)
                act.wait_ge(S["qT_ps"], i + 1)
                A.copy(zT[:, 4, bass.ds(i * (TB * P), TB * P)],
                       ps[:, 0:2, :].rearrange("p b c -> p (b c)")[:, 0:TB * P]).then_inc(S["qT_sb"], 1)
            chain.n = NODE_TURNS
            act.wait_ge(S["k_sub"], 1)
            A.activation(kv[:, :, 0:HD], kv[:, :, 0:HD], ACT.Exp)
            A.activation(memk[:], memk[:], ACT.Exp).then_inc(S["k_exp"], 1)

            act.sem_inc(S["z_evac"], 2)

            def evacuate(i, k):
                g1 = i * 4 + (k + 1)
                b = k % 2
                act.wait_ge(S["sel_done"], g1 + 2)
                act.wait_ge(S["added"], g1)
                bank = ps[:, 4 + b, 0:8 * WIN].rearrange("p (q w) -> p q w", q=8)
                A.copy(stage[0:64, b], bank[0:64, 0:4])
                A.copy(stage[64:128, b], bank[64:128, 4:8]).then_inc(S["z_evac"], 1)

            act.wait_ge(S["ctx_sb"], 1)
            def silu(s, n=CHUNK):
                A.activation(h_r[:, s, 0:n], ps[:, s, 0:n], ACT.Silu, scale=ES_SCALE)
                return A.activation(h_f[64:128, s, 0:n], ps[64:128, s, 0:n], ACT.Silu, scale=ES_SCALE)

            act.wait_ge(S["h_ready"], 1)
            silu(0).then_inc(S["silu_done"], 1)
            with act.Fori(0, EDGE_TURNS) as i:
                act.wait_ge(S["h_ready"], i * 2 + 2)
                act.wait_ge(S["w_ready"], i * 4 + 1)
                silu(1).then_inc(S["silu_done"], 1)
                evacuate(i, 0)
                act.wait_ge(S["h_ready"], i * 2 + 3)
                act.wait_ge(S["w_ready"], i * 4 + 2)
                silu(0).then_inc(S["silu_done"], 1)
                evacuate(i, 1)
                evacuate(i, 2)
                evacuate(i, 3)
            act.wait_ge(S["flag_ready"], 1)
            flag = act.value_load(flag_i[0:1, 0:1], min_val=0, max_val=ET * P)
            act.wait_ge(S["added"], EG + 3)
            with act.If(flag > 0):
                with act.Fori(0, ET) as t:
                    act.wait_ge(S["stray_step_pe"], t * (STRAY_TURNS + 2) + 1)
                    silu(0, P).then_inc(S["stray_step_act"], 1)
            with act.Else():
                act.sem_inc(S["turn_act"], 1)
            act.sem_inc(S["xlT_sb"], 2)
            act.sem_inc(S["gnn_sb"], TB)
            act.sem_inc(S["xl_stored"], TB)
            def normalized(out, i, j, done):
                A.activation(out.rearrange("p a c -> p (a c)"), resid[:, bass.ds(i * TB + j, 1), :].rearrange("p a c -> p (a c)"),
                             ACT.Identity, scale=col[:, 6, j:j + 1], bias=col[:, 7, j:j + 1]).then_inc(done, 1)

            def lin2_scaled(i):
                for j in range(TB):
                    act.wait_ge(S["om_ready"], i * TB + (TB + j + 1))
                    if j == 0:
                        act.wait_ge(S["x_summed"], i + 1)
                    A.activation(gnn[:, j, :], ps[:, j, 0:256], ACT.Identity, scale=node_a_sb[:, bass.ds(i * TB + j, 1)]).then_inc(S["gnn_sb"], 1)

            def norm_root(i):
                act.wait_ge(S["om_var"], i + 1)
                A.activation(col[:, 1, :], col[:, 0, :], ACT.Sqrt, scale=float(D)).then_inc(S["om_norm"], 1)

            def combine_act(i, last):
                act.wait_ge(S["x2_var"], i + 1)
                A.activation(col[:, 3, :], col[:, 2, :], ACT.Sqrt).then_inc(S["x2_std"], 1)
                act.wait_ge(S["xl_scale"], i + 1)
                for j in range(TB):
                    normalized(xls[:, j:j + 1, :], i, j, S["xl_ready"])
                if not last:
                    lin2_scaled(i + 1)
                    norm_root(i + 1)
                for j in range(TB):
                    act.wait_ge(S["xlT_ps"], i * TB + (j + 1))
                    act.wait_ge(S["gate_ps"], i * TB + (1 + max(0, j - 1)))
                    A.copy(xlT[:, j % 2], ps[:, 5 + j % 2, 0:256].rearrange("p (k c) -> p k c", k=2)).then_inc(S["xlT_sb"], 1)
                    normalized(xl[:, bass.ds(i * TB + j, 1), :], i, j, S["xl_stored"])

            lin2_scaled(0)
            norm_root(0)
            with act.Fori(0, NODE_TURNS - 1) as i:
                combine_act(i, False)
            combine_act(NODE_TURNS - 1, True)
            act.wait_ge(S["l_sub"], 1)
            A.activation(rt[:, 1, :], rt[:, 0, :], ACT.Exp).then_inc(S["l_exp"], 1)
            act.sem_inc(S["hid_sb"], 3)
            with act.Fori(0, E // 2) as i:
                for s in range(2):
                    act.wait_ge(we_in[s], i * 64 + 64)
                    act.wait_ge(S["yexp_ps"], i * 8 + (4 * s + 1))
                    for f in range(FB):
                        act.wait_ge(S["hid_ps"], i * (2 * FB) + s * FB + f + 1)
                        A.activation(hid[:, f, :], ps[:, 2 + (s * FB + f) % 3, 0:CAP], ACT.Relu, bias=b1_sb[:, s, f:f + 1]).then_inc(S["hid_sb"], 1)
                    e = i * 2 + s
                    for c in range(4):
                        act.wait_ge(S["yst_ready"], i * 8 + (4 * s + c + 3))
                        act.sem_inc(S["turn_act"], 1)
                        rows = P if c < 3 else LAST_C
                        act.dma_start(ybuf_dram[bass.ds(e * SLOTS + c * P, rows), :], yst[0:rows, s, c, :]).then_inc(y_out[s], 16)

        @block.vector
        def _(dve):
            V = nc.vector
            chain = Chain(dve, S["dve_chain"])
            link = chain.link
            V.memset(es_r[:].bitcast(F32), 0.0)
            link(V.memset(fc1_r[:].bitcast(F32), 0.0))
            V.memset(kmx[:], -FLT_MAX)
            dve.wait_ge(S["weights_in"], 16 * 15)
            dve.wait_ge(S["consts_in"], 32)
            V.tensor_scalar(wy[:], wy[:], Y_SCALE, None, ALU.mult)
            V.tensor_scalar(ws[:], ws[:], S_SCALE, None, ALU.mult)
            V.tensor_scalar(wz[:], wz[:], Z_SCALE, None, ALU.mult)
            V.tensor_scalar(gout_b[:], gout_b[:], math.sqrt(D), None, ALU.mult)
            V.tensor_scalar(fc2_sb[:, 0:192], fc2_sb[:, 0:192], W_SCALE, None, ALU.mult)
            link(V.tensor_scalar(fc2_sb[:, 192:256], fc2_sb[:, 192:256], W_SCALE * INV_SQRT3, None, ALU.mult))
            V.tensor_copy(fc2_r[:, 0, :], fc2_sb[:])
            link(V.tensor_copy(fc1_hl[:, 0, :].bitcast(F32R), fc1_sb[:]))
            V.tensor_tensor(fc2_r[:, 1, :], fc2_sb[:], fc2_r[:, 0, :].bitcast(F32), ALU.subtract)
            link(V.tensor_tensor(fc1_hl[:, 1, :].bitcast(F32R), fc1_sb[:], fc1_hl[:, 0, :], ALU.subtract))
            link(V.tensor_scalar(fc1_hl[:, 1, :], fc1_hl[:, 1, :], cst[0:32, C_LOW:C_END], None, ALU.mult))
            V.scalar_tensor_tensor(fc1_r[0:32, :], fc1_hl[:, 0, :], cst[0:32, C_HIGH:C_LOW], fc1_hl[:, 1, :], ALU.mult, ALU.add)
            for k in range(2):
                last = V.tensor_scalar(wqkv[:, k, :], wqkv[:, k, :], gpre[:, k:k + 1], math.sqrt(D), ALU.mult, ALU.mult)
            last.then_inc(S["scaled"], 1)
            dve.sem_inc(S["s_sb"], 2)
            dve.sem_inc(S["kmax_sb"], 1)
            dve.sem_inc(S["qn_ready"], 1)

            with dve.Fori(0, NODE_TURNS) as i:
                chain.enter(i, 10)
                xc = resid[:, bass.ds(i * TB, TB), :]
                dve.wait_ge(S["x_in"], i * 16 + 16)
                dve.sem_inc(S["turn_dve"], 1)
                for j in range(TB):
                    last = V.bn_stats(st[:, j, :], resid[:, bass.ds(i * TB + j, 1), :].rearrange("p a c -> p (a c)"))
                link(last)
                dve.sem_inc(S["turn_dve"], 1)
                for j in range(TB):
                    last = V.bn_aggr(mv[:, j, :], st[:, j, :])
                link(last)
                V.tensor_scalar(col[:, 0, :], mv[:, :, 1], EPS, None, ALU.add).then_inc(S["var_ready"], 1)
                dve.wait_ge(S["std_ready"], i + 1)
                link(V.reciprocal(col[:, 2, :], col[:, 1, :]))
                for j in range(TB):
                    last = V.tensor_scalar(xn[:, j, :], resid[:, bass.ds(i * TB + j, 1), :].rearrange("p a c -> p (a c)"),
                                           mv[:, j, 0:1], col[:, 2, j:j + 1], ALU.subtract, ALU.mult)
                last.then_inc(S["xn_ready"], 1)
                dve.wait_ge(S["xn_ready"], i + 1)
                link(V.tensor_tensor(xc, xc, xn[:], ALU.add))
                dve.wait_ge(S["norm_ready"], i + 1)
                link(V.tensor_scalar(col[:, 5, :], col[:, 4, :], 1e-12, None, ALU.max))
                link(V.reciprocal(col[:, 6, :], col[:, 5, :]))
                V.tensor_tensor(col[:, 7, :], col[:, 5, :], node_a_sb[:, bass.ds(i * TB, TB)], ALU.mult)
                for j in range(TB):
                    V.tensor_scalar(xm[:, j, :], xn[:, j, :], col[:, 6, j:j + 1], None, ALU.mult).then_inc(S["xm_ready"], 1)
                dve.wait_ge(S["xm_ready"], i * TB + TB)
                for j in range(TB):
                    dve.wait_ge(S["y_sb"], i * TB + (j + 3))
                    xt = resid[:, bass.ds(i * TB + j, 1), :].rearrange("p a c -> p (a c)")
                    V.scalar_tensor_tensor(xt, ps[:, 2 + j % 2, 256:512], col[:, 7, j:j + 1], xt, ALU.mult, ALU.add).then_inc(S["s_sb"], 1)
                dve.wait_ge(S["qkv_sb"], i * TB + (TB + 2))
                q4 = qs[:].rearrange("p t (h d) -> p (t h) d", d=DH)
                n4 = qn[:].rearrange("p t (h d) -> p (t h) d", d=DH)
                link(V.tensor_reduce(qcol[:, 0, :], q4, AX.X, ALU.max))
                V.tensor_tensor(q4, q4, bc(qcol[:, 0, :], 2, DH), ALU.subtract).then_inc(S["q_sub"], 1)
                dve.wait_ge(S["q_exp"], i + 1)
                link(V.tensor_reduce(qcol[:, 0, :], q4, AX.X, ALU.add))
                link(V.reciprocal(qcol[:, 1, :], qcol[:, 0, :]))
                dve.wait_ge(S["qT_sb"], i + 1)
                V.tensor_tensor(n4, q4, bc(qcol[:, 1, :], 2, DH), ALU.mult).then_inc(S["qn_ready"], 1)
                dve.wait_ge(S["kt_ps"], i + 2)
                link(V.tensor_reduce(kmx[:, 1:2], ps[:, 6:8, :].rearrange("p b c -> p (b c)")[:, 0:TB * P], AX.X, ALU.max))
                V.tensor_tensor(kmx[:, 0:1], kmx[:, 0:1], kmx[:, 1:2], ALU.max).then_inc(S["kmax_sb"], 1)
                dve.wait_ge(S["kmax_sb"], i + 2)
            chain.leave(NODE_TURNS)

            link(V.tensor_reduce(kmx[:, 1:2], memkt[:], AX.X, ALU.max))
            link(V.tensor_tensor(kmx[:, 0:1], kmx[:, 0:1], kmx[:, 1:2], ALU.max))
            V.tensor_scalar(xn[:, 0, 0:P], ident, kmx[:, 0:1], None, ALU.mult).then_inc(S["kdiag"], 1)
            dve.wait_ge(S["kmax_b"], 1)
            dve.wait_ge(S["qkv_sb"], NT + 2)
            V.tensor_tensor(kv[:, :, 0:HD], kv[:, :, 0:HD], bc(ps[:, 0, 0:HD], 1, NT), ALU.subtract)
            V.tensor_tensor(memk[:], memk[:], ps[0:NUM_MEM, 0, 0:HD], ALU.subtract).then_inc(S["k_sub"], 1)
            dve.wait_ge(S["k_exp"], 1)
            V.tensor_scalar(kv[:, NT - 1, 0:HD], kv[:, NT - 1, 0:HD], valid, None, ALU.mult).then_inc(S["kdiag"], 1)
            dve.wait_ge(S["ctx_ps"], 1)
            link(V.reciprocal(small[:, 0:1], ps[:, 2, 0:1]))
            V.tensor_tensor(xn[:, 1, 0:P], ps[:, 1, 0:HD], block_mask, ALU.mult).then_inc(S["ctx_sb"], 1)
            dve.wait_ge(S["mixw_ps"], 1)
            V.tensor_scalar(mix_w[:], ps[:, 3, 0:D], small[:, 0:1], SM_SCALE, ALU.mult, ALU.mult).then_inc(S["mixw_sb"], 1)
            dve.wait_ge(S["mixw_sb"], 1)

            dve.wait_ge(S["edges_in"], 48)
            V.tensor_copy(first_f, first_i[0:1, 1:1 + EG]).then_inc(S["first_row"], 1)
            link(V.tensor_copy(relf, dst_i[:]))
            dve.wait_ge(S["first_ps"], 1)
            rel3 = relf.rearrange("p (g j) -> p g j", j=GT)
            dst3 = stray_dst.rearrange("p (g j) -> p g j", j=GT)
            V.tensor_copy(stray_dst, relf)
            link(V.tensor_tensor(rel3, rel3, bc(ps[:, 7, 0:EG], 2, GT), ALU.subtract))
            link(V.tensor_scalar(inw, relf, 0.0, None, ALU.is_ge))
            link(V.scalar_tensor_tensor(inw, relf, float(WIN), inw, ALU.is_lt, ALU.mult))
            dve.wait_ge(S["zero_in"], 16)
            link(V.scalar_tensor_tensor(junk, inw, -8192.0, stray_dst, ALU.mult, ALU.add))
            V.tensor_copy(stray_dst, junk)
            V.tensor_reduce(flag_f[:, 0:1], inw, AX.X, ALU.add).then_inc(S["strays_sum"], 1)
            V.memset(stage[:], 0.0)
            dve.wait_ge(S["flag_ps"], 1)
            V.tensor_scalar(flag_i[0:1, 0:1], ps[0:1, 6, 0:1], -1.0, float(ET * P), ALU.mult, ALU.add).then_inc(S["flag_ready"], 1)
            dve.wait_ge(S["flag_ready"], 1)
            dve.sem_inc(S["added"], 1)

            def low_part(s, n=CHUNK):
                return V.tensor_tensor(h_r[64:128, s, 0:n], h_f[64:128, s, 0:n], h_r[64:128, s, 0:n].bitcast(F32), ALU.subtract)

            def products(i, k):
                g1 = i * 4 + (k + 1)
                b = k % 2
                dve.wait_ge(rows_in[k], i * (16 * GT) + 16 * GT)
                dve.wait_ge(S["w_ready"], g1)
                dve.wait_ge(S["sel_done"], g1)
                w = ps[:, 2 + b, :].rearrange("p (j c) -> p j c", j=GT)
                V.tensor_tensor(prod[:, b, :, 0:128].rearrange("p j (a u) -> p j a u", a=2),
                                w[:, :, 0:128].rearrange("p j (a u) -> p j a u", a=2),
                                bc(xg[:, k, :, 0:64], 2, 2), ALU.mult)
                for j in range(GT):
                    last = V.tensor_tensor(prod[:, b, j, 128:512].rearrange("p (c a u) -> p c a u", c=3, a=2),
                                           bc(w[:, j, 128:256].rearrange("p (a u) -> p a u", a=2), 1, 3),
                                           bc(xg[:, k, j, 64:256].rearrange("p (c u) -> p c u", c=3), 2, 2), ALU.mult)
                last.then_inc(S["prod_ready"], 1)

            def add(i, k, first):
                g = i * 4 + (k + 1)
                b = k % 2
                base = dve.value_load(first_i[0:1, bass.ds(g, 1)] if first is None else first, min_val=0, max_val=N - 1)
                z = zT[:, 0:4, bass.ds(base, WIN)]
                dve.wait_ge(S["z_evac"], g + 2)
                dve.wait_ge(S["added"], g + 1)
                V.tensor_tensor(z, z, stage[:, b % 2], ALU.add).then_inc(S["added"], 1)

            def selection(i, s):
                dve.wait_ge(S["sel_done"], i * 4 + (2 * s + 1))
                dve.sem_inc(S["turn_dve"], 1)
                link(V.tensor_tensor(hot[:, s], bc(iota[:, 0:WIN], 1, 4), bc(relf[:, bass.ds(i * TPT + 4 * s, 4)], 2, WIN), ALU.is_equal))
                V.tensor_tensor(sel[:, s], bc(hot[:, s], 2, 4), bc(ea_sb[:, bass.ds(i * TPT + 4 * s, 4), :], 3, WIN), ALU.mult)

            dve.wait_ge(S["silu_done"], 1)
            low_part(0).then_inc(S["lo_ready"], 1)
            with dve.Fori(0, EDGE_TURNS) as i:
                chain.enter(i, 2)
                selection(i, 0)
                products(i, 0)
                dve.wait_ge(S["silu_done"], i * 2 + 2)
                low_part(1).then_inc(S["lo_ready"], 1)
                add(i, -1, None)
                products(i, 1)
                add(i, 0, None)
                selection(i, 1)
                products(i, 2)
                dve.wait_ge(S["silu_done"], i * 2 + 3)
                low_part(0).then_inc(S["lo_ready"], 1)
                add(i, 1, None)
                products(i, 3)
                add(i, 2, None)
            chain.leave(EDGE_TURNS)
            add(EDGE_TURNS, -1, first_i[0:1, EG:EG + 1])
            dve.wait_ge(S["added"], EG + 2)
            dve.sem_inc(S["added"], 1)
            flag = dve.value_load(flag_i[0:1, 0:1], min_val=0, max_val=ET * P)
            with dve.If(flag > 0):
                dve.sem_inc(S["stray_step_dve"], 1)
                with dve.Fori(0, ET) as t:
                    base = STRAY_TURNS + 3
                    dve.wait_ge(S["stray_step_act"], t + 1)
                    low_part(0, P).then_inc(S["stray_step_dve"], 1)
                    dve.wait_ge(S["stray_gathered"], t * 16 + 16)
                    dve.wait_ge(S["stray_step_pe"], t * (STRAY_TURNS + 2) + 2)
                    w = ps[:, 2, 0:256]
                    V.tensor_tensor(prod[:, 0, 0, 0:128].rearrange("p (a u) -> p a u", a=2),
                                    w[:, 0:128].rearrange("p (a u) -> p a u", a=2), bc(xg[:, 0, 0, 0:64], 1, 2), ALU.mult)
                    V.tensor_tensor(prod[:, 0, 0, 128:512].rearrange("p (c a u) -> p c a u", c=3, a=2),
                                    bc(w[:, 128:256].rearrange("p (a u) -> p a u", a=2), 1, 3),
                                    bc(xg[:, 0, 0, 64:256].rearrange("p (c u) -> p c u", c=3), 2, 2), ALU.mult)
                    V.tensor_copy(stray_cur[:, 0:1], stray_dst[:, bass.ds(t, 1)]).then_inc(S["stray_step_dve"], 1)
                    dve.wait_ge(S["stray_step_dve"], t * base + 3)
                    dve.sem_inc(S["turn_dve"], 1)
                    with dve.Fori(0, STRAY_TURNS) as n:
                        step = t * (3 * STRAY_TURNS) + n * 3
                        V.tensor_scalar(stray_hot, iota, stray_cur[:, 0:1], None, ALU.is_equal).then_inc(S["kdiag"], 1)
                        dve.wait_ge(S["kdiag"], step + 3)
                        V.tensor_scalar(stray_cur[:, 0:1], stray_cur[:, 0:1], -float(STRAY_WIN), None, ALU.add).then_inc(S["kdiag"], 1)
                        dve.wait_ge(S["kdiag"], step + 4)
                        V.tensor_tensor(stray_sel, bc(stray_hot, 1, 4),
                                        bc(ea_sb[:, bass.ds(t, 1), :].rearrange("p a c -> p (a c)"), 2, STRAY_WIN), ALU.mult).then_inc(S["kdiag"], 1)
                        dve.wait_ge(S["kdiag"], step + 5)
                        dve.wait_ge(S["stray_step_pe"], t * (STRAY_TURNS + 2) + n + 3)
                        cols = bass.ds(n * STRAY_WIN, STRAY_WIN)
                        V.tensor_tensor(zT[0:64, 3, cols], zT[0:64, 3, cols], ps[0:64, 4, 0:STRAY_WIN], ALU.add)
                        V.tensor_tensor(zT[64:128, 0:3, cols], zT[64:128, 0:3, cols],
                                        ps[64:128, 4, STRAY_WIN:4 * STRAY_WIN].rearrange("p (c w) -> p c w", c=3), ALU.add)
                        V.tensor_tensor(zT[0:64, 0:3, cols], zT[0:64, 0:3, cols], ps[0:64, 5:8, 0:STRAY_WIN], ALU.add)
                        V.tensor_tensor(zT[64:128, 3, cols], zT[64:128, 3, cols], ps[64:128, 5, STRAY_WIN:2 * STRAY_WIN], ALU.add).then_inc(S["stray_step_dve"], 1)
                        dve.wait_ge(S["stray_step_dve"], t * base + n + 4)
                    dve.sem_inc(S["stray_step_dve"], 1)
            with dve.Else():
                dve.sem_inc(S["turn_dve"], 1)
            dve.sem_inc(S["sums_ready"], 1)

            dve.sem_inc(S["om_ready"], TB)

            def take_logits(i):
                dve.wait_ge(S["gate_ps"], i * TB + 1)
                V.tensor_tensor(logits_all[:, bass.ds(i * (TB * E), TB * E)].rearrange("p (t e) -> p t e", e=E),
                                ps[:, 7, 0:TB * E].rearrange("p (t e) -> p t e", e=E), bc(gateb_b[:], 1, TB), ALU.add).then_inc(S["logit_sb"], 1)

            with dve.Fori(0, NODE_TURNS) as i:
                chain.enter(i, 10)
                xt = resid[:, bass.ds(i * TB, TB), :]
                for j in range(TB):
                    dve.wait_ge(S["gnn_ps"], i * TB + (j + 1))
                    V.tensor_tensor(om[:, j, :], ps[:, j, 256:512], bout_b[:], ALU.add).then_inc(S["om_ready"], 1)
                dve.wait_ge(S["om_ready"], i * TB + 2 * TB)
                dve.sem_inc(S["turn_dve"], 1)
                for j in range(TB):
                    last = V.bn_stats(cstat[:, j, :], om[:, j, :])
                link(last)
                dve.sem_inc(S["turn_dve"], 1)
                for j in range(TB):
                    last = V.bn_aggr(mv[:, j, :], cstat[:, j, :])
                link(last)
                link(V.tensor_tensor(col[:, 4, :], mv[:, :, 0], mv[:, :, 0], ALU.mult))
                V.tensor_tensor(col[:, 0, :], col[:, 4, :], mv[:, :, 1], ALU.add).then_inc(S["om_var"], 1)
                dve.wait_ge(S["om_norm"], i + 1)
                link(V.tensor_scalar(col[:, 4, :], col[:, 1, :], 1e-12, None, ALU.max))
                link(V.reciprocal(col[:, 5, :], col[:, 4, :]))
                for j in range(TB):
                    last = V.scalar_tensor_tensor(om[:, j, :], om[:, j, :], col[:, 5, j:j + 1], gout_b[:], ALU.mult, ALU.mult)
                link(last)
                dve.wait_ge(S["x_summed"], i + 2)
                link(V.tensor_tensor(xt, xt, om[:], ALU.add))
                dve.sem_inc(S["turn_dve"], 1)
                for j in range(TB):
                    last = V.bn_stats(cstat[:, j, :], resid[:, bass.ds(i * TB + j, 1), :].rearrange("p a c -> p (a c)"))
                link(last)
                dve.sem_inc(S["turn_dve"], 1)
                for j in range(TB):
                    last = V.bn_aggr(mv[:, j, :], cstat[:, j, :])
                link(last)
                V.tensor_scalar(col[:, 2, :], mv[:, :, 1], EPS, None, ALU.add).then_inc(S["x2_var"], 1)
                take_logits(i)
                dve.wait_ge(S["x2_std"], i + 1)
                dve.wait_ge(S["xl_stored"], i * TB + TB)
                link(V.reciprocal(col[:, 6, :], col[:, 3, :]))
                V.scalar_tensor_tensor(col[:, 7, :], mv[:, :, 0], -1.0, col[:, 6, :], ALU.mult, ALU.mult).then_inc(S["xl_scale"], 1)
            chain.leave(NODE_TURNS)
            take_logits(NODE_TURNS)
            dve.wait_ge(S["logit_sb"], NODE_TURNS + 1)
            dve.wait_ge(S["xl_stored"], NT + TB)

            l3 = logits.rearrange("p (t e) -> p t e", e=E)

            def r(n):
                return rt[:, n, :].rearrange("p (t e) -> p t e", e=E)

            link(V.tensor_reduce(rcol[:, 0, :], l3, AX.X, ALU.max))
            V.tensor_tensor(r(0), l3, bc(rcol[:, 0, :], 2, E), ALU.subtract).then_inc(S["l_sub"], 1)
            dve.wait_ge(S["l_exp"], 1)
            link(V.tensor_reduce(rcol[:, 1, :], r(1), AX.X, ALU.add))
            link(V.reciprocal(rcol[:, 2, :], rcol[:, 1, :]))
            link(V.tensor_scalar(r(2), r(0), 0.0, None, ALU.is_ge))
            link(V.scalar_tensor_tensor(r(3), r(2), -float(E), bc(iota8, 1, NT), ALU.mult, ALU.add))
            link(V.tensor_reduce(rcol[:, 3, :], r(3), AX.X, ALU.min))
            link(V.tensor_tensor(r(4), r(3), bc(rcol[:, 3, :], 2, E), ALU.is_equal))
            V.tensor_scalar(rt[:, 4, (NT - 1) * E:], rt[:, 4, (NT - 1) * E:], valid, None, ALU.mult).then_inc(S["hot_ready"], 1)
            dve.wait_ge(S["hot_ready"], 1)
            dve.wait_ge(S["pre_ps"], 1)
            tot_et = rt[:, 5, :].rearrange("p (e t) -> p e t", t=NT)
            link(V.tensor_copy(tot_et, ps[:, 6, 0:NT * E].rearrange("p (t e) -> p e t", e=E)))
            link(V.tensor_tensor_scan(rt[:, 6, :], reset, rt[:, 5, :], 0.0, ALU.mult, ALU.add))
            link(V.tensor_tensor(rt[:, 7, :], rt[:, 6, :], rt[:, 5, :], ALU.subtract))
            link(V.tensor_tensor(r(8), ps[:, 5, 0:NT * E].rearrange("p (t e) -> p t e", e=E),
                                 rt[:, 7, :].rearrange("p (e t) -> p t e", t=NT), ALU.add))
            link(V.tensor_tensor(r(9), r(8), r(4), ALU.mult))
            link(V.tensor_reduce(rcol[:, 4, :], r(9), AX.X, ALU.add))
            link(V.tensor_scalar(rcol[:, 5, :], rcol[:, 4, :], float(CAP), None, ALU.is_le))
            link(V.tensor_scalar(rcol[:, 5, NT - 1:NT], rcol[:, 5, NT - 1:NT], valid, None, ALU.mult))
            link(V.tensor_scalar(rcol[:, 6, :], rcol[:, 3, :], float(E), float(SLOTS), ALU.add, ALU.mult))
            link(V.tensor_scalar(rcol[:, 7, :], rcol[:, 4, :], -1.0, None, ALU.add))
            link(V.tensor_tensor(rcol[:, 8, :], rcol[:, 6, :], rcol[:, 7, :], ALU.add))
            link(V.tensor_tensor(rcol[:, 8, :], rcol[:, 8, :], trash_row, ALU.subtract))
            link(V.tensor_tensor(rcol[:, 8, :], rcol[:, 8, :], rcol[:, 5, :], ALU.mult))
            link(V.tensor_tensor(scat_i[:], rcol[:, 8, :], trash_row, ALU.add))
            link(V.tensor_scalar(rcol[:, 9, :], rcol[:, 7, :], float(CAP - 1), 0.0, ALU.min, ALU.max))
            V.tensor_tensor(rcol[:, 10, :], rcol[:, 2, :], rcol[:, 5, :], ALU.mult)
            V.tensor_tensor(gath_i[:], rcol[:, 6, :], rcol[:, 9, :], ALU.add).then_inc(S["slots_ready"], 1)

            dve.sem_inc(S["xbT_sb"], 1)
            dve.sem_inc(S["yst_ready"], 2)

            def rows_copied(pair, s):
                for k in range(2):
                    dve.wait_ge(S["xbT_ps"], pair * 4 + (2 * s + k + 1))
                    V.tensor_copy(xbT[:, k, 0:CAP], ps[:, k, 0:CAP]).then_inc(S["xbT_sb"], 1)

            def results(pair, s, first):
                dve.wait_ge(we_in[s], pair * 64 + 64)
                if not first:
                    dve.wait_ge(y_out[s], pair * 64)
                for c in range(4):
                    dve.wait_ge(S["yexp_ps"], pair * 8 + (4 * s + c + 2))
                    rows = P if c < 3 else LAST_C
                    V.tensor_tensor(yst[0:rows, s, c, :], ps[0:rows, 5 + c % 2, 0:D], b2_sb[0:rows, s, :], ALU.add).then_inc(S["yst_ready"], 1)

            def dve_pair(pair, first, last):
                rows_copied(pair, 1)
                results(pair, 0, first)
                if not last:
                    rows_copied(pair + 1, 0)
                results(pair, 1, first)

            rows_copied(0, 0)
            dve_pair(0, True, False)
            with dve.Fori(1, E // 2 - 1) as i:
                dve_pair(i, False, False)
            dve_pair(E // 2 - 1, False, True)
            for g in range(NODE_TURNS):
                dve.wait_ge(back_in[g], 16 * TB)
                y = xl[:, g * TB:(g + 1) * TB, :]
                big = zflat[:, 0:TB * D].rearrange("p (t c) -> p t c", t=TB)
                low = zflat[:, 1280:1280 + TB * D].rearrange("p (t c) -> p t c", t=TB)
                fin = zflat[:, 2560:2560 + TB * D].rearrange("p (t c) -> p t c", t=TB)
                link(V.tensor_tensor(y, y, bc(rcol[:, 10, g * TB:(g + 1) * TB], 2, D), ALU.mult))
                V.tensor_scalar(fin.bitcast(I32), y, 0.0, 0.0, ALU.mult, ALU.is_equal)
                link(V.tensor_scalar(big, y, FLT_MAX, 1e4, ALU.is_gt, ALU.mult))
                link(V.tensor_scalar(low, y, -FLT_MAX, -1e4, ALU.is_lt, ALU.mult))
                link(V.tensor_tensor(big, big, low, ALU.add))
                link(V.copy_predicated(big, fin.bitcast(I32), y))
                x2 = resid[:, g * TB:(g + 1) * TB, :]
                V.tensor_tensor(x2, x2, big, ALU.add).then_inc(S["out_ready"], 1)

        @block.tensor
        def _(pe):
            T = nc.tensor

            def keep_busy(times, bank, n=512):
                for _ in range(times):
                    T.matmul(ps[:, bank, 0:n], ident, cst[:, 0:n], start=True, stop=True)

            pe.wait_ge(S["scaled"], 1)
            pe.sem_inc(S["kt_ps"], 1)

            def transposes(i, j):
                pe.wait_ge(S["xm_ready"], i * TB + (j + 1))
                if j == 0:
                    pe.wait_ge(S["qT_sb"], i + 1)
                else:
                    pe.wait_ge(S["xT_sb"], i * TB + (j + 1))
                for k in range(2):
                    last = T.transpose(ps[:, j % 2, k * P:(k + 1) * P], xm[:, j, k * P:(k + 1) * P], ident)
                last.then_inc(S["xT_ps"], 1)

            with pe.Fori(0, NODE_TURNS) as i:
                transposes(i, 0)
                transposes(i, 1)
                for j in range(TB):
                    n = i * TB + (j + 1) + (1 if j == 0 else 0)
                    pe.wait_ge(S["xT_sb"], i * TB + (j + 3))
                    pe.wait_ge(S["y_sb"], n)
                    pe.wait_ge(S["s_sb"], n)
                    for k in range(2):
                        T.matmul(ps[:, 2 + j % 2, k * P:(k + 1) * P], xT[:, j, k, :], wy[:, k, :], start=(k == 0), stop=False, skip_group_check=True)
                    for k in range(2):
                        last = T.matmul(ps[:, 2 + j % 2, 256 + k * P:256 + (k + 1) * P], xT[:, j, k, :], ws[:, k, :], start=False, stop=(k == 1), skip_group_check=True)
                    last.then_inc(S["ys_ps"], 1)
                    pe.wait_ge(S["qkv_sb"], n)
                    for k in range(2):
                        last = T.matmul(ps[:, 4 + j % 2, 0:3 * HD], xT[:, j, k, :], wqkv[:, k, :], start=(k == 0), stop=(k == 1))
                    last.then_inc(S["qkv_ps"], 1)
                    if j + 2 < TB:
                        transposes(i, j + 2)
                pe.wait_ge(S["kmax_sb"], i + 1)
                for n, (a, b) in enumerate(((0, 2), (2, 4), (4, 5))):
                    bank, c0 = 6 + n // 2, 256 * (n % 2)
                    for k in range(2):
                        last = T.matmul(ps[:, bank, c0:c0 + (b - a) * P], wqkv[:, k, HD:2 * HD], xT[:, a:b, k, :],
                                        start=(k == 0), stop=(k == 1))
                last.then_inc(S["kt_ps"], 1)
                pe.wait_ge(S["qn_ready"], i + 2)
                pe.wait_ge(S["xT_sb"], i * TB + (TB + 2))
                for j in range(TB):
                    last = T.transpose(ps[:, j // 4, (j % 4) * P:(j % 4 + 1) * P], qn[:, j, :], ident)
                last.then_inc(S["qT_ps"], 1)
            pe.wait_ge(S["kdiag"], 1)
            pe.wait_ge(S["qT_sb"], NODE_TURNS + 1)
            T.matmul(ps[:, 0, 0:P], ones, xn[:, 0, 0:P], start=True, stop=True).then_inc(S["kmax_b"], 1)
            pe.wait_ge(S["kdiag"], 2)
            pe.wait_ge(S["k_exp"], 1)
            pe.wait_ge(S["y_sb"], NT + 2)
            pe.wait_ge(S["s_sb"], NT + 2)
            for t in range(NT):
                T.matmul(ps[:, 1, 0:HD], kv[:, t, HD:2 * HD], kv[:, t, 0:HD], start=(t == 0), stop=False)
                T.matmul(ps[:, 2, 0:1], kv[:, t, 0:HD], ones[:, 0:1], start=(t == 0), stop=False)
            T.matmul(ps[:, 1, 0:HD], memv[:], memk[:], start=False, stop=True)
            T.matmul(ps[:, 2, 0:1], memk[:], ones[0:NUM_MEM, 0:1], start=False, stop=True).then_inc(S["ctx_ps"], 1)
            pe.wait_ge(S["ctx_sb"], 1)
            T.matmul(ps[:, 3, 0:D], xn[:, 1, 0:P], wout[:], start=True, stop=True).then_inc(S["mixw_ps"], 1)
            pe.wait_ge(S["first_row"], 1)
            T.matmul(ps[:, 7, 0:EG], ones[0:1, :], first_f, start=True, stop=True).then_inc(S["first_ps"], 1)
            pe.wait_ge(S["strays_sum"], 1)
            T.matmul(ps[0:1, 6, 0:1], flag_f[:, 0:1], ones[:, 0:1], start=True, stop=True).then_inc(S["flag_ps"], 1)
            pe.sem_inc(S["sel_done"], 2)

            def hidden(s, landed, silus):
                pe.wait_ge(es_in[s], landed)
                if silus is not None:
                    pe.wait_ge(S["silu_done"], silus)
                T.matmul(ps[:, s, :], fc1_r[:], es_r[:, s, :], start=True, stop=True).then_inc(S["h_ready"], 1)

            def tile_weights(out, s, c0):
                for part in range(2):
                    last = T.matmul(out, h_r[:, s, c0:c0 + P], fc2_r[:, part, :], start=(part == 0), stop=(part == 1))
                return last

            def weights(k, lows, free):
                pe.wait_ge(S["lo_ready"], lows)
                if free is not None:
                    pe.wait_ge(S["prod_ready"], free)
                for j in range(GT):
                    c0 = (GT * (k % 2) + j) * P
                    last = tile_weights(ps[:, 2 + k % 2, j * 256:(j + 1) * 256], k // 2, c0)
                last.then_inc(S["w_ready"], 1)

            def sums(i, k):
                g1 = i * 4 + (k + 1)
                b = k % 2
                pe.wait_ge(S["prod_ready"], g1)
                pe.wait_ge(S["z_evac"], g1)
                bank = ps[:, 4 + b, 0:8 * WIN].rearrange("p (q w) -> p q w", q=8)
                for j in range(GT):
                    m = sel[:, k // 2, (k % 2) * GT + j]
                    T.matmul(bank[:, 3:7], prod[:, b, j, 0:P], m, start=(j == 0), stop=False, skip_group_check=True)
                    for c in range(1, 4):
                        last = T.matmul(bank[:, c - 1:8:8 - c], prod[:, b, j, c * P:(c + 1) * P], m[:, 0:c + 1:c],
                                        start=False, stop=(j == GT - 1 and c == 3), skip_group_check=True)
                last.then_inc(S["sel_done"], 1)

            hidden(0, 32, None)
            pe.wait_ge(S["flag_ready"], 1)
            keep_busy(5, 3)
            weights(0, 1, None)
            with pe.Fori(0, EDGE_TURNS) as i:
                hidden(1, i * 32 + 32, i * 2 + 1)
                weights(1, i * 2 + 1, None)
                sums(i, 0)
                hidden(0, i * 32 + 64, i * 2 + 1)
                weights(2, i * 2 + 2, i * 4 + 1)
                sums(i, 1)
                weights(3, i * 2 + 2, i * 4 + 2)
                sums(i, 2)
                weights(0, i * 2 + 3, i * 4 + 3)
                sums(i, 3)
            pe.wait_ge(S["flag_ready"], 1)
            flag = pe.value_load(flag_i[0:1, 0:1], min_val=0, max_val=ET * P)
            pe.wait_ge(S["added"], EG + 3)
            with pe.If(flag > 0):
                with pe.Fori(0, ET) as t:
                    base = STRAY_TURNS + 3
                    pe.wait_ge(es_in[1], t * 32 + 32 * (EDGE_TURNS + 1))
                    T.matmul(ps[:, 0, 0:P], fc1_r[:], es_r[:, 1, 0:P], start=True, stop=True).then_inc(S["stray_step_pe"], 1)
                    pe.wait_ge(S["stray_step_dve"], t * base + 2)
                    tile_weights(ps[:, 2, 0:256], 0, 0).then_inc(S["stray_step_pe"], 1)
                    with pe.Fori(0, STRAY_TURNS) as n:
                        pe.wait_ge(S["kdiag"], t * (3 * STRAY_TURNS) + n * 3 + 5)
                        pe.wait_ge(S["stray_step_dve"], t * base + n + 3)
                        T.matmul(ps[:, 4, 0:4 * STRAY_WIN], prod[:, 0, 0, 0:P], stray_sel, start=True, stop=True)
                        for c in range(1, 4):
                            T.matmul(ps[:, 4 + c, 0:STRAY_WIN], prod[:, 0, 0, c * P:(c + 1) * P], stray_sel[:, 0, :],
                                     start=True, stop=False, skip_group_check=True)
                            last = T.matmul(ps[:, 5, STRAY_WIN:2 * STRAY_WIN], prod[:, 0, 0, c * P:(c + 1) * P], stray_sel[:, c, :],
                                            start=False, stop=(c == 3), skip_group_check=True)
                        last.then_inc(S["stray_step_pe"], 1)
            with pe.Else():
                pe.sem_inc(S["turn_pe"], 1)
            pe.wait_ge(S["sums_ready"], 1)

            pe.sem_inc(S["gate_ps"], 1)
            keep_busy(4, 3)

            def lin2_and_attention(i, j):
                pe.wait_ge(S["gnn_sb"], i * TB + (j + 1))
                nodes = slice((i * TB + j) * P, (i * TB + j + 1) * P)
                for b, c0 in ((3, 0), (0, 64), (1, 128), (2, 192)):
                    T.matmul(ps[:, j, c0:c0 + MUL], zT[:, b, nodes], wz[:, b, :], start=(b == 3), stop=False, skip_group_check=True)
                T.matmul(ps[:, j, 256:512], zT[:, 4, nodes], mix_w[:], start=False, stop=True, skip_group_check=True).then_inc(S["gnn_ps"], 1)

            def xl_transposed(i, j):
                if j == 0:
                    pe.wait_ge(S["logit_sb"], i + 1)
                pe.wait_ge(S["xl_ready"], i * TB + (j + 1))
                pe.wait_ge(S["xlT_sb"], i * TB + (2 + max(0, j - 1)))
                for k in range(2):
                    last = T.transpose(ps[:, 5 + j % 2, k * P:(k + 1) * P], xls[:, j, k * P:(k + 1) * P], ident)
                last.then_inc(S["xlT_ps"], 1)

            def gate(i, j):
                pe.wait_ge(S["xlT_sb"], i * TB + (j + 3))
                for k in range(2):
                    last = T.matmul(ps[:, 7, j * E:(j + 1) * E], xlT[:, j % 2, k, :], gatew[:, k, :], start=(k == 0), stop=(k == 1))
                last.then_inc(S["gate_ps"], 1)

            for j in range(TB):
                lin2_and_attention(0, j)
            for i in range(NODE_TURNS + 1):
                for j in range(TB):
                    if i > 0:
                        xl_transposed(i - 1, j)
                    if i + 1 < NODE_TURNS:
                        lin2_and_attention(i + 1, j)
                    if i > 0:
                        gate(i - 1, j)
                keep_busy(22 if i == 0 else 12, 5, 256)
            pe.wait_ge(S["hot_ready"], 1)
            T.matmul(ps[:, 5, 0:NT * E], tri, rt[:, 4, :], start=True, stop=True)
            T.matmul(ps[:, 6, 0:NT * E], ones, rt[:, 4, :], start=True, stop=True).then_inc(S["pre_ps"], 1)
            pe.wait_ge(S["slots_ready"], 1)
            pe.sem_inc(S["yexp_ps"], 1)

            def rows_transposed(pair, s):
                pe.wait_ge(xb_in[s], pair * 32 + 32)
                pe.wait_ge(S["xbT_sb"], pair * 4 + (2 * s + 1))
                for k in range(2):
                    for c in range(4):
                        rows = P if c < 3 else LAST_C
                        last = T.transpose(ps[:, k, c * P:c * P + rows], xb[0:rows, s, c, k * P:(k + 1) * P], ident[0:rows, 0:rows])
                    last.then_inc(S["xbT_ps"], 1)

            def layer1(pair, s):
                pe.wait_ge(we_in[s], pair * 64 + 64)
                pe.wait_ge(S["xbT_sb"], pair * 4 + (2 * s + 3))
                for f in range(FB):
                    pe.wait_ge(S["hid_sb"], pair * (2 * FB) + (s * FB + f + 1))
                    for k in range(2):
                        last = T.matmul(ps[:, 2 + (s * FB + f) % 3, 0:CAP], w1_sb[:, s, k, f * P:(f + 1) * P], xbT[:, k, 0:CAP],
                                        start=(k == 0), stop=(k == 1))
                    last.then_inc(S["hid_ps"], 1)

            def layer2(pair, s):
                for c in range(4):
                    pe.wait_ge(S["yst_ready"], pair * 8 + (4 * s + c + 1))
                    rows = P if c < 3 else LAST_C
                    for f in range(FB):
                        if c == 0:
                            pe.wait_ge(S["hid_sb"], pair * (2 * FB) + (s * FB + f + 4))
                        last = T.matmul(ps[0:rows, 5 + c % 2, 0:D], hid[:, f, c * P:c * P + rows], w2_sb[:, s, f, :],
                                        start=(f == 0), stop=(f == FB - 1))
                    last.then_inc(S["yexp_ps"], 1)

            def pe_pair(pair, last):
                layer1(pair, 0)
                rows_transposed(pair, 1)
                layer2(pair, 0)
                layer1(pair, 1)
                if not last:
                    rows_transposed(pair + 1, 0)
                layer2(pair, 1)

            rows_transposed(0, 0)
            with pe.Fori(0, E // 2 - 1) as i:
                pe_pair(i, False)
            pe_pair(E // 2 - 1, True)


def kernel(**inputs):
    import numpy as np
    import concourse.bacc as bacc
    from concourse.bass_utils import run_bass_kernel_spmd as run

    g = {k: np.asarray(v) for k, v in inputs.items()}
    perm = np.concatenate([np.arange(MUL)] + [MUL + 3 * np.arange(MUL) + c for c in range(3)])
    back = np.argsort(perm)
    zero = np.zeros((MUL, MUL), np.float32)

    def rows128(a):
        return a.reshape(2, P, -1).transpose(1, 0, 2)

    def diag(a, b):
        return np.block([[a, zero], [zero, b]])

    pad_e = ET * P - EDGES
    src = np.pad(g["src"], (0, pad_e), mode="edge")
    dst = np.pad(g["dst"], (0, pad_e), mode="edge")
    ea = np.pad(g["edge_attr_4"], ((0, pad_e), (0, 0)))
    es = np.pad(g["edge_attr_8"], ((0, pad_e + CHUNK), (0, 0))).T
    sc0, sc1, l0, l1 = (g["L0_gnn_" + n] for n in ("sc_w0", "sc_w1", "lin1_w0", "lin1_w1"))
    w00, w01, w10, w11 = (g["L0_gnn_lin2_w" + n] for n in ("00", "01", "10", "11"))
    fc2 = g["L0_gnn_fc_w2"].reshape(MUL, 4, MUL)[:, [0, 2, 3, 1]].reshape(MUL, 4 * MUL)
    zc = np.concatenate([w11, w10])
    mem = g["L0_mix_mem_kv"].reshape(2, HD, NUM_MEM)
    consts = np.zeros((P, C_END), np.float32)
    consts[:, C_IDENT:C_TRI] = np.eye(P)
    consts[:, C_TRI:C_BLOCK] = np.triu(np.ones((P, P)))
    consts[:, C_BLOCK:C_ONES] = np.kron(np.eye(HEADS), np.ones((DH, DH)))
    consts[:, C_ONES:C_IOTA] = 1.0
    consts[:, C_IOTA:C_VALID] = np.arange(STRAY_WIN)
    consts[:LAST, C_VALID] = 1.0
    consts[:, C_RESET:C_IOTA8] = (np.arange(NT * E) % NT != 0)
    consts[:, C_IOTA8:C_TRASH] = np.arange(E)
    consts[:, C_TRASH:C_HIGH] = TRASH + np.arange(NT)[None, :] * P + np.arange(P)[:, None]
    consts[0:16, C_HIGH] = 1.0
    consts[16:32, C_LOW] = 1.0
    arrays = dict(
        x=np.pad(g["x"][:, perm], ((0, NPAD - N), (0, 0)), mode="edge"),
        node_a=np.pad(g["node_vec1"][:, 0], (0, NPAD - N), mode="edge").reshape(NT, P).T,
        src=src.reshape(EG, GT, P).transpose(2, 0, 1),
        dst=dst.reshape(ET, P).T,
        dst_first=np.concatenate([np.zeros(1, dst.dtype), dst[::GT * P]])[None],
        ea=ea.reshape(ET, P, 4).transpose(1, 0, 2),
        es=es.reshape(P, -1),
        w_y=rows128(np.concatenate([diag(l0, l1), diag(l1, l1)])),
        w_s=rows128(np.concatenate([diag(sc0, sc1), diag(sc1, sc1)])),
        w_z=np.stack([zc, zc, zc, np.concatenate([w00, w01])], 1),
        fc1=np.tile(g["L0_gnn_fc_w1"], (4, 2)),
        fc2=np.tile(fc2, (2, 1)),
        w_qkv=rows128(g["L0_mix_w_qkv"][perm]),
        g_pre=g["L0_mix_g_pre"][perm].reshape(2, P).T,
        mem_kt=mem[0],
        mem_k=mem[0].T,
        mem_v=mem[1].T,
        w_out=g["L0_mix_w_out"][:, perm],
        b_out=g["L0_mix_b_out"][perm][None],
        g_out=g["L0_mix_g_out"][perm][None],
        gate_w=rows128(g["L0_ffn_gate_w"][perm]),
        gate_b=g["L0_ffn_gate_b"][None],
        w1=g["L0_ffn_w1"][:, perm].reshape(E, 2, P, F).transpose(0, 2, 1, 3),
        b1=g["L0_ffn_b1"].reshape(E, FB, P).transpose(0, 2, 1),
        w2=g["L0_ffn_w2"][:, :, perm].reshape(E, FB, P, D).transpose(0, 2, 1, 3),
        b2=g["L0_ffn_b2"][:, perm],
        consts=consts,
    )
    nc = bacc.Bacc("TRN2", target_bir_lowering=False, num_devices=1)
    data, args = {}, {}
    for name, a in arrays.items():
        data[f"in_{name}"] = np.ascontiguousarray(a)
        args[name] = nc.dram_tensor(f"in_{name}", a.shape, mybir.dt.from_np(a.dtype), kind="ExternalInput").ap()
    args["out"] = nc.dram_tensor("out_0", (NPAD, D), F32, kind="ExternalOutput").ap()
    program(nc, **args)
    result = run(nc, [data], core_ids=[0])
    return result.results[0]["out_0"][:N][:, back]
```

```python
from contextlib import ExitStack
import math

import concourse.bass as bass
from concourse import mybir

F32 = mybir.dt.float32
I32 = mybir.dt.int32
F32R = mybir.dt.float32r
ALU = mybir.AluOpType
ACT = mybir.ActivationFunctionType
AX = mybir.AxisListType

P = 128
N = 3125
D = 256
MUL = 64
NT = 25
TB = 5
NODE_TURNS = NT // TB
NPAD = NT * P
LAST = N - (NT - 1) * P
EDGES = 53125
GT = 2
GROUPS_PER_TURN = 4
TPT = GT * GROUPS_PER_TURN
EDGE_TURNS = -(-EDGES // (P * TPT))
ET = EDGE_TURNS * TPT
EG = ET // GT
CHUNK = 4 * P
WIN = 24
STRAY_WIN = 120
STRAY_TURNS = -(-N // STRAY_WIN)
NZ = STRAY_TURNS * STRAY_WIN
assert NZ >= N + WIN and NZ >= NPAD
HD = 128
HEADS, DH = 4, 32
NUM_MEM = 4
E = 8
CAP = -(-5 * N // (4 * E))
SLOTS = CAP
F = 1024
FB = F // P
LAST_C = CAP - 3 * P
TRASH = E * SLOTS

W_SCALE = 1.679 / 8.0
INV_SQRT3 = 1.0 / math.sqrt(3.0)
Y_SCALE = 1.0 / 8.0
S_SCALE = math.sin(math.pi / 8.0) / 8.0
Z_SCALE = math.cos(math.pi / 8.0) / math.sqrt(128.0) / math.sqrt(20.0)
SM_SCALE = DH ** -0.5
ES_SCALE = 1.0 / math.sqrt(8.0)
EPS = 1e-5
FLT_MAX = 3.4028234663852886e38

C_IDENT, C_TRI, C_BLOCK, C_ONES, C_IOTA, C_VALID, C_RESET, C_IOTA8, C_TRASH, C_HIGH, C_LOW, C_END = (
    0, 128, 256, 384, 512, 632, 633, 833, 841, 866, 867, 868)


class Chain:

    def __init__(self, eng, sem):
        self.eng, self.sem, self.n, self.offset = eng, sem, 0, 0

    def link(self, ins):
        self.n += 1
        ins.then_inc(self.sem, 1)
        self.eng.wait_ge(self.sem, self.offset + self.n)

    def enter(self, i, per_turn):
        self.start, self.per_turn, self.offset = self.n, per_turn, i * per_turn

    def leave(self, turns):
        assert self.n - self.start == self.per_turn, (self.n - self.start, self.per_turn)
        self.n, self.offset = self.start + turns * self.per_turn, 0


def bc(ap, axis, n):
    v = ap.unsqueeze(axis)
    shape = list(v.shape)
    shape[axis] = n
    return v.to_broadcast(shape)


def program(nc, x, node_a, src, dst, dst_first, ea, es, w_y, w_s, w_z, fc1, fc2, w_qkv, g_pre,
            mem_kt, mem_k, mem_v, w_out, b_out, g_out, gate_w, gate_b, w1, b1, w2, b2, consts, out):
    y_dram = nc.dram_tensor("y_dram", (NPAD, D), F32)
    buf_dram = nc.dram_tensor("buf_dram", (TRASH + NPAD, D), F32)
    es_len = es.shape[1] * P // 8
    es_hl = nc.dram_tensor("es_hl", (2 * 8, es_len), F32)
    ybuf_dram = nc.dram_tensor("ybuf_dram", (E * SLOTS, D), F32)

    with ExitStack() as ctx:
        def sb(name, shape, dt=F32):
            return ctx.enter_context(nc.sbuf_tensor(name, shape, dt))

        def sem(name):
            return ctx.enter_context(nc.semaphore(name))

        ps = ctx.enter_context(nc.psum_tensor("ps", [P, 8, 512], F32))

        cst = sb("cst", [P, C_END])
        ident, tri, block_mask = cst[:, C_IDENT:C_TRI], cst[:, C_TRI:C_BLOCK], cst[:, C_BLOCK:C_ONES]
        ones, iota = cst[:, C_ONES:C_IOTA], cst[:, C_IOTA:C_VALID]
        valid, reset, iota8 = cst[:, C_VALID:C_RESET], cst[:, C_RESET:C_IOTA8], cst[:, C_IOTA8:C_TRASH]
        trash_row = cst[:, C_TRASH:C_HIGH]
        resid = sb("resid", [P, NT, D])
        zT = sb("zT", [P, 5, NZ])
        wys = sb("wys", [P, 2, 2, P])
        wz = sb("wz", [P, 4, MUL])
        fc1_sb = sb("fc1_sb", [4 * 8, P])
        fc1_hl = sb("fc1_hl", [4 * 8, 2, P])
        fc1_r = sb("fc1_r", [P, P], F32R)
        fc2_sb = sb("fc2_sb", [P, 256])
        fc2_r = sb("fc2_r", [P, 2, 256], F32R)
        es_r = sb("es_r", [P, 2, CHUNK], F32R)
        h_r = sb("h_r", [P, 2, CHUNK], F32R)
        wqkv = sb("wqkv", [P, 2, 3 * HD])
        gpre = sb("gpre", [P, 2])
        node_a_sb = sb("node_a_sb", [P, NT])
        memkt = sb("memkt", [P, NUM_MEM])
        memk = sb("memk", [NUM_MEM, HD])
        memv = sb("memv", [NUM_MEM, HD + 1])
        wout = sb("wout", [P, D])
        bout_b = sb("bout_b", [P, D])
        gout_b = sb("gout_b", [P, D])
        gatew = sb("gatew", [P, 2, E])
        gateb_b = sb("gateb_b", [P, E])
        mix_w = sb("mix_w", [P, D])
        ksum_inv = sb("ksum_inv", [P, 1])
        ea_sb = sb("ea_sb", [P, ET, 4])
        dst_i = sb("dst_i", [P, ET], I32)
        first_i = sb("first_i", [1, 3 + EG], I32)
        region = sb("region", [P, 14200])
        KV = 2 * HD + 1
        kv = region[:, 0:NT * KV].rearrange("p (t c) -> p t c", t=NT)
        r0 = NT * KV
        xm = region[:, r0:r0 + 1280].rearrange("p (t c) -> p t c", t=TB)
        xT = region[:, r0 + 1280:r0 + 2560].rearrange("p (t k c) -> p t k c", t=TB, k=2)
        ysb = region[:, r0 + 2560:r0 + 3840].rearrange("p (t c) -> p t c", t=TB)
        qs = region[:, r0 + 3840:r0 + 4480].rearrange("p (t c) -> p t c", t=TB)
        qn = region[:, r0 + 4480:r0 + 5120].rearrange("p (t c) -> p t c", t=TB)
        st = region[:, r0 + 5120:r0 + 5270].rearrange("p (t c) -> p t c", t=NT)
        kmax_run = region[:, r0 + 5280:r0 + 5408]
        kmax_turn = region[:, r0 + 5408:r0 + 5536]
        kmax_diag = region[:, r0 + 5536:r0 + 5664]
        ctx_kv = region[:, r0 + 5664:r0 + 5792]
        ctx_vk = region[:, r0 + 5792:r0 + 5920]
        (n_var, n_std, n_size, n_rstd, n_norm, n_inv, n_yscale, n_xmscale, n_resscale, n_resbias) = (
            region[:, r0 + 5920 + n * NT:r0 + 5920 + (n + 1) * NT] for n in range(10))
        mv_x = region[:, r0 + 6200:r0 + 6250].rearrange("p (t c) -> p t c", t=NT)
        mv = sb("mv", [P, TB, 2])
        col = sb("col", [P, 8, TB])
        qcol = sb("qcol", [P, 2, TB * HEADS])
        kmx = sb("kmx", [P, 4])
        prod = region[:, 3800:3800 + 2048].rearrange("p (g j c) -> p g j c", g=2, j=GT)
        h_f = region[:, 5900:5900 + 1024].rearrange("p (s c) -> p s c", s=2)
        sel = region[:, 8100:8100 + 8 * 4 * WIN].rearrange("p (s t c w) -> p s t c w", s=2, t=4, c=4)
        hot = region[:, 8900:8900 + TPT * WIN].rearrange("p (t w) -> p t w", t=TPT)
        stage = region[:, 9200:9200 + 2 * 4 * WIN].rearrange("p (s b w) -> p s b w", s=2, b=4)
        stray_cur = region[:, 9820:9822]
        stray_hot = region[:, 9830:9830 + STRAY_WIN]
        stray_sel = region[:, 9950:9950 + 4 * STRAY_WIN].rearrange("p (c w) -> p c w", c=4)
        idx_sb = sb("idx_sb", [P, GROUPS_PER_TURN, GT], I32)
        flag_i = sb("flag_i", [1, 2], I32)
        flag_f = sb("flag_f", [P, 2])
        xl = region[:, 0:NT * 256].rearrange("p (t c) -> p t c", t=NT)
        om = region[:, 9600:10880].rearrange("p (t c) -> p t c", t=TB)
        xls = region[:, 10880:12160].rearrange("p (t c) -> p t c", t=TB)
        gnn = region[:, 12160:13440].rearrange("p (t c) -> p t c", t=TB)
        xlT = region[:, 13440:13952].rearrange("p (s k c) -> p s k c", s=2, k=2)
        rt = region[:, 9600:9600 + 12 * NT * E].rearrange("p (a c) -> p a c", a=12)
        logits_all = sb("logits_all", [P, (NODE_TURNS + 1) * TB * E])
        logits = logits_all[:, TB * E:]
        rcol = sb("rcol", [P, 12, NT])
        cstat = sb("cstat", [P, TB, 6])
        scat_i = sb("scat_i", [P, NT], I32)
        gath_i = sb("gath_i", [P, NT], I32)
        w1_sb = sb("w1_sb", [P, 2, 2, F])
        w1_flat = w1_sb[:].rearrange("p s k f -> p (s k f)")
        xg = w1_flat[:, 0:TPT * D].rearrange("p (g j c) -> p g j c", g=4, j=GT)
        relf, inw, stray_new, stray_dst = (w1_flat[:, TPT * D + n * ET:TPT * D + (n + 1) * ET] for n in range(4))
        first_f = w1_flat[0:1, TPT * D + 4 * ET:TPT * D + 4 * ET + EG]
        zflat = zT[:].rearrange("p b z -> p (b z)")
        w2_sb = zflat[:, 0:2 * FB * D].rearrange("p (s f d) -> p s f d", s=2, f=FB)
        ew = es.shape[1]
        es_hi, es_lo, es_in_f = (zflat[:, n * ew:(n + 1) * ew] for n in range(3))
        o = 2 * FB * D
        hid = zflat[:, o:o + FB * CAP].rearrange("p (f c) -> p f c", f=FB)
        o += FB * CAP + 8
        xb = zflat[:, o:o + 2048].rearrange("p (s c d) -> p s c d", s=2, c=4)
        o += 2048
        xbT = zflat[:, o:o + 1024].rearrange("p (k c) -> p k c", k=2)
        o += 1024
        yst = zflat[:, o:o + 2048].rearrange("p (s c d) -> p s c d", s=2, c=4)
        o += 2048
        assert o <= 5 * NZ
        b1_sb = sb("b1_sb", [P, 2, FB])
        b2_sb = sb("b2_sb", [P, 2, D])

        S = {}
        for name in """consts_in weights_in later_in es_raw_in es_split es_stored zeroed lo_ready edges_in scaled dve_chain act_chain turn_dve turn_pe turn_act turn_pool turn_sp
            var_ready std_ready size_ready norm_ready cols_ready resid_ready xm_ready xT_ps xT_sb ys_ps y_sb s_sb qkv_ps qkv_sb kmaxT_ps kmax_sb q_sub q_exp
            qn_ready qT_ps qT_sb kdiag kmax_b k_sub k_exp k_masked ctx_ps ctx_norm ctxT_ps ctx_sb mixw_ps mixw_sb
            first_row first_ps strays_sum flag_ps flag_ready h_ready silu_done w_ready prod_ready hot_done sel_made sel_done z_evac added
            stray_gathered stray_step_dve stray_step_act stray_step_pe
            sums_ready gnn_ps om_ready om_var om_norm gnn_sb x_summed x2_var x2_std xl_scale xl_ready xl_stored xlT_ps xlT_sb gate_ps logit_sb
            l_sub l_exp hot_ready pre_ps slots_ready scattered zero_in
            xbT_ps xbT_sb hid_ps hid_sb yexp_ps yst_ready y_scaled inf_ready inf_scaled out_ready out_stored""".split():
            S[name] = sem(name)
        y_stored = [sem(f"y_stored{j}") for j in range(TB)]
        x_in = [sem(f"x_in{s}") for s in range(NODE_TURNS)]
        es_in = [sem(f"es_in{s}") for s in range(2)]
        idx_in = [sem(f"idx_in{k}") for k in range(4)]
        rows_in = [sem(f"rows_in{k}") for k in range(4)]
        we_in = [sem(f"we_in{s}") for s in range(2)]
        xb_in = [sem(f"xb_in{s}") for s in range(2)]
        y_out = [sem(f"y_out{s}") for s in range(2)]
        back_in = [sem(f"back_in{s}") for s in range(NODE_TURNS)]

        x_v = x.rearrange("(t p) c -> p t c", p=P)
        y_v = y_dram[:].rearrange("(t p) c -> p t c", p=P)
        out_v = out.rearrange("(t p) c -> p t c", p=P)

        block = ctx.enter_context(nc.Block())

        @block.sync
        def _(sp):
            def load_scalars(s, first, n):
                for half in range(2):
                    sp.dma_start(es_r[16 * half:16 * half + 16, s, 0:n].bitcast(F32), es_hl[:, bass.ds(first, n)]).then_inc(es_in[s], 16)

            def load_rows(s, e):
                sp.dma_start(xb[:, s, 0:3, :], buf_dram[bass.ds(e * SLOTS, 3 * P), :].rearrange("(c p) d -> p c d", p=P)).then_inc(xb_in[s], 16)
                sp.dma_start(xb[0:LAST_C, s, 3, :], buf_dram[bass.ds(e * SLOTS + 3 * P, LAST_C), :]).then_inc(xb_in[s], 16)

            for i in range(NODE_TURNS):
                sp.dma_start(resid[:, i * TB:(i + 1) * TB, :], x_v[:, i * TB:(i + 1) * TB, :]).then_inc(x_in[i], 16)
            sp.dma_start(cst[:], consts).then_inc(S["consts_in"], 16)
            sp.dma_start(node_a_sb[:], node_a).then_inc(S["consts_in"], 16)
            sp.dma_start(ea_sb[:], ea).then_inc(S["edges_in"], 16)
            sp.dma_start(dst_i[:], dst).then_inc(S["edges_in"], 16)
            sp.dma_start(first_i[:], dst_first).then_inc(S["edges_in"], 16)
            for k in range(GROUPS_PER_TURN):
                sp.dma_start(idx_sb[:, k, :], src[:, k, :]).then_inc(idx_in[k], 16)
            with sp.Fori(0, NODE_TURNS) as i:
                for j in range(TB):
                    sp.wait_ge(S["y_sb"], i * TB + (j + 3))
                    sp.sem_inc(S["turn_sp"], 1)
                    sp.dma_start(y_v[:, bass.ds(i * TB + j, 1), :].rearrange("p a c -> p (a c)"), ysb[:, j, :]).then_inc(y_stored[j], 16)
            sp.wait_ge(S["scaled"], 1)
            sp.wait_ge(S["es_stored"], 32)
            for s in range(2):
                load_scalars(s, s * CHUNK, CHUNK)
            with sp.Fori(1, EDGE_TURNS) as i:
                for s in range(2):
                    sp.wait_ge(S["h_ready"], i * 2 + (s - 1))
                    sp.sem_inc(S["turn_sp"], 1)
                    load_scalars(s, i * (2 * CHUNK) + s * CHUNK, CHUNK)
                    for k in range(2 * s, 2 * s + 2):
                        sp.wait_ge(rows_in[k], i * (16 * GT))
                        sp.sem_inc(S["turn_sp"], 1)
                        sp.dma_start(idx_sb[:, k, :], src[:, bass.ds(i * GROUPS_PER_TURN + k, 1), :]
                                     .rearrange("p a j -> p (a j)")).then_inc(idx_in[k], 16)
            sp.wait_ge(S["h_ready"], 2 * EDGE_TURNS - 1)
            load_scalars(0, 2 * EDGE_TURNS * CHUNK, CHUNK)
            sp.wait_ge(S["h_ready"], 2 * EDGE_TURNS)
            load_scalars(1, (2 * EDGE_TURNS + 1) * CHUNK, CHUNK)
            sp.wait_ge(S["flag_ready"], 1)
            flag = sp.value_load(flag_i[0:1, 0:1], min_val=0, max_val=ET * P)
            sp.wait_ge(S["added"], EG + 5)
            with sp.If(flag > 0):
                with sp.Fori(0, ET) as t:
                    sp.wait_ge(S["stray_step_dve"], t * (STRAY_TURNS + 3) + 1)
                    sp.sem_inc(S["turn_sp"], 1)
                    load_scalars(1, t * P, P)
                    sp.wait_ge(es_in[1], t * 32 + 32 * (EDGE_TURNS + 2))
                    sp.sem_inc(S["turn_sp"], 1)
                    sp.dma_start(idx_sb[:, 0, 0:1], src.rearrange("p g j -> p (g j)")[:, bass.ds(t, 1)],
                                 allow_slow_non_contiguous=True).then_inc(idx_in[0], 16)
            with sp.Else():
                sp.sem_inc(S["turn_sp"], 1)
            sp.wait_ge(S["sums_ready"], 1)
            for e in range(2):
                sp.dma_start(w1_sb[:, e], w1[e]).then_inc(we_in[e], 16)
                sp.dma_start(b1_sb[:, e], b1[e]).then_inc(we_in[e], 16)
                sp.dma_start(b2_sb[:, e], b2[e:e + 1, :].partition_broadcast(P)).then_inc(we_in[e], 16)
            sp.wait_ge(S["gnn_ps"], NT)
            for e in range(2):
                sp.dma_start(w2_sb[:, e], w2[e]).then_inc(we_in[e], 16)
            sp.wait_ge(S["scattered"], 16 * NT)
            for e in range(2):
                load_rows(e, e)
            with sp.Fori(0, E // 2 - 1) as i:
                for s in range(2):
                    e = i * 2 + (2 + s)
                    sp.wait_ge(S["xbT_ps"], i * 4 + 2 * s + 2)
                    sp.sem_inc(S["turn_sp"], 1)
                    load_rows(s, e)
                    sp.wait_ge(S["hid_sb"], i * (2 * FB) + (s + 1) * FB + 3)
                    sp.sem_inc(S["turn_sp"], 1)
                    sp.dma_start(w1_sb[:, s], w1[bass.ds(e, 1)].rearrange("a p k f -> p (a k) f")).then_inc(we_in[s], 16)
                    sp.dma_start(b1_sb[:, s], b1[bass.ds(e, 1)].rearrange("a p k -> p (a k)")).then_inc(we_in[s], 16)
                    sp.wait_ge(S["yst_ready"], i * 8 + 4 * s + 6)
                    sp.sem_inc(S["turn_sp"], 1)
                    sp.dma_start(w2_sb[:, s], w2[bass.ds(e, 1)].rearrange("a p k f -> p (a k) f")).then_inc(we_in[s], 16)
                    sp.dma_start(b2_sb[:, s], b2[bass.ds(e, 1), :].partition_broadcast(P)).then_inc(we_in[s], 16)
            for g in range(NODE_TURNS):
                sp.wait_ge(S["out_ready"], g + 1)
                sp.dma_start(out_v[:, g * TB:(g + 1) * TB, :], resid[:, g * TB:(g + 1) * TB, :]).then_inc(S["out_stored"], 16)
            sp.wait_ge(S["out_stored"], 16 * NODE_TURNS)

        @block.gpsimd
        def _(pool):
            pool.wait_ge(S["es_raw_in"], 16)
            nc.gpsimd.tensor_copy(es_hi.bitcast(F32R), es_in_f).then_inc(S["es_split"], 1)
            pool.wait_ge(S["es_split"], 1)
            nc.gpsimd.tensor_tensor(es_lo.bitcast(F32R), es_in_f, es_hi, ALU.subtract).then_inc(S["es_split"], 1)
            pool.wait_ge(S["es_split"], 2)
            for part, rows in ((es_hi, es_hl[0:8, :]), (es_lo, es_hl[8:16, :])):
                pool.dma_start(rows.rearrange("r e -> (r e)").rearrange("(p f) -> p f", p=P),
                               part).then_inc(S["es_stored"], 16)
            pool.wait_ge(S["es_stored"], 32)
            nc.gpsimd.memset(zT[:, 0:4], 0.0).then_inc(S["zeroed"], 1)
            pool.wait_ge(S["zeroed"], 1)
            pool.dma_start(buf_dram[0:TRASH, :].rearrange("r d -> (r d)").rearrange("(p f) -> p f", p=P),
                           zflat[:, 0:TRASH * D // P]).then_inc(S["zero_in"], 16)
            for j in range(TB):
                pool.wait_ge(y_stored[j], 16 * NODE_TURNS)

            def gather(k):
                for j in range(GT):
                    pool.indirect_dma_start(xg[:, k, j, :], None, y_dram[:], bass.IndirectOffsetOnAxis(
                        ap=idx_sb[:, k, j:j + 1], axis=0)).then_inc(rows_in[k], 16)

            for k in range(GROUPS_PER_TURN):
                pool.wait_ge(idx_in[k], 16)
                gather(k)
            with pool.Fori(1, EDGE_TURNS) as i:
                for k in range(GROUPS_PER_TURN):
                    pool.wait_ge(S["prod_ready"], i * 4 + (k - 3))
                    pool.sem_inc(S["turn_pool"], 1)
                    pool.wait_ge(idx_in[k], i * 16 + 16)
                    pool.sem_inc(S["turn_pool"], 1)
                    gather(k)
            pool.wait_ge(S["flag_ready"], 1)
            flag = pool.value_load(flag_i[0:1, 0:1], min_val=0, max_val=ET * P)
            pool.wait_ge(S["added"], EG + 5)
            with pool.If(flag > 0):
                with pool.Fori(0, ET) as t:
                    pool.wait_ge(idx_in[0], t * 16 + 16 * (EDGE_TURNS + 1))
                    pool.sem_inc(S["turn_pool"], 1)
                    pool.indirect_dma_start(xg[:, 0, 0, :], None, y_dram[:], bass.IndirectOffsetOnAxis(
                        ap=idx_sb[:, 0, 0:1], axis=0)).then_inc(S["stray_gathered"], 16)
                    pool.wait_ge(S["stray_gathered"], t * 16 + 16)
                    pool.sem_inc(S["turn_pool"], 1)
            with pool.Else():
                pool.sem_inc(S["turn_pool"], 1)
            pool.sem_inc(S["x_summed"], 1)
            with pool.Fori(0, NODE_TURNS) as i:
                pool.wait_ge(S["gnn_sb"], i * TB + 2 * TB)
                xt = resid[:, bass.ds(i * TB, TB), :]
                nc.gpsimd.tensor_tensor(xt, xt, gnn[:], ALU.add).then_inc(S["x_summed"], 1)
            pool.wait_ge(S["slots_ready"], 1)
            pool.wait_ge(S["zero_in"], 16)
            for t in range(NT):
                pool.indirect_dma_start(buf_dram[:], bass.IndirectOffsetOnAxis(ap=scat_i[:, t:t + 1], axis=0),
                                        xl[:, t, :], None).then_inc(S["scattered"], 16)
            pool.wait_ge(S["scattered"], 16 * NT)
            for s in range(2):
                pool.wait_ge(y_out[s], 16 * 4 * (E // 2))
            for t in range(NT):
                pool.indirect_dma_start(xl[:, t, :], None, ybuf_dram[:], bass.IndirectOffsetOnAxis(
                    ap=gath_i[:, t:t + 1], axis=0)).then_inc(back_in[t // TB], 16)

        @block.scalar
        def _(act):
            A = nc.scalar
            chain = Chain(act, S["act_chain"])
            loads = [(wys[:, :, 0, :], w_y), (wys[:, :, 1, :], w_s), (wqkv[:], w_qkv), (gpre[:], g_pre)]
            later = [(wz[:], w_z), (fc1_sb[:], fc1),
                     (fc2_sb[:], fc2), (memkt[:], mem_kt), (memk[:], mem_k), (memv[:, 0:HD], mem_v), (wout[:], w_out),
                     (bout_b[:], b_out.partition_broadcast(P)), (gout_b[:], g_out.partition_broadcast(P)),
                     (gatew[:], gate_w), (gateb_b[:], gate_b.partition_broadcast(P))]
            for to, of in loads:
                act.dma_start(to, of).then_inc(S["weights_in"], 16)
            for to, of in later:
                act.dma_start(to, of).then_inc(S["later_in"], 16)
            act.dma_start(es_in_f, es).then_inc(S["es_raw_in"], 16)
            act.sem_inc(S["xT_sb"], 2)
            act.sem_inc(S["y_sb"], 2)
            act.sem_inc(S["qkv_sb"], 2)

            act.wait_ge(S["var_ready"], 1)
            A.activation(n_std, n_var, ACT.Sqrt).then_inc(S["std_ready"], 1)
            act.wait_ge(S["size_ready"], 1)
            A.activation(n_norm, n_size, ACT.Sqrt, scale=float(D)).then_inc(S["norm_ready"], 1)
            act.wait_ge(S["cols_ready"], 1)

            def x_transposed(i, j):
                act.wait_ge(S["xT_ps"], i * TB + (j + 1))
                A.copy(xT[:, j % TB], ps[:, (j % TB) % 2, 0:256].rearrange("p (k c) -> p k c", k=2)).then_inc(S["xT_sb"], 1)

            def q_transposed(i):
                act.wait_ge(S["qT_ps"], i + 2)
                A.copy(zT[:, 4, bass.ds(i * (TB * P), TB * P)],
                       ps[:, 6:8, :].rearrange("p b c -> p (b c)")[:, 0:TB * P]).then_inc(S["qT_sb"], 1)

            def node_act(i, first, last):
                for j in range(TB):
                    xt = resid[:, bass.ds(i * TB + j, 1), :].rearrange("p a c -> p (a c)")
                    act.wait_ge(S["xm_ready"], i * TB + (j + 1))
                    A.activation(xt, xt, ACT.Identity, scale=n_resscale[:, bass.ds(i * TB + j, 1)],
                                 bias=n_resbias[:, bass.ds(i * TB + j, 1)]).then_inc(S["resid_ready"], 1)
                    act.wait_ge(S["ys_ps"], i * TB + (j + 1))
                    if not first:
                        act.wait_ge(y_stored[j], i * 16)
                    A.activation(ysb[:, j, :], ps[:, 2 + j % 2, 0:256], ACT.Identity,
                                 scale=n_yscale[:, bass.ds(i * TB + j, 1)]).then_inc(S["y_sb"], 1)
                    act.wait_ge(S["qkv_ps"], i * TB + (j + 1))
                    if j == 0:
                        act.wait_ge(S["qn_ready"], i + 1)
                    A.copy(qs[:, j, :], ps[:, 4 + j % 2, 0:HD])
                    A.copy(kv[:, bass.ds(i * TB + j, 1), 0:2 * HD].rearrange("p a c -> p (a c)"),
                           ps[:, 4 + j % 2, HD:3 * HD]).then_inc(S["qkv_sb"], 1)
                    if not last or j + 2 < TB:
                        x_transposed(i, j + 2)
                    if j == 3 and not first:
                        q_transposed(i - 1)
                act.wait_ge(S["q_sub"], i + 1)
                A.activation(qs[:], qs[:], ACT.Exp).then_inc(S["q_exp"], 1)

            x_transposed(0, 0)
            x_transposed(0, 1)
            node_act(0, True, False)
            with act.Fori(1, NODE_TURNS - 1) as i:
                node_act(i, False, False)
            node_act(NODE_TURNS - 1, False, True)
            q_transposed(NODE_TURNS - 1)
            for g in range(NODE_TURNS):
                act.wait_ge(S["k_sub"], g + 1)
                tiles = kv[:, g * TB:(g + 1) * TB, 0:HD]
                A.activation(tiles, tiles, ACT.Exp).then_inc(S["k_exp"], 1)
            act.wait_ge(S["k_sub"], NODE_TURNS + 1)
            A.activation(memk[:], memk[:], ACT.Exp).then_inc(S["k_exp"], 1)

            act.sem_inc(S["z_evac"], 3)

            def evacuate(i, k):
                g1 = i * 4 + (k + 1)
                b = k % 2
                act.wait_ge(S["sel_done"], g1 + 2)
                act.wait_ge(S["added"], g1 + 2)
                bank = ps[:, 4 + b, 0:8 * WIN].rearrange("p (q w) -> p q w", q=8)
                A.copy(stage[0:64, b], bank[0:64, 0:4])
                A.copy(stage[64:128, b], bank[64:128, 4:8]).then_inc(S["z_evac"], 1)

            act.wait_ge(S["ctx_sb"], 1)
            def silu(s, n=CHUNK):
                A.activation(h_r[:, s, 0:n], ps[:, s, 0:n], ACT.Silu, scale=ES_SCALE)
                return A.activation(h_f[64:128, s, 0:n], ps[64:128, s, 0:n], ACT.Silu, scale=ES_SCALE)

            for s in range(2):
                act.wait_ge(S["h_ready"], s + 1)
                silu(s).then_inc(S["silu_done"], 1)
            with act.Fori(0, EDGE_TURNS) as i:
                evacuate(i, 0)
                act.wait_ge(S["h_ready"], i * 2 + 3)
                act.wait_ge(S["w_ready"], i * 4 + 2)
                silu(0).then_inc(S["silu_done"], 1)
                evacuate(i, 1)
                act.wait_ge(S["h_ready"], i * 2 + 4)
                act.wait_ge(S["w_ready"], i * 4 + 4)
                silu(1).then_inc(S["silu_done"], 1)
                evacuate(i, 2)
                evacuate(i, 3)
            act.wait_ge(S["flag_ready"], 1)
            flag = act.value_load(flag_i[0:1, 0:1], min_val=0, max_val=ET * P)
            act.wait_ge(S["added"], EG + 5)
            with act.If(flag > 0):
                with act.Fori(0, ET) as t:
                    act.wait_ge(S["stray_step_pe"], t * (STRAY_TURNS + 2) + 1)
                    silu(0, P).then_inc(S["stray_step_act"], 1)
            with act.Else():
                act.sem_inc(S["turn_act"], 1)
            act.sem_inc(S["xlT_sb"], 2)
            act.sem_inc(S["gnn_sb"], TB)
            act.sem_inc(S["xl_stored"], TB)
            def normalized(out, i, j, done):
                A.activation(out.rearrange("p a c -> p (a c)"), resid[:, bass.ds(i * TB + j, 1), :].rearrange("p a c -> p (a c)"),
                             ACT.Identity, scale=col[:, 6, j:j + 1], bias=col[:, 7, j:j + 1]).then_inc(done, 1)

            def lin2_scaled(i):
                for j in range(TB):
                    act.wait_ge(S["om_ready"], i * TB + (TB + j + 1))
                    if j == 0:
                        act.wait_ge(S["x_summed"], i + 1)
                    A.activation(gnn[:, j, :], ps[:, j, 0:256], ACT.Identity, scale=node_a_sb[:, bass.ds(i * TB + j, 1)]).then_inc(S["gnn_sb"], 1)

            def norm_root(i):
                act.wait_ge(S["om_var"], i + 1)
                A.activation(col[:, 1, :], col[:, 0, :], ACT.Sqrt, scale=float(D)).then_inc(S["om_norm"], 1)

            def combine_act(i, last):
                act.wait_ge(S["x2_var"], i + 1)
                A.activation(col[:, 3, :], col[:, 2, :], ACT.Sqrt).then_inc(S["x2_std"], 1)
                act.wait_ge(S["xl_scale"], i + 1)
                for j in range(TB):
                    normalized(xls[:, j:j + 1, :], i, j, S["xl_ready"])
                if not last:
                    lin2_scaled(i + 1)
                    norm_root(i + 1)
                for j in range(TB):
                    act.wait_ge(S["xlT_ps"], i * TB + (j + 1))
                    act.wait_ge(S["gate_ps"], i * TB + (1 + max(0, j - 1)))
                    A.copy(xlT[:, j % 2], ps[:, 5 + j % 2, 0:256].rearrange("p (k c) -> p k c", k=2)).then_inc(S["xlT_sb"], 1)
                    normalized(xl[:, bass.ds(i * TB + j, 1), :], i, j, S["xl_stored"])

            lin2_scaled(0)
            norm_root(0)
            with act.Fori(0, NODE_TURNS - 1) as i:
                combine_act(i, False)
            combine_act(NODE_TURNS - 1, True)
            act.wait_ge(S["l_sub"], 1)
            A.activation(rt[:, 1, :], rt[:, 0, :], ACT.Exp).then_inc(S["l_exp"], 1)
            act.sem_inc(S["hid_sb"], 3)
            with act.Fori(0, E // 2) as i:
                for s in range(2):
                    act.wait_ge(we_in[s], i * 64 + 64)
                    act.wait_ge(S["yexp_ps"], i * 8 + (4 * s + 1))
                    for f in range(FB):
                        act.wait_ge(S["hid_ps"], i * (2 * FB) + s * FB + f + 1)
                        A.activation(hid[:, f, :], ps[:, 2 + (s * FB + f) % 3, 0:CAP], ACT.Relu, bias=b1_sb[:, s, f:f + 1]).then_inc(S["hid_sb"], 1)
                    e = i * 2 + s
                    for c in range(4):
                        act.wait_ge(S["yst_ready"], i * 8 + (4 * s + c + 3))
                        act.sem_inc(S["turn_act"], 1)
                        rows = P if c < 3 else LAST_C
                        act.dma_start(ybuf_dram[bass.ds(e * SLOTS + c * P, rows), :], yst[0:rows, s, c, :]).then_inc(y_out[s], 16)

            for g in range(NODE_TURNS):
                act.wait_ge(back_in[g], 16 * TB)
                for t in range(g * TB, (g + 1) * TB):
                    A.activation(xl[:, t, :], xl[:, t, :], ACT.Copy, scale=rcol[:, 10, t:t + 1]).then_inc(S["y_scaled"], 1)
                act.wait_ge(S["inf_ready"], g + 1)
                if g > 1:
                    act.wait_ge(S["out_ready"], g - 1)
                A.activation(zflat[:, 2560 + (g % 2) * 1280:2560 + (g % 2 + 1) * 1280], zflat[:, 0:TB * D],
                             ACT.Copy, scale=1e4).then_inc(S["inf_scaled"], 1)

        @block.vector
        def _(dve):
            V = nc.vector
            chain = Chain(dve, S["dve_chain"])
            link = chain.link
            V.memset(es_r[:].bitcast(F32), 0.0)
            link(V.memset(fc1_r[:].bitcast(F32), 0.0))
            V.memset(kmax_run, -FLT_MAX)
            V.memset(kv[:, :, 2 * HD:KV], 1.0)
            dve.sem_inc(S["s_sb"], 2)
            dve.sem_inc(S["qn_ready"], 1)

            for i in range(NODE_TURNS):
                dve.wait_ge(x_in[i], 16)
                for j in range(TB):
                    last = V.bn_stats(st[:, i * TB + j, :], resid[:, i * TB + j, :])
            link(last)
            for t in range(NT):
                last = V.bn_aggr(mv_x[:, t, :], st[:, t, :])
            link(last)
            V.tensor_scalar(n_var, mv_x[:, :, 1], EPS, None, ALU.add).then_inc(S["var_ready"], 1)
            dve.wait_ge(S["weights_in"], 16 * 4)
            V.tensor_scalar(wys[:, :, 0, :], wys[:, :, 0, :], Y_SCALE, None, ALU.mult)
            V.tensor_scalar(wys[:, :, 1, :], wys[:, :, 1, :], S_SCALE, None, ALU.mult)
            for k in range(2):
                last = V.tensor_scalar(wqkv[:, k, :], wqkv[:, k, :], gpre[:, k:k + 1], math.sqrt(D), ALU.mult, ALU.mult)
            last.then_inc(S["scaled"], 1)
            dve.wait_ge(S["std_ready"], 1)
            dve.wait_ge(S["consts_in"], 32)
            link(V.reciprocal(n_rstd, n_std))
            link(V.tensor_tensor(n_size, mv_x[:, :, 1], n_rstd, ALU.mult))
            V.tensor_tensor(n_size, n_size, n_rstd, ALU.mult).then_inc(S["size_ready"], 1)
            dve.wait_ge(S["norm_ready"], 1)
            link(V.tensor_scalar(n_norm, n_norm, 1e-12, None, ALU.max))
            link(V.reciprocal(n_inv, n_norm))
            V.tensor_tensor(n_yscale, n_norm, node_a_sb[:], ALU.mult)
            V.tensor_tensor(n_xmscale, n_rstd, n_inv, ALU.mult)
            V.tensor_scalar(n_resscale, n_rstd, 1.0, None, ALU.add)
            V.scalar_tensor_tensor(n_resbias, mv_x[:, :, 0], -1.0, n_rstd, ALU.mult, ALU.mult).then_inc(S["cols_ready"], 1)
            dve.wait_ge(S["cols_ready"], 1)

            def scaled_x(i, j):
                V.tensor_scalar(xm[:, j, :], resid[:, bass.ds(i * TB + j, 1), :].rearrange("p a c -> p (a c)"),
                                mv_x[:, bass.ds(i * TB + j, 1), 0:1].rearrange("p a c -> p (a c)"),
                                n_xmscale[:, bass.ds(i * TB + j, 1)], ALU.subtract, ALU.mult).then_inc(S["xm_ready"], 1)

            for j in range(TB):
                scaled_x(0, j)
            dve.wait_ge(S["later_in"], 16 * 11)
            V.memset(memv[:, HD:HD + 1], 1.0)
            V.tensor_scalar(wz[:], wz[:], Z_SCALE, None, ALU.mult)
            V.tensor_scalar(gout_b[:], gout_b[:], math.sqrt(D), None, ALU.mult)
            V.tensor_scalar(fc2_sb[:, 0:192], fc2_sb[:, 0:192], W_SCALE, None, ALU.mult)
            link(V.tensor_scalar(fc2_sb[:, 192:256], fc2_sb[:, 192:256], W_SCALE * INV_SQRT3, None, ALU.mult))
            V.tensor_copy(fc2_r[:, 0, :], fc2_sb[:])
            link(V.tensor_copy(fc1_hl[:, 0, :].bitcast(F32R), fc1_sb[:]))
            V.tensor_tensor(fc2_r[:, 1, :], fc2_sb[:], fc2_r[:, 0, :].bitcast(F32), ALU.subtract)
            link(V.tensor_tensor(fc1_hl[:, 1, :].bitcast(F32R), fc1_sb[:], fc1_hl[:, 0, :], ALU.subtract))
            link(V.tensor_scalar(fc1_hl[:, 1, :], fc1_hl[:, 1, :], cst[0:32, C_LOW:C_END], None, ALU.mult))
            link(V.scalar_tensor_tensor(fc1_r[0:32, :], fc1_hl[:, 0, :], cst[0:32, C_HIGH:C_LOW], fc1_hl[:, 1, :], ALU.mult, ALU.add))

            def k_maximum(i):
                link(V.tensor_reduce(kmax_turn, kv[:, bass.ds(i * TB, TB), 0:HD].rearrange("p t c -> p c t"), AX.X, ALU.max))
                link(V.tensor_tensor(kmax_run, kmax_run, kmax_turn, ALU.max))

            def node_dve(i, last):
                for j in range(TB):
                    dve.wait_ge(S["resid_ready"], i * TB + (j + 1))
                    dve.wait_ge(S["y_sb"], i * TB + (j + 3))
                    xt = resid[:, bass.ds(i * TB + j, 1), :].rearrange("p a c -> p (a c)")
                    V.scalar_tensor_tensor(xt, ps[:, 2 + j % 2, 256:512], n_yscale[:, bass.ds(i * TB + j, 1)], xt,
                                           ALU.mult, ALU.add).then_inc(S["s_sb"], 1)
                    if not last:
                        dve.wait_ge(S["xT_ps"], i * TB + (j + 1))
                        scaled_x(i + 1, j)
                dve.wait_ge(S["qkv_sb"], i * TB + (TB + 2))
                if last:
                    k_maximum(i)
                    dve.sem_inc(S["kmax_sb"], 1)
                q4 = qs[:].rearrange("p t (h d) -> p (t h) d", d=DH)
                n4 = qn[:].rearrange("p t (h d) -> p (t h) d", d=DH)
                link(V.tensor_reduce(qcol[:, 0, :], q4, AX.X, ALU.max))
                V.tensor_tensor(q4, q4, bc(qcol[:, 0, :], 2, DH), ALU.subtract).then_inc(S["q_sub"], 1)
                if not last:
                    k_maximum(i)
                dve.wait_ge(S["q_exp"], i + 1)
                link(V.tensor_reduce(qcol[:, 0, :], q4, AX.X, ALU.add))
                link(V.reciprocal(qcol[:, 1, :], qcol[:, 0, :]))
                dve.wait_ge(S["qT_ps"], i + 1)
                V.tensor_tensor(n4, q4, bc(qcol[:, 1, :], 2, DH), ALU.mult).then_inc(S["qn_ready"], 1)

            with dve.Fori(0, NODE_TURNS - 1) as i:
                chain.enter(i, 5)
                node_dve(i, False)
            chain.leave(NODE_TURNS - 1)
            node_dve(NODE_TURNS - 1, True)

            link(V.tensor_reduce(kmx[:, 1:2], memkt[:], AX.X, ALU.max))
            dve.wait_ge(S["kmaxT_ps"], 1)
            link(V.tensor_reduce(kmx[:, 0:1], ps[:, 0, 0:P], AX.X, ALU.max))
            link(V.tensor_tensor(kmx[:, 0:1], kmx[:, 0:1], kmx[:, 1:2], ALU.max))
            V.tensor_scalar(kmax_diag, ident, kmx[:, 0:1], None, ALU.mult).then_inc(S["kdiag"], 1)
            dve.wait_ge(S["kmax_b"], 1)
            for g in range(NODE_TURNS):
                tiles = kv[:, g * TB:(g + 1) * TB, 0:HD]
                V.tensor_tensor(tiles, tiles, bc(ps[:, 1, 0:HD], 1, TB), ALU.subtract).then_inc(S["k_sub"], 1)
            V.tensor_tensor(memk[:], memk[:], ps[0:NUM_MEM, 1, 0:HD], ALU.subtract).then_inc(S["k_sub"], 1)
            dve.wait_ge(S["edges_in"], 48)
            V.tensor_copy(first_f, first_i[0:1, 3:3 + EG]).then_inc(S["first_row"], 1)
            link(V.tensor_copy(relf, dst_i[:]))
            dve.wait_ge(S["first_ps"], 1)
            rel3 = relf.rearrange("p (g j) -> p g j", j=GT)
            dst3 = stray_dst.rearrange("p (g j) -> p g j", j=GT)
            V.tensor_copy(stray_dst, relf)
            link(V.tensor_tensor(rel3, rel3, bc(ps[:, 7, 0:EG], 2, GT), ALU.subtract))
            link(V.tensor_scalar(inw, relf, 0.0, None, ALU.is_ge))
            link(V.scalar_tensor_tensor(inw, relf, float(WIN), inw, ALU.is_lt, ALU.mult))
            dve.wait_ge(S["zero_in"], 16)
            link(V.scalar_tensor_tensor(stray_new, inw, -8192.0, stray_dst, ALU.mult, ALU.add))
            V.tensor_copy(stray_dst, stray_new)
            V.tensor_reduce(flag_f[:, 0:1], inw, AX.X, ALU.add).then_inc(S["strays_sum"], 1)
            dve.wait_ge(S["k_exp"], NODE_TURNS)
            V.tensor_scalar(kv[:, NT - 1, 0:HD], kv[:, NT - 1, 0:HD], valid, None, ALU.mult).then_inc(S["k_masked"], 1)
            dve.wait_ge(S["ctx_ps"], 1)
            link(V.reciprocal(ksum_inv[:], ps[:, 2, HD:HD + 1]))
            V.scalar_tensor_tensor(ctx_kv, ps[:, 2, 0:HD], ksum_inv[:], block_mask, ALU.mult, ALU.mult).then_inc(S["ctx_norm"], 1)
            dve.wait_ge(S["ctxT_ps"], 1)
            V.tensor_copy(ctx_vk, ps[:, 3, 0:HD]).then_inc(S["ctx_sb"], 1)
            dve.wait_ge(S["mixw_ps"], 1)
            V.tensor_scalar(mix_w[:], ps[:, 4, 0:D], SM_SCALE, None, ALU.mult).then_inc(S["mixw_sb"], 1)
            dve.wait_ge(S["mixw_sb"], 1)

            for j in range(TB):
                dve.wait_ge(y_stored[j], 16 * NODE_TURNS)
            V.memset(stage[:], 0.0)
            dve.wait_ge(S["flag_ps"], 1)
            V.tensor_scalar(flag_i[0:1, 0:1], ps[0:1, 6, 0:1], -1.0, float(ET * P), ALU.mult, ALU.add).then_inc(S["flag_ready"], 1)
            dve.wait_ge(S["flag_ready"], 1)
            dve.sem_inc(S["added"], 1)

            def low_part(s, n=CHUNK):
                return V.tensor_tensor(h_r[64:128, s, 0:n], h_f[64:128, s, 0:n], h_r[64:128, s, 0:n].bitcast(F32), ALU.subtract)

            def products(i, k):
                g1 = i * 4 + (k + 1)
                b = k % 2
                dve.wait_ge(rows_in[k], i * (16 * GT) + 16 * GT)
                dve.wait_ge(S["w_ready"], g1)
                dve.wait_ge(S["sel_done"], g1)
                w = ps[:, 2 + b, :].rearrange("p (j c) -> p j c", j=GT)
                V.tensor_tensor(prod[:, b, :, 0:128].rearrange("p j (a u) -> p j a u", a=2),
                                w[:, :, 0:128].rearrange("p j (a u) -> p j a u", a=2),
                                bc(xg[:, k, :, 0:64], 2, 2), ALU.mult)
                for j in range(GT):
                    last = V.tensor_tensor(prod[:, b, j, 128:512].rearrange("p (c a u) -> p c a u", c=3, a=2),
                                           bc(w[:, j, 128:256].rearrange("p (a u) -> p a u", a=2), 1, 3),
                                           bc(xg[:, k, j, 64:256].rearrange("p (c u) -> p c u", c=3), 2, 2), ALU.mult)
                last.then_inc(S["prod_ready"], 1)

            def add(i, k, first=None):
                g = i * 4 + (k + 3)
                base = dve.value_load(first_i[0:1, bass.ds(g, 1)] if first is None else first, min_val=0, max_val=N - 1)
                z = zT[:, 0:4, bass.ds(base, WIN)]
                dve.wait_ge(S["z_evac"], g + 1)
                dve.wait_ge(S["added"], g + 1)
                V.tensor_tensor(z, z, stage[:, k % 2], ALU.add).then_inc(S["added"], 1)

            def one_hot(i):
                dve.wait_ge(S["sel_made"], i * 2 + 1)
                V.tensor_tensor(hot[:], bc(iota[:, 0:WIN], 1, TPT), bc(relf[:, bass.ds(i * TPT, TPT)], 2, WIN),
                                ALU.is_equal).then_inc(S["hot_done"], 1)

            def selection(i, s):
                dve.wait_ge(S["hot_done"], i + 1)
                dve.wait_ge(S["sel_done"], i * 4 + (2 * s + 1))
                V.tensor_tensor(sel[:, s], bc(hot[:, 4 * s:4 * s + 4], 2, 4), bc(ea_sb[:, bass.ds(i * TPT + 4 * s, 4), :], 3, WIN),
                                ALU.mult).then_inc(S["sel_made"], 1)

            dve.wait_ge(S["silu_done"], 1)
            low_part(0).then_inc(S["lo_ready"], 1)
            dve.sem_inc(S["sel_made"], 1)
            with dve.Fori(0, EDGE_TURNS) as i:
                one_hot(i)
                add(i, -3)
                selection(i, 0)
                products(i, 0)
                add(i, -2)
                dve.wait_ge(S["silu_done"], i * 2 + 2)
                low_part(1).then_inc(S["lo_ready"], 1)
                products(i, 1)
                add(i, -1)
                selection(i, 1)
                products(i, 2)
                add(i, 0)
                dve.wait_ge(S["silu_done"], i * 2 + 3)
                low_part(0).then_inc(S["lo_ready"], 1)
                products(i, 3)
            for k in range(-3, 0):
                add(EDGE_TURNS, k, first_i[0:1, EG + k + 3:EG + k + 4])
            dve.wait_ge(S["added"], EG + 4)
            dve.sem_inc(S["added"], 1)
            flag = dve.value_load(flag_i[0:1, 0:1], min_val=0, max_val=ET * P)
            with dve.If(flag > 0):
                dve.sem_inc(S["stray_step_dve"], 1)
                with dve.Fori(0, ET) as t:
                    base = STRAY_TURNS + 3
                    dve.wait_ge(S["stray_step_act"], t + 1)
                    low_part(0, P).then_inc(S["stray_step_dve"], 1)
                    dve.wait_ge(S["stray_gathered"], t * 16 + 16)
                    dve.wait_ge(S["stray_step_pe"], t * (STRAY_TURNS + 2) + 2)
                    w = ps[:, 2, 0:256]
                    V.tensor_tensor(prod[:, 0, 0, 0:128].rearrange("p (a u) -> p a u", a=2),
                                    w[:, 0:128].rearrange("p (a u) -> p a u", a=2), bc(xg[:, 0, 0, 0:64], 1, 2), ALU.mult)
                    V.tensor_tensor(prod[:, 0, 0, 128:512].rearrange("p (c a u) -> p c a u", c=3, a=2),
                                    bc(w[:, 128:256].rearrange("p (a u) -> p a u", a=2), 1, 3),
                                    bc(xg[:, 0, 0, 64:256].rearrange("p (c u) -> p c u", c=3), 2, 2), ALU.mult)
                    V.tensor_copy(stray_cur[:, 0:1], stray_dst[:, bass.ds(t, 1)]).then_inc(S["stray_step_dve"], 1)
                    dve.wait_ge(S["stray_step_dve"], t * base + 3)
                    dve.sem_inc(S["turn_dve"], 1)
                    with dve.Fori(0, STRAY_TURNS) as n:
                        step = t * (3 * STRAY_TURNS) + n * 3
                        V.tensor_scalar(stray_hot, iota, stray_cur[:, 0:1], None, ALU.is_equal).then_inc(S["kdiag"], 1)
                        dve.wait_ge(S["kdiag"], step + 2)
                        V.tensor_scalar(stray_cur[:, 0:1], stray_cur[:, 0:1], -float(STRAY_WIN), None, ALU.add).then_inc(S["kdiag"], 1)
                        dve.wait_ge(S["kdiag"], step + 3)
                        V.tensor_tensor(stray_sel, bc(stray_hot, 1, 4),
                                        bc(ea_sb[:, bass.ds(t, 1), :].rearrange("p a c -> p (a c)"), 2, STRAY_WIN), ALU.mult).then_inc(S["kdiag"], 1)
                        dve.wait_ge(S["kdiag"], step + 4)
                        dve.wait_ge(S["stray_step_pe"], t * (STRAY_TURNS + 2) + n + 3)
                        cols = bass.ds(n * STRAY_WIN, STRAY_WIN)
                        V.tensor_tensor(zT[0:64, 3, cols], zT[0:64, 3, cols], ps[0:64, 4, 0:STRAY_WIN], ALU.add)
                        V.tensor_tensor(zT[64:128, 0:3, cols], zT[64:128, 0:3, cols],
                                        ps[64:128, 4, STRAY_WIN:4 * STRAY_WIN].rearrange("p (c w) -> p c w", c=3), ALU.add)
                        V.tensor_tensor(zT[0:64, 0:3, cols], zT[0:64, 0:3, cols], ps[0:64, 5:8, 0:STRAY_WIN], ALU.add)
                        V.tensor_tensor(zT[64:128, 3, cols], zT[64:128, 3, cols], ps[64:128, 5, STRAY_WIN:2 * STRAY_WIN], ALU.add).then_inc(S["stray_step_dve"], 1)
                        dve.wait_ge(S["stray_step_dve"], t * base + n + 4)
                    dve.sem_inc(S["stray_step_dve"], 1)
            with dve.Else():
                dve.sem_inc(S["turn_dve"], 1)
            dve.sem_inc(S["sums_ready"], 1)

            dve.sem_inc(S["om_ready"], TB)

            def take_logits(i):
                dve.wait_ge(S["gate_ps"], i * TB + 1)
                V.tensor_tensor(logits_all[:, bass.ds(i * (TB * E), TB * E)].rearrange("p (t e) -> p t e", e=E),
                                ps[:, 7, 0:TB * E].rearrange("p (t e) -> p t e", e=E), bc(gateb_b[:], 1, TB), ALU.add).then_inc(S["logit_sb"], 1)

            with dve.Fori(0, NODE_TURNS) as i:
                chain.enter(i, 10)
                xt = resid[:, bass.ds(i * TB, TB), :]
                for j in range(TB):
                    dve.wait_ge(S["gnn_ps"], i * TB + (j + 1))
                    V.tensor_tensor(om[:, j, :], ps[:, j, 256:512], bout_b[:], ALU.add).then_inc(S["om_ready"], 1)
                dve.wait_ge(S["om_ready"], i * TB + 2 * TB)
                dve.sem_inc(S["turn_dve"], 1)
                for j in range(TB):
                    last = V.bn_stats(cstat[:, j, :], om[:, j, :])
                link(last)
                dve.sem_inc(S["turn_dve"], 1)
                for j in range(TB):
                    last = V.bn_aggr(mv[:, j, :], cstat[:, j, :])
                link(last)
                link(V.tensor_tensor(col[:, 4, :], mv[:, :, 0], mv[:, :, 0], ALU.mult))
                V.tensor_tensor(col[:, 0, :], col[:, 4, :], mv[:, :, 1], ALU.add).then_inc(S["om_var"], 1)
                dve.wait_ge(S["om_norm"], i + 1)
                link(V.tensor_scalar(col[:, 4, :], col[:, 1, :], 1e-12, None, ALU.max))
                link(V.reciprocal(col[:, 5, :], col[:, 4, :]))
                for j in range(TB):
                    last = V.scalar_tensor_tensor(om[:, j, :], om[:, j, :], col[:, 5, j:j + 1], gout_b[:], ALU.mult, ALU.mult)
                link(last)
                dve.wait_ge(S["x_summed"], i + 2)
                link(V.tensor_tensor(xt, xt, om[:], ALU.add))
                dve.sem_inc(S["turn_dve"], 1)
                for j in range(TB):
                    last = V.bn_stats(cstat[:, j, :], resid[:, bass.ds(i * TB + j, 1), :].rearrange("p a c -> p (a c)"))
                link(last)
                dve.sem_inc(S["turn_dve"], 1)
                for j in range(TB):
                    last = V.bn_aggr(mv[:, j, :], cstat[:, j, :])
                link(last)
                V.tensor_scalar(col[:, 2, :], mv[:, :, 1], EPS, None, ALU.add).then_inc(S["x2_var"], 1)
                take_logits(i)
                dve.wait_ge(S["x2_std"], i + 1)
                dve.wait_ge(S["xl_stored"], i * TB + TB)
                link(V.reciprocal(col[:, 6, :], col[:, 3, :]))
                V.scalar_tensor_tensor(col[:, 7, :], mv[:, :, 0], -1.0, col[:, 6, :], ALU.mult, ALU.mult).then_inc(S["xl_scale"], 1)
            chain.leave(NODE_TURNS)
            take_logits(NODE_TURNS)
            dve.wait_ge(S["logit_sb"], NODE_TURNS + 1)
            dve.wait_ge(S["xl_stored"], NT + TB)

            l3 = logits.rearrange("p (t e) -> p t e", e=E)

            def r(n):
                return rt[:, n, :].rearrange("p (t e) -> p t e", e=E)

            link(V.tensor_reduce(rcol[:, 0, :], l3, AX.X, ALU.max))
            V.tensor_tensor(r(0), l3, bc(rcol[:, 0, :], 2, E), ALU.subtract).then_inc(S["l_sub"], 1)
            dve.wait_ge(S["l_exp"], 1)
            link(V.tensor_reduce(rcol[:, 1, :], r(1), AX.X, ALU.add))
            link(V.reciprocal(rcol[:, 2, :], rcol[:, 1, :]))
            link(V.tensor_scalar(r(2), r(0), 0.0, None, ALU.is_ge))
            link(V.scalar_tensor_tensor(r(3), r(2), -float(E), bc(iota8, 1, NT), ALU.mult, ALU.add))
            link(V.tensor_reduce(rcol[:, 3, :], r(3), AX.X, ALU.min))
            link(V.tensor_tensor(r(4), r(3), bc(rcol[:, 3, :], 2, E), ALU.is_equal))
            V.tensor_scalar(rt[:, 4, (NT - 1) * E:], rt[:, 4, (NT - 1) * E:], valid, None, ALU.mult).then_inc(S["hot_ready"], 1)
            dve.wait_ge(S["hot_ready"], 1)
            dve.wait_ge(S["pre_ps"], 1)
            tot_et = rt[:, 5, :].rearrange("p (e t) -> p e t", t=NT)
            link(V.tensor_copy(tot_et, ps[:, 6, 0:NT * E].rearrange("p (t e) -> p e t", e=E)))
            link(V.tensor_tensor_scan(rt[:, 6, :], reset, rt[:, 5, :], 0.0, ALU.mult, ALU.add))
            link(V.tensor_tensor(rt[:, 7, :], rt[:, 6, :], rt[:, 5, :], ALU.subtract))
            link(V.tensor_tensor(r(8), ps[:, 5, 0:NT * E].rearrange("p (t e) -> p t e", e=E),
                                 rt[:, 7, :].rearrange("p (e t) -> p t e", t=NT), ALU.add))
            link(V.tensor_tensor(r(9), r(8), r(4), ALU.mult))
            link(V.tensor_reduce(rcol[:, 4, :], r(9), AX.X, ALU.add))
            link(V.tensor_scalar(rcol[:, 5, :], rcol[:, 4, :], float(CAP), None, ALU.is_le))
            link(V.tensor_scalar(rcol[:, 5, NT - 1:NT], rcol[:, 5, NT - 1:NT], valid, None, ALU.mult))
            link(V.tensor_scalar(rcol[:, 6, :], rcol[:, 3, :], float(E), float(SLOTS), ALU.add, ALU.mult))
            link(V.tensor_scalar(rcol[:, 7, :], rcol[:, 4, :], -1.0, None, ALU.add))
            link(V.tensor_tensor(rcol[:, 8, :], rcol[:, 6, :], rcol[:, 7, :], ALU.add))
            link(V.tensor_tensor(rcol[:, 8, :], rcol[:, 8, :], trash_row, ALU.subtract))
            link(V.tensor_tensor(rcol[:, 8, :], rcol[:, 8, :], rcol[:, 5, :], ALU.mult))
            link(V.tensor_tensor(scat_i[:], rcol[:, 8, :], trash_row, ALU.add))
            link(V.tensor_scalar(rcol[:, 9, :], rcol[:, 7, :], float(CAP - 1), 0.0, ALU.min, ALU.max))
            V.tensor_tensor(rcol[:, 10, :], rcol[:, 2, :], rcol[:, 5, :], ALU.mult)
            V.tensor_tensor(gath_i[:], rcol[:, 6, :], rcol[:, 9, :], ALU.add).then_inc(S["slots_ready"], 1)

            dve.sem_inc(S["xbT_sb"], 1)
            dve.sem_inc(S["yst_ready"], 2)

            def rows_copied(pair, s):
                for k in range(2):
                    dve.wait_ge(S["xbT_ps"], pair * 4 + (2 * s + k + 1))
                    V.tensor_copy(xbT[:, k, 0:CAP], ps[:, k, 0:CAP]).then_inc(S["xbT_sb"], 1)

            def results(pair, s, first):
                dve.wait_ge(we_in[s], pair * 64 + 64)
                if not first:
                    dve.wait_ge(y_out[s], pair * 64)
                for c in range(4):
                    dve.wait_ge(S["yexp_ps"], pair * 8 + (4 * s + c + 2))
                    rows = P if c < 3 else LAST_C
                    V.tensor_tensor(yst[0:rows, s, c, :], ps[0:rows, 5 + c % 2, 0:D], b2_sb[0:rows, s, :], ALU.add).then_inc(S["yst_ready"], 1)

            def dve_pair(pair, first, last):
                rows_copied(pair, 1)
                results(pair, 0, first)
                if not last:
                    rows_copied(pair + 1, 0)
                results(pair, 1, first)

            rows_copied(0, 0)
            dve_pair(0, True, False)
            with dve.Fori(1, E // 2 - 1) as i:
                dve_pair(i, False, False)
            dve_pair(E // 2 - 1, False, True)
            for g in range(NODE_TURNS):
                y = xl[:, g * TB:(g + 1) * TB, :]
                inf = zflat[:, 0:TB * D].rearrange("p (t c) -> p t c", t=TB)
                fin = zflat[:, 1280:1280 + TB * D].rearrange("p (t c) -> p t c", t=TB)
                big = zflat[:, 2560 + (g % 2) * 1280:2560 + (g % 2 + 1) * 1280].rearrange("p (t c) -> p t c", t=TB)
                dve.wait_ge(S["y_scaled"], TB * (g + 1))
                if g > 0:
                    dve.wait_ge(S["inf_scaled"], g)
                link(V.tensor_scalar(inf, y, -FLT_MAX, -1.0, ALU.is_lt, ALU.mult))
                V.scalar_tensor_tensor(inf, y, FLT_MAX, inf, ALU.is_gt, ALU.add).then_inc(S["inf_ready"], 1)
                link(V.tensor_scalar(fin.bitcast(I32), y, 0.0, 0.0, ALU.mult, ALU.is_equal))
                dve.wait_ge(S["inf_scaled"], g + 1)
                link(V.copy_predicated(big, fin.bitcast(I32), y))
                x2 = resid[:, g * TB:(g + 1) * TB, :]
                V.tensor_tensor(x2, x2, big, ALU.add).then_inc(S["out_ready"], 1)

        @block.tensor
        def _(pe):
            T = nc.tensor

            def keep_busy(times, bank, n=512):
                for _ in range(times):
                    T.matmul(ps[:, bank, 0:n], ident, cst[:, 0:n], start=True, stop=True)

            pe.wait_ge(S["consts_in"], 32)
            keep_busy(4, 7)
            pe.wait_ge(S["scaled"], 1)
            pe.sem_inc(S["qT_ps"], 1)

            def transposes(i, j):
                pe.wait_ge(S["xm_ready"], i * TB + (j + 1))
                pe.wait_ge(S["xT_sb"], i * TB + (j + 1) + (1 if j % TB == 0 else 0))
                for k in range(2):
                    last = T.transpose(ps[:, (j % TB) % 2, k * P:(k + 1) * P], xm[:, j % TB, k * P:(k + 1) * P], ident)
                last.then_inc(S["xT_ps"], 1)

            def q_transposes(i):
                pe.wait_ge(S["qn_ready"], i + 2)
                for j in range(TB):
                    last = T.transpose(ps[:, 6 + j // 4, (j % 4) * P:(j % 4 + 1) * P], qn[:, j, :], ident)
                last.then_inc(S["qT_ps"], 1)

            def node_pe(i, first, last_turn):
                for j in range(TB):
                    n = i * TB + (j + 1) + (1 if j == 0 else 0)
                    pe.wait_ge(S["xT_sb"], i * TB + (j + 3))
                    pe.wait_ge(S["y_sb"], n)
                    pe.wait_ge(S["s_sb"], n)
                    ys = ps[:, 2 + j % 2, :].rearrange("p (w c) -> p w c", w=2)
                    for k in range(2):
                        last = T.matmul(ys[:, :, k * P:(k + 1) * P], xT[:, j, k, :], wys[:, k], start=True, stop=True, skip_group_check=True)
                    last.then_inc(S["ys_ps"], 1)
                    pe.wait_ge(S["qkv_sb"], n)
                    for k in range(2):
                        last = T.matmul(ps[:, 4 + j % 2, 0:3 * HD], xT[:, j, k, :], wqkv[:, k, :], start=(k == 0), stop=(k == 1))
                    last.then_inc(S["qkv_ps"], 1)
                    if not last_turn or j + 2 < TB:
                        transposes(i, j + 2)
                    if j == 2 and not first:
                        q_transposes(i - 1)

            transposes(0, 0)
            transposes(0, 1)
            node_pe(0, True, False)
            with pe.Fori(1, NODE_TURNS - 1) as i:
                node_pe(i, False, False)
            node_pe(NODE_TURNS - 1, False, True)
            pe.wait_ge(S["kmax_sb"], 1)
            T.transpose(ps[:, 0, 0:P], kmax_run, ident).then_inc(S["kmaxT_ps"], 1)
            q_transposes(NODE_TURNS - 1)
            pe.wait_ge(S["kdiag"], 1)
            T.matmul(ps[:, 1, 0:P], ones, kmax_diag, start=True, stop=True).then_inc(S["kmax_b"], 1)
            pe.wait_ge(S["qT_sb"], NODE_TURNS)
            pe.wait_ge(S["s_sb"], NT + 2)
            for t in range(NT):
                if t % TB == 0:
                    pe.wait_ge(S["k_exp"], t // TB + 1)
                if t == 2 * TB:
                    pe.wait_ge(S["first_row"], 1)
                    T.matmul(ps[:, 7, 0:EG], ones[0:1, :], first_f, start=True, stop=True).then_inc(S["first_ps"], 1)
                if t == NT - 1:
                    pe.wait_ge(S["k_masked"], 1)
                T.matmul(ps[:, 2, 0:HD + 1], kv[:, t, 0:HD], kv[:, t, HD:KV], start=(t == 0), stop=False)
            pe.wait_ge(S["k_exp"], NODE_TURNS + 1)
            T.matmul(ps[:, 2, 0:HD + 1], memk[:], memv[:], start=False, stop=True).then_inc(S["ctx_ps"], 1)
            pe.wait_ge(S["ctx_norm"], 1)
            T.transpose(ps[:, 3, 0:P], ctx_kv, ident).then_inc(S["ctxT_ps"], 1)
            pe.wait_ge(S["ctx_sb"], 1)
            T.matmul(ps[:, 4, 0:D], ctx_vk, wout[:], start=True, stop=True).then_inc(S["mixw_ps"], 1)
            pe.wait_ge(S["strays_sum"], 1)
            T.matmul(ps[0:1, 6, 0:1], flag_f[:, 0:1], ones[:, 0:1], start=True, stop=True).then_inc(S["flag_ps"], 1)
            pe.sem_inc(S["sel_done"], 2)

            def hidden(s, landed, silus):
                pe.wait_ge(es_in[s], landed)
                if silus is not None:
                    pe.wait_ge(S["silu_done"], silus)
                T.matmul(ps[:, s, :], fc1_r[:], es_r[:, s, :], start=True, stop=True).then_inc(S["h_ready"], 1)

            def tile_weights(out, s, c0):
                for part in range(2):
                    last = T.matmul(out, h_r[:, s, c0:c0 + P], fc2_r[:, part, :], start=(part == 0), stop=(part == 1))
                return last

            def weights(k, lows, free):
                pe.wait_ge(S["lo_ready"], lows)
                if free is not None:
                    pe.wait_ge(S["prod_ready"], free)
                for j in range(GT):
                    c0 = (GT * (k % 2) + j) * P
                    last = tile_weights(ps[:, 2 + k % 2, j * 256:(j + 1) * 256], k // 2, c0)
                last.then_inc(S["w_ready"], 1)

            def sums(i, k):
                g1 = i * 4 + (k + 1)
                b = k % 2
                pe.wait_ge(S["prod_ready"], g1)
                pe.wait_ge(S["z_evac"], g1 + 1)
                bank = ps[:, 4 + b, 0:16 * WIN].rearrange("p (r q w) -> p r q w", r=2, q=8)
                for j in range(GT):
                    m = sel[:, k // 2, (k % 2) * GT + j]
                    T.matmul(bank[:, 0, 3:7], prod[:, b, j, 0:P], m, start=(j == 0), stop=False, skip_group_check=True)
                    for c in range(1, 4):
                        last = T.matmul(bank[:, :, c - 1:8:8 - c], prod[:, b, j, c * P:(c + 1) * P], bc(m[:, 0:c + 1:c], 1, 2),
                                        start=False, stop=(j == GT - 1 and c == 3), skip_group_check=True)
                last.then_inc(S["sel_done"], 1)

            hidden(0, 32, None)
            hidden(1, 32, None)
            pe.wait_ge(S["flag_ready"], 1)
            weights(0, 1, None)
            with pe.Fori(0, EDGE_TURNS) as i:
                weights(1, i * 2 + 1, None)
                sums(i, 0)
                hidden(0, i * 32 + 64, i * 2 + 1)
                weights(2, i * 2 + 2, i * 4 + 1)
                sums(i, 1)
                weights(3, i * 2 + 2, i * 4 + 2)
                hidden(1, i * 32 + 64, i * 2 + 2)
                sums(i, 2)
                weights(0, i * 2 + 3, i * 4 + 3)
                sums(i, 3)
            pe.wait_ge(S["flag_ready"], 1)
            flag = pe.value_load(flag_i[0:1, 0:1], min_val=0, max_val=ET * P)
            pe.wait_ge(S["added"], EG + 5)
            with pe.If(flag > 0):
                with pe.Fori(0, ET) as t:
                    base = STRAY_TURNS + 3
                    pe.wait_ge(es_in[1], t * 32 + 32 * (EDGE_TURNS + 2))
                    T.matmul(ps[:, 0, 0:P], fc1_r[:], es_r[:, 1, 0:P], start=True, stop=True).then_inc(S["stray_step_pe"], 1)
                    pe.wait_ge(S["stray_step_dve"], t * base + 2)
                    tile_weights(ps[:, 2, 0:256], 0, 0).then_inc(S["stray_step_pe"], 1)
                    with pe.Fori(0, STRAY_TURNS) as n:
                        pe.wait_ge(S["kdiag"], t * (3 * STRAY_TURNS) + n * 3 + 4)
                        pe.wait_ge(S["stray_step_dve"], t * base + n + 3)
                        T.matmul(ps[:, 4, 0:4 * STRAY_WIN], prod[:, 0, 0, 0:P], stray_sel, start=True, stop=True)
                        for c in range(1, 4):
                            T.matmul(ps[:, 4 + c, 0:STRAY_WIN], prod[:, 0, 0, c * P:(c + 1) * P], stray_sel[:, 0, :],
                                     start=True, stop=False, skip_group_check=True)
                            last = T.matmul(ps[:, 5, STRAY_WIN:2 * STRAY_WIN], prod[:, 0, 0, c * P:(c + 1) * P], stray_sel[:, c, :],
                                            start=False, stop=(c == 3), skip_group_check=True)
                        last.then_inc(S["stray_step_pe"], 1)
            with pe.Else():
                pe.sem_inc(S["turn_pe"], 1)
            pe.wait_ge(S["sums_ready"], 1)

            pe.sem_inc(S["gate_ps"], 1)
            keep_busy(4, 3)

            def lin2_and_attention(i, j):
                pe.wait_ge(S["gnn_sb"], i * TB + (j + 1))
                nodes = slice((i * TB + j) * P, (i * TB + j + 1) * P)
                for b, c0 in ((3, 0), (0, 64), (1, 128), (2, 192)):
                    T.matmul(ps[:, j, c0:c0 + MUL], zT[:, b, nodes], wz[:, b, :], start=(b == 3), stop=False, skip_group_check=True)
                T.matmul(ps[:, j, 256:512], zT[:, 4, nodes], mix_w[:], start=False, stop=True, skip_group_check=True).then_inc(S["gnn_ps"], 1)

            def xl_transposed(i, j):
                if j == 0:
                    pe.wait_ge(S["logit_sb"], i + 1)
                pe.wait_ge(S["xl_ready"], i * TB + (j + 1))
                pe.wait_ge(S["xlT_sb"], i * TB + (2 + max(0, j - 1)))
                for k in range(2):
                    last = T.transpose(ps[:, 5 + j % 2, k * P:(k + 1) * P], xls[:, j, k * P:(k + 1) * P], ident)
                last.then_inc(S["xlT_ps"], 1)

            def gate(i, j):
                pe.wait_ge(S["xlT_sb"], i * TB + (j + 3))
                for k in range(2):
                    last = T.matmul(ps[:, 7, j * E:(j + 1) * E], xlT[:, j % 2, k, :], gatew[:, k, :], start=(k == 0), stop=(k == 1))
                last.then_inc(S["gate_ps"], 1)

            for j in range(TB):
                lin2_and_attention(0, j)
            for i in range(NODE_TURNS + 1):
                for j in range(TB):
                    if i > 0:
                        xl_transposed(i - 1, j)
                    if i + 1 < NODE_TURNS:
                        lin2_and_attention(i + 1, j)
                    if i > 0:
                        gate(i - 1, j)
                if i < NODE_TURNS - 1:
                    keep_busy(22 if i == 0 else 12, 5, 256)
            pe.wait_ge(S["hot_ready"], 1)
            T.matmul(ps[:, 5, 0:NT * E], tri, rt[:, 4, :], start=True, stop=True)
            T.matmul(ps[:, 6, 0:NT * E], ones, rt[:, 4, :], start=True, stop=True).then_inc(S["pre_ps"], 1)
            pe.wait_ge(S["slots_ready"], 1)
            pe.sem_inc(S["yexp_ps"], 1)

            def rows_transposed(pair, s):
                pe.wait_ge(xb_in[s], pair * 32 + 32)
                pe.wait_ge(S["xbT_sb"], pair * 4 + (2 * s + 1))
                for k in range(2):
                    for c in range(4):
                        rows = P if c < 3 else LAST_C
                        last = T.transpose(ps[:, k, c * P:c * P + rows], xb[0:rows, s, c, k * P:(k + 1) * P], ident[0:rows, 0:rows])
                    last.then_inc(S["xbT_ps"], 1)

            def layer1(pair, s):
                pe.wait_ge(we_in[s], pair * 64 + 64)
                pe.wait_ge(S["xbT_sb"], pair * 4 + (2 * s + 3))
                for f in range(FB):
                    pe.wait_ge(S["hid_sb"], pair * (2 * FB) + (s * FB + f + 1))
                    for k in range(2):
                        last = T.matmul(ps[:, 2 + (s * FB + f) % 3, 0:CAP], w1_sb[:, s, k, f * P:(f + 1) * P], xbT[:, k, 0:CAP],
                                        start=(k == 0), stop=(k == 1))
                    last.then_inc(S["hid_ps"], 1)

            def layer2(pair, s):
                for c in range(4):
                    pe.wait_ge(S["yst_ready"], pair * 8 + (4 * s + c + 1))
                    rows = P if c < 3 else LAST_C
                    for f in range(FB):
                        if c == 0:
                            pe.wait_ge(S["hid_sb"], pair * (2 * FB) + (s * FB + f + 4))
                        last = T.matmul(ps[0:rows, 5 + c % 2, 0:D], hid[:, f, c * P:c * P + rows], w2_sb[:, s, f, :],
                                        start=(f == 0), stop=(f == FB - 1))
                    last.then_inc(S["yexp_ps"], 1)

            def pe_pair(pair, last):
                layer1(pair, 0)
                rows_transposed(pair, 1)
                layer2(pair, 0)
                layer1(pair, 1)
                if not last:
                    rows_transposed(pair + 1, 0)
                layer2(pair, 1)

            rows_transposed(0, 0)
            with pe.Fori(0, E // 2 - 1) as i:
                pe_pair(i, False)
            pe_pair(E // 2 - 1, True)


def kernel(**inputs):
    import numpy as np
    import concourse.bacc as bacc
    from concourse.bass_utils import run_bass_kernel_spmd as run

    g = {k: np.asarray(v) for k, v in inputs.items()}
    perm = np.concatenate([np.arange(MUL)] + [MUL + 3 * np.arange(MUL) + c for c in range(3)])
    back = np.argsort(perm)
    zero = np.zeros((MUL, MUL), np.float32)

    def rows128(a):
        return a.reshape(2, P, -1).transpose(1, 0, 2)

    def diag(a, b):
        return np.block([[a, zero], [zero, b]])

    pad_e = ET * P - EDGES
    src = np.pad(g["src"], (0, pad_e), mode="edge")
    dst = np.pad(g["dst"], (0, pad_e), mode="edge")
    ea = np.pad(g["edge_attr_4"], ((0, pad_e), (0, 0)))
    es = np.pad(g["edge_attr_8"], ((0, pad_e + 2 * CHUNK), (0, 0))).T
    sc0, sc1, l0, l1 = (g["L0_gnn_" + n] for n in ("sc_w0", "sc_w1", "lin1_w0", "lin1_w1"))
    w00, w01, w10, w11 = (g["L0_gnn_lin2_w" + n] for n in ("00", "01", "10", "11"))
    fc2 = g["L0_gnn_fc_w2"].reshape(MUL, 4, MUL)[:, [0, 2, 3, 1]].reshape(MUL, 4 * MUL)
    zc = np.concatenate([w11, w10])
    mem = g["L0_mix_mem_kv"].reshape(2, HD, NUM_MEM)
    consts = np.zeros((P, C_END), np.float32)
    consts[:, C_IDENT:C_TRI] = np.eye(P)
    consts[:, C_TRI:C_BLOCK] = np.triu(np.ones((P, P)))
    consts[:, C_BLOCK:C_ONES] = np.kron(np.eye(HEADS), np.ones((DH, DH)))
    consts[:, C_ONES:C_IOTA] = 1.0
    consts[:, C_IOTA:C_VALID] = np.arange(STRAY_WIN)
    consts[:LAST, C_VALID] = 1.0
    consts[:, C_RESET:C_IOTA8] = (np.arange(NT * E) % NT != 0)
    consts[:, C_IOTA8:C_TRASH] = np.arange(E)
    consts[:, C_TRASH:C_HIGH] = TRASH + np.arange(NT)[None, :] * P + np.arange(P)[:, None]
    consts[0:16, C_HIGH] = 1.0
    consts[16:32, C_LOW] = 1.0
    arrays = dict(
        x=np.pad(g["x"][:, perm], ((0, NPAD - N), (0, 0)), mode="edge"),
        node_a=np.pad(g["node_vec1"][:, 0], (0, NPAD - N), mode="edge").reshape(NT, P).T,
        src=src.reshape(EG, GT, P).transpose(2, 0, 1),
        dst=dst.reshape(ET, P).T,
        dst_first=np.concatenate([np.zeros(3, dst.dtype), dst[::GT * P]])[None],
        ea=ea.reshape(ET, P, 4).transpose(1, 0, 2),
        es=es.reshape(P, -1),
        w_y=rows128(np.concatenate([diag(l0, l1), diag(l1, l1)])),
        w_s=rows128(np.concatenate([diag(sc0, sc1), diag(sc1, sc1)])),
        w_z=np.stack([zc, zc, zc, np.concatenate([w00, w01])], 1),
        fc1=np.tile(g["L0_gnn_fc_w1"], (4, 2)),
        fc2=np.tile(fc2, (2, 1)),
        w_qkv=rows128(g["L0_mix_w_qkv"][perm]),
        g_pre=g["L0_mix_g_pre"][perm].reshape(2, P).T,
        mem_kt=mem[0],
        mem_k=mem[0].T,
        mem_v=mem[1].T,
        w_out=g["L0_mix_w_out"][:, perm],
        b_out=g["L0_mix_b_out"][perm][None],
        g_out=g["L0_mix_g_out"][perm][None],
        gate_w=rows128(g["L0_ffn_gate_w"][perm]),
        gate_b=g["L0_ffn_gate_b"][None],
        w1=g["L0_ffn_w1"][:, perm].reshape(E, 2, P, F).transpose(0, 2, 1, 3),
        b1=g["L0_ffn_b1"].reshape(E, FB, P).transpose(0, 2, 1),
        w2=g["L0_ffn_w2"][:, :, perm].reshape(E, FB, P, D).transpose(0, 2, 1, 3),
        b2=g["L0_ffn_b2"][:, perm],
        consts=consts,
    )
    nc = bacc.Bacc("TRN2", target_bir_lowering=False, num_devices=1)
    data, args = {}, {}
    for name, a in arrays.items():
        data[f"in_{name}"] = np.ascontiguousarray(a)
        args[name] = nc.dram_tensor(f"in_{name}", a.shape, mybir.dt.from_np(a.dtype), kind="ExternalInput").ap()
    args["out"] = nc.dram_tensor("out_0", (NPAD, D), F32, kind="ExternalOutput").ap()
    program(nc, **args)
    result = run(nc, [data], core_ids=[0])
    return result.results[0]["out_0"][:N][:, back]
```
